# Optimizing a Trainium2 kernel written in Bass

```python
import numpy as np
import jax
import jax.numpy as jnp

def _softmax(x, axis=-1):
    return jax.nn.softmax(x, axis=axis)

def _gelu(x):
    return jax.nn.gelu(x, approximate=True)

def _silu(x):
    return jax.nn.silu(x)

def _sigmoid(x):
    return jax.nn.sigmoid(x)

def _layernorm(x, axis=-1, eps=1e-05):
    m = jnp.mean(x, axis=axis, keepdims=True)
    v = jnp.var(x, axis=axis, keepdims=True)
    return (x - m) / jnp.sqrt(v + eps)

def _scatter_add(tgt, idx, src, axis=0):
    return tgt.at[idx].add(src)

def _segment_sum(src, seg, n):
    return jax.ops.segment_sum(src, seg, n)
kernel_name = 'mk_flamingo_gated_d2_seqx_r8_6dcc77'

def setup_inputs(seed: int=0):
    np.random.seed(seed)
    _w = jnp.asarray

    def _rec_inputs():
        import jax
        import jax.numpy as jnp
        _rk = jax.random.key(seed)
        x = -0.000125 + 0.9999 * jax.random.normal(jax.random.fold_in(_rk, 1), (8, 256, 128), jnp.float32)
        _lenS = 256 - jax.random.randint(jax.random.fold_in(_rk, 7), (8,), 0, max(1, 256 // 4) + 1, jnp.int32)
        _lenS2 = 1601 - jax.random.randint(jax.random.fold_in(_rk, 8), (8,), 0, max(1, 1601 // 4) + 1, jnp.int32)
        _ctx_768P = jax.random.normal(jax.random.fold_in(_rk, 11), (8, 16, 96), jnp.float32)
        _ctx_768c = jax.random.dirichlet(jax.random.fold_in(_rk, 511), 0.3 * jnp.ones((16,), jnp.float32), (8, 1601))
        _ctx_768t = jnp.einsum('bsk,bkd->bsd', _ctx_768c, _ctx_768P)
        _ctx_768t = _ctx_768t * jax.lax.rsqrt(jnp.mean(jnp.square(_ctx_768t)) + 1e-12) * 0.953939
        ctx_768 = 0.00272024 + 0.999456 * (_ctx_768t + 0.3 * jax.random.normal(jax.random.fold_in(_rk, 611), (8, 1601, 96), jnp.float32))
        _g = jax.random.normal(jax.random.fold_in(_rk, 9001), (2, 2), jnp.float32)
        _g = jnp.sign(_g) * jnp.maximum(jnp.abs(_g), 1.0) + (_g == 0) * 1.0
        g_xattn = _g[0]
        g_ffn = _g[1]
        return (x, ctx_768, g_xattn, g_ffn)
    x, ctx_768, g_xattn, g_ffn = _rec_inputs()

    def _L0_xattn_setup():
        import jax, jax.numpy as jnp
        import numpy as np
        B, N, M = (8, 512, 77)
        Q_DIM, CTX_DIM = (128, 96)
        H, D = (16, 64)
        INNER = H * D
        key = jax.random.key(seed)
        ks = jax.random.split(key, 7)
        x = jax.random.normal(ks[0], (B, N, Q_DIM), dtype=jnp.float32)
        context = jax.random.normal(ks[1], (B, M, CTX_DIM), dtype=jnp.float32)
        Wq = jax.random.normal(ks[2], (Q_DIM, INNER), dtype=jnp.float32) * Q_DIM ** (-0.5)
        Wk = jax.random.normal(ks[3], (CTX_DIM, INNER), dtype=jnp.float32) * CTX_DIM ** (-0.5)
        Wv = jax.random.normal(ks[4], (CTX_DIM, INNER), dtype=jnp.float32) * CTX_DIM ** (-0.5)
        Wo = jax.random.normal(ks[5], (INNER, Q_DIM), dtype=jnp.float32) * INNER ** (-0.5)
        bo = jax.random.normal(ks[6], (Q_DIM,), dtype=jnp.float32) * 0.01
        return {'x': x, 'context': context, 'Wq': Wq, 'Wk': Wk, 'Wv': Wv, 'Wo': Wo, 'bo': bo}
    _L0_xattn_all = _L0_xattn_setup()
    _L0_xattn_in = {k: v for k, v in _L0_xattn_all.items() if k in ('Wq', 'Wk', 'Wv', 'Wo', 'bo')}
    del _L0_xattn_all

    def _L0_ffn_setup():
        import jax, jax.numpy as jnp
        import numpy as np
        NQ, NK, H, DH = (128, 64, 8, 64)
        key = jax.random.key(seed)
        ks = jax.random.split(key, 8)
        b, n, d, g = (4, 512, 128, 4)
        di = H * DH
        s = lambda fan: 1.0 / np.sqrt(fan)
        return {'x': jax.random.normal(ks[0], (b, n, d), jnp.float32), 'w_qr': jax.random.normal(ks[1], (g, d), jnp.float32) * s(d), 'w_kvr': jax.random.normal(ks[2], (g, d), jnp.float32) * s(d), 'w_q': jax.random.normal(ks[3], (g, di, d), jnp.float32) * s(d), 'w_kv': jax.random.normal(ks[4], (g, 2 * di, d), jnp.float32) * s(d), 'w_out': jax.random.normal(ks[5], (g, d, di), jnp.float32) * s(di), 'null_kv': jax.random.normal(ks[6], (2, g, H, 1, DH), jnp.float32), 'null_token': jax.random.normal(ks[7], (1, 1, d), jnp.float32)}
    _L0_ffn_all = _L0_ffn_setup()
    _L0_ffn_in = {k: v for k, v in _L0_ffn_all.items() if k in ('w_qr', 'w_kvr', 'w_q', 'w_kv', 'w_out', 'null_kv', 'null_token')}
    del _L0_ffn_all

    def _L1_xattn_setup():
        import jax, jax.numpy as jnp
        import numpy as np
        N_HEADS = 16
        key = jax.random.key(seed)
        ks = jax.random.split(key, 8)
        b, l, m = (8, 128, 128)
        d_embed, d_cross = (128, 96)
        s_q = 1.0 / np.sqrt(d_embed)
        s_kv = 1.0 / np.sqrt(d_cross)
        return {'x': jax.random.normal(ks[0], (b, l, d_embed), jnp.float32), 'y': jax.random.normal(ks[1], (b, m, d_cross), jnp.float32), 'Wq': jax.random.normal(ks[2], (d_embed, d_embed), jnp.float32) * s_q, 'bq': jax.random.normal(ks[3], (d_embed,), jnp.float32) * 0.01, 'Wkv': jax.random.normal(ks[4], (2 * d_embed, d_cross), jnp.float32) * s_kv, 'bkv': jax.random.normal(ks[5], (2 * d_embed,), jnp.float32) * 0.01, 'Wo': jax.random.normal(ks[6], (d_embed, d_embed), jnp.float32) * s_q, 'bo': jax.random.normal(ks[7], (d_embed,), jnp.float32) * 0.01}
    _L1_xattn_all = _L1_xattn_setup()
    _L1_xattn_in = {k: v for k, v in _L1_xattn_all.items() if k in ('Wq', 'bq', 'Wkv', 'bkv', 'Wo', 'bo')}
    del _L1_xattn_all

    def _L1_ffn_setup():
        import jax, jax.numpy as jnp
        import numpy as np
        D = 128
        E = 12
        HS = 2 * D
        HR = 3 * D
        TAU = 1.5

        def _geglu(h):
            a, g = jnp.split(h, 2, axis=-1)
            return a * jax.nn.gelu(g, approximate=False)
        key = jax.random.key(seed)
        ks = jax.random.split(key, 12)

        def xavier(k, shape):
            fan_in, fan_out = (shape[-2], shape[-1])
            lim = jnp.sqrt(6.0 / (fan_in + fan_out))
            return jax.random.uniform(k, shape, jnp.float32, -lim, lim)
        x = jax.random.normal(ks[0], (2, 128, D), jnp.float32)
        Ws1 = xavier(ks[1], (D, 2 * HS))
        bs1 = jnp.zeros((2 * HS,), jnp.float32)
        Ws2 = xavier(ks[2], (HS, D))
        bs2 = jnp.zeros((D,), jnp.float32)
        We1 = xavier(ks[3], (E, D, 2 * HR))
        be1 = jnp.zeros((E, 2 * HR), jnp.float32)
        We2 = xavier(ks[4], (E, HR, D))
        be2 = jnp.zeros((E, D), jnp.float32)
        Wr = xavier(ks[5], (D, E))
        br = jnp.zeros((E,), jnp.float32)
        return {'x': x, 'Ws1': Ws1, 'bs1': bs1, 'Ws2': Ws2, 'bs2': bs2, 'We1': We1, 'be1': be1, 'We2': We2, 'be2': be2, 'Wr': Wr, 'br': br}
    _L1_ffn_all = _L1_ffn_setup()
    _L1_ffn_in = {k: v for k, v in _L1_ffn_all.items() if k in ('Ws1', 'bs1', 'Ws2', 'bs2', 'We1', 'be1', 'We2', 'be2', 'Wr', 'br')}
    del _L1_ffn_all
    return {'x': x, 'ctx_768': ctx_768, 'g_xattn': g_xattn, 'g_ffn': g_ffn, 'L0_xattn_Wq': _L0_xattn_in['Wq'], 'L0_xattn_Wk': _L0_xattn_in['Wk'], 'L0_xattn_Wv': _L0_xattn_in['Wv'], 'L0_xattn_Wo': _L0_xattn_in['Wo'], 'L0_xattn_bo': _L0_xattn_in['bo'], 'L0_ffn_w_qr': _L0_ffn_in['w_qr'], 'L0_ffn_w_kvr': _L0_ffn_in['w_kvr'], 'L0_ffn_w_q': _L0_ffn_in['w_q'], 'L0_ffn_w_kv': _L0_ffn_in['w_kv'], 'L0_ffn_w_out': _L0_ffn_in['w_out'], 'L0_ffn_null_kv': _L0_ffn_in['null_kv'], 'L0_ffn_null_token': _L0_ffn_in['null_token'], 'L1_xattn_Wq': _L1_xattn_in['Wq'], 'L1_xattn_bq': _L1_xattn_in['bq'], 'L1_xattn_Wkv': _L1_xattn_in['Wkv'], 'L1_xattn_bkv': _L1_xattn_in['bkv'], 'L1_xattn_Wo': _L1_xattn_in['Wo'], 'L1_xattn_bo': _L1_xattn_in['bo'], 'L1_ffn_Ws1': _L1_ffn_in['Ws1'], 'L1_ffn_bs1': _L1_ffn_in['bs1'], 'L1_ffn_Ws2': _L1_ffn_in['Ws2'], 'L1_ffn_bs2': _L1_ffn_in['bs2'], 'L1_ffn_We1': _L1_ffn_in['We1'], 'L1_ffn_be1': _L1_ffn_in['be1'], 'L1_ffn_We2': _L1_ffn_in['We2'], 'L1_ffn_be2': _L1_ffn_in['be2'], 'L1_ffn_Wr': _L1_ffn_in['Wr'], 'L1_ffn_br': _L1_ffn_in['br']}

def reference(x, ctx_768, g_xattn, g_ffn, L0_xattn_Wq, L0_xattn_Wk, L0_xattn_Wv, L0_xattn_Wo, L0_xattn_bo, L0_ffn_w_qr, L0_ffn_w_kvr, L0_ffn_w_q, L0_ffn_w_kv, L0_ffn_w_out, L0_ffn_null_kv, L0_ffn_null_token, L1_xattn_Wq, L1_xattn_bq, L1_xattn_Wkv, L1_xattn_bkv, L1_xattn_Wo, L1_xattn_bo, L1_ffn_Ws1, L1_ffn_bs1, L1_ffn_Ws2, L1_ffn_bs2, L1_ffn_We1, L1_ffn_be1, L1_ffn_We2, L1_ffn_be2, L1_ffn_Wr, L1_ffn_br):
    import jax
    import jax.numpy as jnp

    def _L0_xattn_ref(x, context, Wq, Wk, Wv, Wo, bo):
        import jax, jax.numpy as jnp
        import numpy as np
        B, N, M = (8, 512, 77)
        Q_DIM, CTX_DIM = (128, 96)
        H, D = (16, 64)
        INNER = H * D
        scale = D ** (-0.5)

        def heads(t):
            b, s, _ = t.shape
            return t.reshape(b, s, H, D).transpose(0, 2, 1, 3)
        q = heads(x @ Wq)
        k = heads(context @ Wk)
        v = heads(context @ Wv)
        scores = jnp.einsum('bhid,bhjd->bhij', q, k) * scale
        attn = jax.nn.softmax(scores, axis=-1)
        out = jnp.einsum('bhij,bhjd->bhid', attn, v)
        out = out.transpose(0, 2, 1, 3).reshape(x.shape[0], x.shape[1], INNER)
        return out @ Wo + bo

    def _L0_ffn_ref(x, w_qr, w_kvr, w_q, w_kv, w_out, null_kv, null_token):
        import jax, jax.numpy as jnp
        import numpy as np
        NQ, NK, H, DH = (128, 64, 8, 64)
        b, n, d = x.shape
        g = w_qr.shape[0]
        bidx = jnp.arange(b)[:, None, None]
        q_logits = jnp.einsum('bnd,gd->bgn', x, w_qr)
        q_top, q_idx = jax.lax.top_k(q_logits, NQ)
        q_scores = jax.nn.sigmoid(q_top)[..., None]
        queries = x[bidx, q_idx]
        kv_logits = jnp.einsum('bnd,gd->bgn', x, w_kvr)
        kv_top, kv_idx = jax.lax.top_k(kv_logits, NK)
        kv_scores = jax.nn.sigmoid(kv_top)[:, :, None, :, None]
        key_values = x[bidx, kv_idx]
        q = jnp.einsum('bgnd,ged->bgne', queries, w_q)
        kv = jnp.einsum('bgnd,ged->bgne', key_values, w_kv)
        k, v = jnp.split(kv, 2, axis=-1)
        heads = lambda t: t.reshape(b, g, -1, H, DH).transpose(0, 1, 3, 2, 4)
        q, k, v = (heads(q), heads(k), heads(v))
        v = v * kv_scores
        nk = jnp.broadcast_to(null_kv[0][None], (b, g, H, 1, DH))
        nv = jnp.broadcast_to(null_kv[1][None], (b, g, H, 1, DH))
        k = jnp.concatenate([nk, k], axis=-2)
        v = jnp.concatenate([nv, v], axis=-2)
        attn = jax.nn.softmax(jnp.einsum('bghid,bghjd->bghij', q, k) * DH ** (-0.5), axis=-1)
        o = jnp.einsum('bghij,bghjd->bghid', attn, v)
        o = o.transpose(0, 1, 3, 2, 4).reshape(b, g, NQ, H * DH)
        o = jnp.einsum('bgne,gde->bgnd', o, w_out)
        o = o * q_scores
        flat_idx = q_idx.reshape(b, g * NQ)
        flat_o = o.reshape(b, g * NQ, d)
        b2 = jnp.arange(b)[:, None]
        summed = jnp.zeros_like(x).at[b2, flat_idx].add(flat_o)
        counts = jnp.zeros((b, n), x.dtype).at[b2, flat_idx].add(1.0)[..., None]
        meaned = summed / jnp.clip(counts, 1e-05)
        return jnp.where(counts > 0, meaned, null_token)

    def _L1_xattn_ref(x, y, Wq, bq, Wkv, bkv, Wo, bo):
        import jax, jax.numpy as jnp
        import numpy as np
        N_HEADS = 16
        b, l, d = x.shape
        m = y.shape[1]
        h = N_HEADS
        dh = d // h
        q = (jnp.einsum('bld,ed->ble', x, Wq) + bq).reshape(b, l, h, dh)
        kv = (jnp.einsum('bmc,ec->bme', y, Wkv) + bkv).reshape(b, m, h, 2 * dh)
        k, v = (kv[..., :dh], kv[..., dh:])
        scale = 1.0 / jnp.sqrt(jnp.asarray(dh, x.dtype))
        att = jax.nn.softmax(jnp.einsum('blhd,bmhd->blmh', q, k) * scale, axis=2)
        out = jnp.einsum('blmh,bmhd->blhd', att, v).reshape(b, l, d)
        return jnp.einsum('bld,ed->ble', out, Wo) + bo

    def _L1_ffn_ref(x, Ws1, bs1, Ws2, bs2, We1, be1, We2, be2, Wr, br):
        import jax, jax.numpy as jnp
        import numpy as np
        D = 128
        E = 12
        HS = 2 * D
        HR = 3 * D
        TAU = 1.5

        def _geglu(h):
            a, g = jnp.split(h, 2, axis=-1)
            return a * jax.nn.gelu(g, approximate=False)
        B, T, Dm = x.shape
        xf = x.reshape(-1, Dm)
        ys = _geglu(xf @ Ws1 + bs1) @ Ws2 + bs2
        logits = (xf @ Wr + br) / TAU
        top_val, top_idx = jax.lax.top_k(logits, 2)
        top_w = jax.nn.softmax(top_val, axis=-1)
        onehot = jax.nn.one_hot(top_idx, E, dtype=x.dtype)
        w = jnp.einsum('nke,nk->ne', onehot, top_w)
        h = jnp.einsum('nd,edh->enh', xf, We1) + be1[:, None, :]
        act = _geglu(h)
        yE = jnp.einsum('enh,ehd->end', act, We2) + be2[:, None, :]
        yr = jnp.einsum('end,ne->nd', yE, w)
        return (ys + yr).reshape(B, T, Dm)
    x = x + jnp.tanh(g_xattn[0]) * _L0_xattn_ref(_layernorm(x, axis=-1), ctx_768, L0_xattn_Wq, L0_xattn_Wk, L0_xattn_Wv, L0_xattn_Wo, L0_xattn_bo)
    x = x + jnp.tanh(g_ffn[0]) * _L0_ffn_ref(_layernorm(x, axis=-1), L0_ffn_w_qr, L0_ffn_w_kvr, L0_ffn_w_q, L0_ffn_w_kv, L0_ffn_w_out, L0_ffn_null_kv, L0_ffn_null_token)
    x = x + jnp.tanh(g_xattn[1]) * _L1_xattn_ref(_layernorm(x, axis=-1), ctx_768, L1_xattn_Wq, L1_xattn_bq, L1_xattn_Wkv, L1_xattn_bkv, L1_xattn_Wo, L1_xattn_bo)
    x = x + jnp.tanh(g_ffn[1]) * _L1_ffn_ref(_layernorm(x, axis=-1), L1_ffn_Ws1, L1_ffn_bs1, L1_ffn_Ws2, L1_ffn_bs2, L1_ffn_We1, L1_ffn_be1, L1_ffn_We2, L1_ffn_be2, L1_ffn_Wr, L1_ffn_br)
    return x

_drawn_inputs = setup_inputs


def setup_inputs(seed=0):
    import zlib

    import numpy as np

    out = dict(_drawn_inputs(seed))
    spreads = {'g_ffn': (-1.0, 0.6),
     'L1_ffn_bs1': (0.0, 0.1),
     'L1_ffn_bs2': (0.0, 0.1),
     'L1_ffn_be1': (0.0, 0.296),
     'L1_ffn_be2': (0.0, 0.1),
     'L1_ffn_br': (0.0, 0.282)}
    factors = {'L0_xattn_bo': 3.7,
     'L0_ffn_null_kv': 4.596,
     'L1_xattn_bq': 25.601,
     'L1_xattn_bkv': 4.556,
     'L1_xattn_bo': 4.507}
    for name, (base, spread) in spreads.items():
        noise = np.random.default_rng([zlib.crc32(name.encode()), seed]).standard_normal(out[name].shape)
        drawn = base * np.exp(spread * noise) if base else spread * noise
        out[name] = jnp.asarray(drawn.astype(out[name].dtype))
    for name, factor in factors.items():
        out[name] = (out[name] * factor).astype(out[name].dtype)
    return out
```

```python
from contextlib import ExitStack

import concourse.bass as bass
from concourse import mybir

P = 128
F32 = mybir.dt.float32
F16 = mybir.dt.float16
ALU = mybir.AluOpType
ACT = mybir.ActivationFunctionType
AX_X = mybir.AxisListType.X

NB, S, D = 8, 256, 128
NT = NB * S // P
TB = S // P
C, T = 96, 1601
C1 = C + 1
H = 16
NP = H // 2
KT = (T + P - 1) // P
KLAST = T - (KT - 1) * P
E0 = 64
EPS = 1e-5
SPLIT = 64.0
UNSPLIT = 1.0 / (SPLIT * SPLIT)
CHUNK = [(0, 401), (401, 400), (801, 400), (1201, 400)]
NC = len(CHUNK)
UNITS = H * TB


def keys(t):
    return P if t < KT - 1 else KLAST


class Chain:

    def __init__(self, eng, sem, base=0):
        self.eng, self.sem, self.base, self.n = eng, sem, base, 0

    def step(self, ins):
        ins.then_inc(self.sem, 1)
        self.n += 1
        self.eng.wait_ge(self.sem, self.base + self.n)


class Pool_:

    def __init__(self, nc, ctx, tag):
        self.nc, self.ctx, self.tag = nc, ctx, tag

    def sb(self, name, shape, dt=F32):
        return self.ctx.enter_context(self.nc.sbuf_tensor(f"{self.tag}_{name}", shape, dt))

    def ps(self, name, shape, dt=F32):
        return self.ctx.enter_context(self.nc.psum_tensor(f"{self.tag}_{name}", shape, dt))

    def sem(self, name):
        return self.ctx.enter_context(self.nc.semaphore(f"{self.tag}_{name}"))


def layernorm(nc, tag, x, xn, xnT, ident):
    with ExitStack() as ctx:
        m = Pool_(nc, ctx, tag)
        stats = m.sb("stats", [P, NT, 6])
        mv = m.sb("mv", [P, NT, 2])
        var = m.sb("var", [P, NT])
        std = m.sb("std", [P, NT])
        r = m.sb("r", [P, NT])
        e = m.sb("e", [P, NT])
        pt = m.ps("pt", [P, 4, 4 * P])
        own = m.sem("own")
        var_ready = m.sem("var_ready")
        std_ready = m.sem("std_ready")
        xn_ready = m.sem("xn_ready")
        turned = m.sem("turned")
        xnt_ready = m.sem("xnt_ready")
        stat_ready = m.sem("stat_ready")
        with nc.Block() as block:
            @block.vector
            def _(dve):
                for t in range(NT):
                    dve.bn_stats(stats[:, t, :], x[:, t, :]).then_inc(stat_ready, 1)
                for t in range(NT):
                    dve.wait_ge(stat_ready, t + 1)
                    dve.bn_aggr(mv[:, t, :], stats[:, t, :]).then_inc(stat_ready, 1)
                dve.wait_ge(stat_ready, 2 * NT)
                dve.tensor_scalar(var[:, :], mv[:, :, 1], EPS, None, ALU.add).then_inc(var_ready, 1)
                dve.wait_ge(std_ready, 1)
                c = Chain(dve, own)
                c.step(dve.reciprocal(r[:, :], std[:, :]))
                c.step(dve.tensor_tensor(e[:, :], r[:, :], r[:, :], ALU.mult))
                c.step(dve.tensor_tensor(e[:, :], e[:, :], var[:, :], ALU.mult))
                c.step(dve.tensor_scalar(e[:, :], e[:, :], -0.5, 1.5, ALU.mult, ALU.add))
                c.step(dve.tensor_tensor(r[:, :], r[:, :], e[:, :], ALU.mult))
                for t in range(NT):
                    dve.tensor_scalar(xn[:, t, :], x[:, t, :], mv[:, t, 0:1], r[:, t:t + 1],
                                      ALU.subtract, ALU.mult).then_inc(xn_ready, 1)

            @block.tensor
            def _(pe):
                for t in range(NT):
                    pe.wait_ge(xn_ready, t + 1)
                    pe.transpose(pt[:, t // 4, (t % 4) * P:(t % 4 + 1) * P], xn[:, t, :],
                                 ident[:, :]).then_inc(turned, 1)

            @block.scalar
            def _(act):
                act.wait_ge(var_ready, 1)
                act.activation(std[:, :], var[:, :], ACT.Sqrt).then_inc(std_ready, 1)
                for g in range(NT // 4):
                    act.wait_ge(turned, 4 * g + 4)
                    act.activation(xnT[:, 4 * g * P:4 * (g + 1) * P], pt[:, g, :],
                                   ACT.Copy).then_inc(xnt_ready, 1)


def wide_setup(nc, A, wide_M, wide_VO, gate):
    HB = 4
    with ExitStack() as ctx:
        m = Pool_(nc, ctx, "ws")
        wq = m.sb("wq", [E0, H, D])
        wk = m.sb("wk", [E0, H, C])
        wv = m.sb("wv", [E0, H, C])
        wo = m.sb("wo", [E0, H, D])
        pm = m.ps("pm", [P, 2, HB, 128])
        pv = m.ps("pv", [P, 2, HB, 128])
        loaded = m.sem("loaded")
        product = m.sem("product")
        kept = m.sem("kept")
        cleared = m.sem("cleared")
        with nc.Block() as block:
            @block.sync
            def _(sp):
                for sb_, dram in ((wq, A["a_wq"]), (wk, A["a_wk"]), (wv, A["a_wv"]), (wo, A["a_wo"])):
                    sp.dma_start(sb_[:, :, :], dram).then_inc(loaded, 16)

            @block.tensor
            def _(pe):
                pe.wait_ge(loaded, 64)
                for g in range(H // HB):
                    if g >= 2:
                        pe.wait_ge(kept, 2 * (g - 1))
                    for j in range(HB):
                        h = g * HB + j
                        pe.matmul(pm[:, g % 2, j, 0:C], wq[:, h, :], wk[:, h, :], start=True, stop=True)
                        ins = pe.matmul(pv[0:C, g % 2, j, :], wv[:, h, :], wo[:, h, :], start=True, stop=True)
                    ins.then_inc(product, 1)

            @block.vector
            def _(dve):
                dve.memset(wide_VO[:, :, :], 0.0).then_inc(cleared, 1)
                dve.wait_ge(cleared, 1)
                dve.memset(wide_VO[C:C1, :, D:D + 1], 1.0)
                for g in range(H // HB):
                    dve.wait_ge(product, g + 1)
                    dve.tensor_scalar(wide_M[:, g * HB:(g + 1) * HB, :], pm[:, g % 2, :, 0:C],
                                      SPLIT * E0 ** -0.5, None, ALU.mult).then_inc(kept, 1)
                    dve.tensor_scalar(wide_VO[0:C, g * HB:(g + 1) * HB, 0:D], pv[0:C, g % 2, :, :],
                                      gate[0:C, 0:1], None, ALU.mult).then_inc(kept, 1)


RING = 3
PRING = 4
PAIR = 2 * S


def score_slot(t):
    return t % RING if t < KT - 1 else RING


def prob_slot(t):
    return t % PRING if t < KT - 1 else PRING


def since_last(t, ring):
    if t == KT - 1:
        return KT
    return ring if t >= ring else ring + 1


def over_batches(eng, batch):
    batch(0, 0, True)
    with eng.Fori(0, NB // 2 - 1) as i:
        batch(2 * i + 1, 1, True)
        batch(2 * i + 2, 0, True)
    batch(NB - 1, 1, False)


def pair_before(b, p):
    if isinstance(p, int) and p == 0:
        return None if isinstance(b, int) and b == 0 else (b - 1, NP - 1)
    return b, p - 1


def over_pairs(eng, pair, prepares):
    first, middle, last = ("first", "middle", "last") if prepares else ("idle",) * 3
    pair(0, 0, first, 0)
    with eng.Fori(0, NP // 2 - 1) as i:
        pair(2 * i + 1, 1, middle, i)
        pair(2 * i + 2, 0, middle, i + 1)
    pair(NP - 1, 1, last, NP // 2 - 1)


def wide_attention(nc, A, x, xnT, wide_M, wide_VO, bias, ident):
    MAXIMA = 2 * TB * NC
    FIRST = NP + NP * MAXIMA + 1
    BATCH = NP + NP * MAXIMA + 1 + TB * NP
    with ExitStack() as ctx:
        m = Pool_(nc, ctx, "wa")
        ctxT = m.sb("ctxT", [C1, T])
        ch = m.sb("ctx_hi", [C1, 2, T], F16)
        cl = m.sb("ctx_lo", [C1, 2, T], F16)
        rows = m.sb("ctx_rows", [P, 2, KT, C1])
        qh = m.sb("q_hi", [C1, 2, H * S], F16)
        ql = m.sb("q_lo", [C1, 2, H * S], F16)
        prob = m.sb("prob", [P, PRING + 1, PAIR])
        acc = m.sb("acc", [C1, 2, PAIR])
        mx = m.sb("mx", [P, UNITS * NC])
        mu = m.sb("mu", [P, UNITS])
        shift = m.sb("shift", [UNITS, P], F16)
        rec = m.sb("rec", [P, 2])
        scores = m.ps("scores", [P, RING + 1, PAIR])
        helper = m.ps("helper", [P, 2, 512])
        pacc = m.ps("pacc", [P, 2, PAIR])

        ctxT_in = m.sem("ctxT_in")
        rows_in = m.sem("rows_in")
        scaled = m.sem("scaled")
        split = m.sem("split")
        q_hi_ready = m.sem("q_hi_ready")
        filled = m.sem("helper_filled")
        freed = m.sem("helper_freed")
        mu_ready = m.sem("mu_ready")
        shift_in = m.sem("shift_in")
        scores_ready = m.sem("scores_ready")
        exp_done = m.sem("exp_done")
        pv_done = m.sem("pv_done")
        acc_ready = m.sem("acc_ready")
        x_step = m.sem("x_step")

        def maxima(kind, t):
            if kind == "first":
                return range(4 * (t - NP), 4 * (t - NP + 1)) if NP <= t < NP + 4 else range(0)
            if kind == "middle":
                return range(MAXIMA * t // KT, MAXIMA * (t + 1) // KT)
            return range(2 * t, 2 * t + 2) if kind == "last" and t < 8 else range(0)

        def fills_before(p, kind):
            if kind == "idle":
                return TB * (p - 1)
            return NP + MAXIMA + (MAXIMA + TB) * (p - 1)

        def start_fill(b, p, kind, par):
            if isinstance(p, int) and p == 0:
                off = 0 if isinstance(b, int) and b == 0 else -TB
            else:
                off = fills_before(p, kind)
            even = NP + MAXIMA if kind not in ("idle",) else 0
            even = 0 if isinstance(p, int) and p == 0 else even
            return FIRST + BATCH * b + off, (FIRST + BATCH * par + even) % 2

        with nc.Block() as block:
            @block.sync
            def _(sp):
                def load_T(b):
                    if b >= 1:
                        sp.wait_ge(split, b)
                    sp.dma_start(ctxT[:, :], A["ctxT"][b]).then_inc(ctxT_in, 16)

                def load_rows(b):
                    if b >= 2:
                        sp.wait_ge(pv_done, KT + (b - 1) * NP * KT)
                    sp.dma_start(rows[:, b % 2, :, :], A["ctx_rows"][b]).then_inc(rows_in, 16)

                def put_shift(b):
                    n = FIRST if b == 0 else FIRST + BATCH * b - TB
                    sp.wait_ge(freed, n)
                    sp.dma_start(qh[C:C1, b % 2, :].rearrange("a (u q) -> a u q", u=UNITS),
                                 shift[:, :]).then_inc(shift_in, 16)

                load_T(0)
                load_rows(0)
                load_T(1)
                load_rows(1)
                put_shift(0)
                for b in range(1, NB):
                    if b + 1 < NB:
                        load_T(b + 1)
                    put_shift(b)
                    if b + 1 < NB:
                        load_rows(b + 1)

            @block.gpsimd
            def _(pool):
                for b in range(NB):
                    pool.wait_ge(ctxT_in, 16 * (b + 1))
                    pool.tensor_scalar(ctxT[:, :], ctxT[:, :], SPLIT, None, ALU.mult).then_inc(scaled, 1)
                    if b >= 2:
                        pool.wait_ge(scores_ready, (b - 1) * NP * KT)
                    pool.wait_ge(scaled, 2 * b + 1)
                    pool.tensor_copy(ch[:, b % 2, :], ctxT[:, :]).then_inc(scaled, 1)
                    pool.wait_ge(scaled, 2 * b + 2)
                    pool.tensor_tensor(cl[:, b % 2, :], ctxT[:, :], ch[:, b % 2, :],
                                       ALU.subtract).then_inc(split, 1)

            @block.tensor
            def _(pe):
                def fill(f):
                    if not (isinstance(f, int) and f < 2):
                        pe.wait_ge(freed, f - 1)

                def q_product(nb, j, f, bank):
                    fill(f)
                    for i in range(2):
                        ins = pe.matmul(helper[0:C, bank, i * S:(i + 1) * S], wide_M[:, 2 * j + i, :],
                                        xnT[:, bass.ds(nb * S, S)], start=True, stop=True)
                    ins.then_inc(filled, 1)

                def maximum(buf, p, k, f, bank):
                    c0, w = CHUNK[k % NC]
                    fill(f)
                    pe.matmul(helper[:, bank, 0:w], qh[0:C, buf, bass.ds((4 * p + k // NC) * P, P)],
                              ch[0:C, buf, c0:c0 + w], start=True, stop=True).then_inc(filled, 1)

                def turn_mu(nb, f, bank):
                    pe.wait_ge(mu_ready, nb + 1)
                    fill(f)
                    pe.transpose(helper[0:UNITS, bank, 0:P], mu[:, :], ident[:, :]).then_inc(filled, 1)

                def score(b, p, buf, t):
                    n = (b * NP + p) * KT + t
                    if t == 0 and isinstance(p, int) and p == 0:
                        pe.wait_ge(shift_in, 16 * b + 16)
                    pe.wait_ge(exp_done, KT + n - since_last(t, RING) + 1)
                    out = scores[0:keys(t), score_slot(t), :]
                    kk = slice(t * P, t * P + keys(t))
                    qq = bass.ds(p * PAIR, PAIR)
                    pe.matmul(out, ch[:, buf, kk], qh[:, buf, qq], start=True, stop=False)
                    pe.matmul(out, ch[0:C, buf, kk], ql[0:C, buf, qq], start=False, stop=False)
                    pe.matmul(out, cl[0:C, buf, kk], qh[0:C, buf, qq],
                              start=False, stop=True).then_inc(scores_ready, 1)

                def project(b, p, par, f, bank):
                    pe.wait_ge(acc_ready, b * NP + p + 3)
                    for i in range(TB):
                        fill(f + i)
                        for j in range(2):
                            ins = pe.matmul(helper[:, (bank + i) % 2, j * (D + 1):(j + 1) * (D + 1)],
                                            acc[:, par, j * S + i * P:j * S + (i + 1) * P],
                                            wide_VO[:, 2 * p + j, :], start=True, stop=True)
                        ins.then_inc(filled, 1)

                def batch(b, buf, prepares):
                    def pair(p, par, kind, _):
                        f, bank = start_fill(b, p, kind, buf)
                        n = (b * NP + p) * KT
                        before = pair_before(b, p)
                        if kind == "first":
                            pe.wait_ge(split, b + 2)
                        k = 0
                        for t in range(KT):
                            if t + 2 < KT:
                                score(b, p, buf, t + 2)
                            elif kind == "last":
                                score(b + 1, 0, 1 - buf, t + 2 - KT)
                            elif not (isinstance(p, int) and p == NP - 1):
                                score(b, p + 1, buf, t + 2 - KT)
                            if kind == "first" and t < NP:
                                q_product(b + 1, t, f + k, (bank + k) % 2)
                                k += 1
                            for i in maxima(kind, t):
                                if i == 0:
                                    pe.wait_ge(q_hi_ready, NP * (b + 1) + p + 1)
                                maximum(1 - buf, p, i, f + k, (bank + k) % 2)
                                k += 1
                            if t == 2 and before:
                                project(*before, 1 - par, f + k, (bank + k) % 2)
                                k += TB
                            if kind == "last" and t == NP + 1:
                                turn_mu(b + 1, f + k, (bank + k) % 2)
                                k += 1
                            if t == 0:
                                pe.wait_ge(acc_ready, b * NP + p + 1)
                                if isinstance(p, int) and p == 0:
                                    pe.wait_ge(rows_in, 16 * b + 16)
                            pe.wait_ge(exp_done, KT + n + t + 1)
                            pe.matmul(pacc[0:C1, par, :], rows[0:keys(t), buf, t, :],
                                      prob[0:keys(t), prob_slot(t), :], start=(t == 0),
                                      stop=(t == KT - 1)).then_inc(pv_done, 1)
                        if kind == "idle" and isinstance(p, int) and p == NP - 1:
                            project(b, p, par, f + k, (bank + k) % 2)
                    over_pairs(pe, pair, prepares)

                pe.wait_ge(split, 1)
                for j in range(NP):
                    q_product(0, j, j, j % 2)
                pe.wait_ge(q_hi_ready, NP)
                with pe.Fori(0, NP) as p:
                    for k in range(MAXIMA):
                        maximum(0, p, k, NP + MAXIMA * p + k, k % 2)
                turn_mu(0, FIRST - 1, (FIRST - 1) % 2)
                for t in range(2):
                    score(0, 0, 0, t)
                over_batches(pe, batch)

            @block.scalar
            def _(act):
                act.sem_inc(exp_done, KT)
                act.sem_inc(acc_ready, 2)

                def keep_q_hi(nb, buf, j, f, bank):
                    act.wait_ge(filled, f + 1)
                    act.activation(qh[0:C, buf, j * PAIR:(j + 1) * PAIR], helper[0:C, bank, :],
                                   ACT.Copy).then_inc(q_hi_ready, 1)

                def keep_acc(b, p, par):
                    act.wait_ge(pv_done, KT * (b * NP + p + 2))
                    act.activation(acc[:, par, :], pacc[0:C1, par, :], ACT.Copy).then_inc(acc_ready, 1)

                def batch(b, buf, prepares):
                    def pair(p, par, kind, _):
                        f, bank = start_fill(b, p, kind, buf)
                        before = pair_before(b, p)
                        n = (b * NP + p) * KT
                        for t in range(KT):
                            act.wait_ge(scores_ready, n + t + 1)
                            act.wait_ge(pv_done, KT + n + t - since_last(t, PRING) + 1)
                            act.activation(prob[0:keys(t), prob_slot(t), :],
                                           scores[0:keys(t), score_slot(t), :], ACT.Exp,
                                           scale=UNSPLIT).then_inc(exp_done, 1)
                            if t == 0 and before:
                                keep_acc(*before, 1 - par)
                            if kind == "first" and t < NP:
                                k = t + TB if before and t > 2 else t
                                keep_q_hi(b + 1, 1 - buf, t, f + k, (bank + k) % 2)
                        if kind == "idle" and isinstance(p, int) and p == NP - 1:
                            keep_acc(b, p, par)
                    over_pairs(act, pair, prepares)

                for j in range(NP):
                    keep_q_hi(0, 0, j, j, j % 2)
                over_batches(act, batch)

            @block.vector
            def _(dve):
                dve.sem_inc(pv_done, KT)
                dve.tensor_tensor(x[:, :, :], x[:, :, :], bias[:, None, :].to_broadcast([P, NT, D]),
                                  ALU.add).then_inc(x_step, 1)
                dve.wait_ge(x_step, 1)

                def keep_q_lo(nb, buf, j, f, bank):
                    dve.wait_ge(q_hi_ready, NP * nb + j + 1)
                    cols = slice(j * PAIR, (j + 1) * PAIR)
                    dve.tensor_tensor(ql[0:C, buf, cols], helper[0:C, bank, :], qh[0:C, buf, cols],
                                      ALU.subtract).then_inc(freed, 1)

                def maximum(p, k, f, bank):
                    w = CHUNK[k % NC][1]
                    dve.wait_ge(filled, f + 1)
                    dve.tensor_reduce(mx[:, bass.ds(MAXIMA * p + k, 1)], helper[:, bank, 0:w], AX_X,
                                      ALU.max).then_inc(freed, 1)

                def gather_mu(f):
                    dve.wait_ge(freed, f)
                    dve.tensor_reduce(mu[:, :], mx[:, :].rearrange("p (u c) -> p u c", c=NC), AX_X,
                                      ALU.max).then_inc(mu_ready, 1)

                def keep_shift(nb, f, bank):
                    dve.wait_ge(filled, f + 1)
                    if not (isinstance(nb, int) and nb == 0):
                        dve.wait_ge(shift_in, 16 * nb)
                    dve.tensor_scalar(shift[:, :], helper[0:UNITS, bank, 0:P], -1.0 / SPLIT, None,
                                      ALU.mult).then_inc(freed, 1)

                def add_out(b, p, f, bank):
                    for i in range(TB):
                        v = helper[:, (bank + i) % 2, 0:2 * (D + 1)].rearrange("p (a c) -> p a c", c=D + 1)
                        xt = x[:, TB * b + i, :]
                        s = 2 * (TB * (b * NP + p) + i) + 1
                        dve.wait_ge(filled, f + i + 1)
                        dve.wait_ge(freed, f + i)
                        dve.reciprocal(rec[:, :], v[:, :, D]).then_inc(x_step, 1)
                        dve.wait_ge(x_step, s + 1)
                        dve.scalar_tensor_tensor(xt, v[:, 0, 0:D], rec[:, 0:1], xt, ALU.mult,
                                                 ALU.add).then_inc(x_step, 1)
                        dve.wait_ge(x_step, s + 2)
                        dve.scalar_tensor_tensor(xt, v[:, 1, 0:D], rec[:, 1:2], xt, ALU.mult,
                                                 ALU.add).then_inc(freed, 1)

                def batch(b, buf, prepares):
                    def pair(p, par, kind, _):
                        f, bank = start_fill(b, p, kind, buf)
                        before = pair_before(b, p)
                        k = 0
                        for t in range(KT):
                            if kind == "first" and t < NP:
                                keep_q_lo(b + 1, 1 - buf, t, f + k, (bank + k) % 2)
                                k += 1
                            for i in maxima(kind, t):
                                maximum(p, i, f + k, (bank + k) % 2)
                                k += 1
                            if t == 2 and before:
                                add_out(*before, f + k, (bank + k) % 2)
                                k += TB
                            if kind == "last" and t == NP:
                                gather_mu(f + k)
                            if kind == "last" and t == NP + 1:
                                keep_shift(b + 1, f + k, (bank + k) % 2)
                                k += 1
                        if kind == "idle" and isinstance(p, int) and p == NP - 1:
                            add_out(b, p, f + k, (bank + k) % 2)
                    over_pairs(dve, pair, prepares)

                for j in range(NP):
                    keep_q_lo(0, 0, j, j, j % 2)
                with dve.Fori(0, NP) as p:
                    for k in range(MAXIMA):
                        maximum(p, k, NP + MAXIMA * p + k, k % 2)
                gather_mu(FIRST - 1)
                keep_shift(0, FIRST - 1, (FIRST - 1) % 2)
                over_batches(dve, batch)


G, NQ, NK, HR, E = 4, 128, 64, 8, 64
KK = NK + 1
CH = HR * E // P


def routed_attention(nc, A, x, xn, xnT, null, gate, ident):
    with ExitStack() as ctx:
        m = Pool_(nc, ctx, "ra")
        wq = m.sb("wq", [D, G, HR * E])
        wk = m.sb("wk", [D, G, HR * E])
        wv = m.sb("wv", [D, G, HR * E])
        wo = m.sb("wo", [P, G, CH, D])
        wr = m.sb("router", [D, G, 2, P])
        before = m.sb("before", [P, TB, S])
        ranks = m.sb("ranks", [P, NK])
        xb = m.sb("xb", [P, TB, D])
        Ls = m.sb("logits", [P, 2, S])
        dg = m.sb("diag", [P, TB, 2, P])
        junk = m.sb("junk", [P, S])
        li = m.sb("own_logit", [P, 2, TB, 2])
        later = m.sb("larger", [P, TB, 2])
        ties = m.sb("ties", [P, TB, 2])
        rank = m.sb("rank", [P, TB, 2])
        sel = m.sb("sel", [P, 2, TB, NK])
        mask = m.sb("mask", [P, 2, TB])
        exq = m.sb("exq", [P, 2, TB])
        qs = m.sb("q_score", [P, 2, TB])
        cnt = m.sb("count", [P, TB])
        inv = m.sb("inverse", [P, TB])
        none = m.sb("none", [P, TB])
        ksT = m.sb("keysT", [D, 2, NK])
        exk = m.sb("exk", [NK, 2])
        kvs = m.sb("kv_score", [NK, 2])
        kT = m.sb("kT", [P, 2, CH, KK])
        V = m.sb("V", [KK, 2, HR * E])
        nk = m.sb("null_k", [P, G, CH])
        nv = m.sb("null_v", [KK, G, HR * E])
        qT = m.sb("qT", [P, 2, CH, S])
        Pr = m.sb("prob", [P, TB, 2, CH, KK])
        m8 = m.sb("m8", [P, TB, 2, CH])
        r8 = m.sb("r8", [P, TB, 2, CH])
        PT = m.sb("PT", [KK, 2, CH, S])
        oT = m.sb("oT", [P, CH, S])
        summed = m.sb("summed", [P, TB, D])
        pA = m.ps("bank_logits", [P, 512])
        pM = m.ps("bank_keys", [P, 512])
        pV = m.ps("bank_values", [P, 512])
        pQ = m.ps("bank_q", [P, CH, S])
        pS = m.ps("bank_scores", [P, 2, 512])
        pT = m.ps("bank_turn", [P, 512])

        w_in = m.sem("w_in")
        const = m.sem("const")
        xb_ready = m.sem("xb_ready")
        L_full = m.sem("L_full")
        L_kept = m.sem("L_kept")
        own = m.sem("own")
        own_li = m.sem("li_ready")
        routed = m.sem("routed")
        exq_done = m.sem("exq_done")
        sel_full = m.sem("sel_full")
        ks_kept = m.sem("ks_kept")
        exk_done = m.sem("exk_done")
        kvs_done = m.sem("kvs_done")
        k_full = m.sem("k_full")
        v_full = m.sem("v_full")
        k_kept = m.sem("k_kept")
        null_in = m.sem("null_in")
        v_kept = m.sem("v_kept")
        q_full = m.sem("q_full")
        q_kept = m.sem("q_kept")
        s_full = m.sem("s_full")
        s_kept = m.sem("s_kept")
        e_done = m.sem("e_done")
        r_done = m.sem("r_done")
        p_ready = m.sem("p_ready")
        t_even = m.sem("t_even")
        t_odd = m.sem("t_odd")
        even_kept = m.sem("even_kept")
        odd_kept = m.sem("odd_kept")
        o_full = m.sem("o_full")
        o_kept = m.sem("o_kept")
        y_full = m.sem("y_full")
        y_kept = m.sem("y_kept")

        def steps(eng, step, first):
            first()
            with eng.Fori(0, NB - 1) as b:
                for g in range(G):
                    step(b, g, True)
            for g in range(G):
                step(NB - 1, g, g < G - 1)

        def following(b, g):
            return (b, g + 1) if g + 1 < G else (b + 1, 0)

        with nc.Block() as block:
            @block.sync
            def _(sp):
                for sb_, name in ((wr, "r_router"), (wq, "r_wq"), (wk, "r_wk"), (wv, "r_wv"), (wo, "r_wo"),
                                  (nk, "r_null_k")):
                    sp.dma_start(sb_[:], A[name]).then_inc(w_in, 16)
                sp.dma_start(nv[NK:KK, :, :], A["r_null_v"]).then_inc(w_in, 16)

            @block.gpsimd
            def _(pool):
                pool.iota(ranks[:, :], pattern=[[1, NK]], base=0, channel_multiplier=0,
                          allow_small_or_imprecise_dtypes=True).then_inc(const, 1)
                pool.memset(before[:, :, :], 1.0).then_inc(const, 1)
                pool.wait_ge(const, 2)
                pool.affine_select(out=before[:, :, :], in_=before[:, :, :], compare_op=ALU.is_gt, fill=0.0,
                                   base=0, pattern=[[P, TB], [-1, S]], channel_multiplier=1).then_inc(const, 1)

                def stage_x(b):
                    pool.tensor_copy(xb[:, :, :], xn[:, bass.ds(b * TB, TB), :]).then_inc(xb_ready, 1)

                def step(b, g, has_next):
                    s = b * G + g
                    if g == G - 1 and has_next:
                        pool.wait_ge(const, 3)
                        pool.wait_ge(sel_full, s + 1)
                        stage_x(b + 1)
                    for i in range(TB):
                        pool.wait_ge(r_done, TB * s + i + 1)
                        pool.tensor_tensor(Pr[:, i].rearrange("p e c k -> p (e c) k"),
                                           Pr[:, i].rearrange("p e c k -> p (e c) k"),
                                           r8[:, i].rearrange("p e c -> p (e c)")[:, :, None].to_broadcast([P, HR, KK]),
                                           ALU.mult).then_inc(p_ready, 1)

                steps(pool, step, lambda: stage_x(0))

            @block.tensor
            def _(pe):
                def logits(b, g):
                    s = b * G + g
                    pe.wait_ge(L_kept, s)
                    pe.wait_ge(odd_kept, 1 if isinstance(s, int) and s == 0 else TB * (s - 1) + 1)
                    for r in range(2):
                        ins = pe.matmul(pA[:, r * S:(r + 1) * S], wr[:, g, r, :], xnT[:, bass.ds(b * S, S)],
                                        start=True, stop=True)
                    ins.then_inc(L_full, 1)

                def queries(b, g):
                    s = b * G + g
                    pe.wait_ge(q_kept, s)
                    if not (isinstance(s, int) and s == 0):
                        pe.wait_ge(o_kept, s)
                    for c in range(CH):
                        ins = pe.matmul(pQ[:, c, :], wq[:, g, c * P:(c + 1) * P], xnT[:, bass.ds(b * S, S)],
                                        start=True, stop=True)
                    ins.then_inc(q_full, 1)

                def gather(b, g, par):
                    s = b * G + g
                    pe.wait_ge(routed, s + 1)
                    pe.wait_ge(xb_ready, b + 1)
                    pe.wait_ge(k_kept, s)
                    for i in range(TB):
                        pe.matmul(pM[:, 0:NK], xb[:, i, :], sel[:, par, i, :], start=(i == 0), stop=(i == TB - 1))
                    for i in range(TB):
                        ins = pe.matmul(pM[0:NK, NK:NK + 1], sel[:, par, i, :], li[:, par, i, 1:2],
                                        start=(i == 0), stop=(i == TB - 1))
                    ins.then_inc(sel_full, 1)

                def keys_values(b, g, par):
                    s = b * G + g
                    pe.wait_ge(ks_kept, s + 1)
                    pe.wait_ge(exk_done, s + 1)
                    for c in range(CH):
                        ins = pe.matmul(pM[:, P + c * NK:P + (c + 1) * NK], wk[:, g, c * P:(c + 1) * P],
                                        ksT[:, par, :], start=True, stop=True)
                    ins.then_inc(k_full, 1)
                    if not (isinstance(s, int) and s == 0):
                        pe.wait_ge(y_kept, TB * (s - 1) + 1)
                    pe.matmul(pV[0:NK, :], ksT[:, par, :], wv[:, g, :], start=True, stop=True).then_inc(v_full, 1)

                def first():
                    pe.wait_ge(w_in, 16 * 7)
                    logits(0, 0)
                    queries(0, 0)
                    gather(0, 0, 0)
                    keys_values(0, 0, 0)

                def step(b, g, has_next):
                    s = b * G + g
                    par = g % 2
                    nb, ng = following(b, g)
                    if has_next:
                        logits(nb, ng)
                    pe.wait_ge(q_kept, s + 1)
                    pe.wait_ge(k_kept, s + 1)
                    pe.wait_ge(null_in, s + 1)
                    for i in range(TB):
                        pe.wait_ge(s_kept, TB * s + i + 1)
                        for c in range(CH):
                            for e in range(2):
                                ins = pe.matmul(pS[:, e, c * KK:(c + 1) * KK],
                                                qT[e * E:(e + 1) * E, par, c, i * P:(i + 1) * P],
                                                kT[e * E:(e + 1) * E, par, c, :], start=True, stop=True)
                        ins.then_inc(s_full, 1)
                        if has_next and i == 0:
                            queries(nb, ng)
                    if has_next:
                        gather(nb, ng, 1 - par)
                        pe.wait_ge(L_kept, s + 2)
                    for i in range(TB):
                        pe.wait_ge(p_ready, TB * s + i + 1)
                        for e, (bank, kept, done) in enumerate(((pT, even_kept, t_even), (pA, odd_kept, t_odd))):
                            pe.wait_ge(kept, TB * s + i + 1)
                            for c in range(CH):
                                ins = pe.transpose(bank[0:KK, c * P:(c + 1) * P], Pr[:, i, e, c, :], ident[:, :])
                            ins.then_inc(done, 1)
                        if has_next and i == 0:
                            keys_values(nb, ng, 1 - par)
                    if has_next:
                        pe.wait_ge(q_kept, s + 2)
                    pe.wait_ge(even_kept, TB * (s + 1) + 1)
                    pe.wait_ge(odd_kept, TB * (s + 1) + 1)
                    pe.wait_ge(v_kept, s + 1)
                    for c in range(CH):
                        for e in range(2):
                            h = 2 * c + e
                            ins = pe.matmul(pQ[e * E:(e + 1) * E, c, :], V[:, par, h * E:(h + 1) * E],
                                            PT[:, e, c, :], start=True, stop=True)
                    ins.then_inc(o_full, 1)
                    pe.wait_ge(o_kept, s + 2)
                    if has_next:
                        pe.wait_ge(v_kept, s + 2)
                    for i in range(TB):
                        for c in range(CH):
                            ins = pe.matmul(pV[:, i * P:(i + 1) * P], oT[:, c, i * P:(i + 1) * P], wo[:, g, c, :],
                                            start=(c == 0), stop=(c == CH - 1))
                    ins.then_inc(y_full, 1)

                steps(pe, step, first)

            @block.scalar
            def _(act):
                act.sem_inc(even_kept, 1)
                act.sem_inc(o_kept, 1)

                def keep_logits(b, g):
                    s = b * G + g
                    act.wait_ge(L_full, s + 1)
                    act.wait_ge(routed, s)
                    act.activation(Ls[:, :, :].rearrange("p r n -> p (r n)"), pA[:, :], ACT.Copy).then_inc(L_kept, 1)

                def keep_queries(b, g, par):
                    s = b * G + g
                    act.wait_ge(q_full, s + 1)
                    act.activation(qT[:, par, :, :], pQ[:, :, :], ACT.Copy, scale=E ** -0.5).then_inc(q_kept, 1)

                def exp_scores(b, g, par):
                    s = b * G + g
                    act.wait_ge(own_li, s + 1)
                    act.activation(exq[:, par, :], li[:, par, :, 0], ACT.Exp, scale=-1.0).then_inc(exq_done, 1)
                    act.wait_ge(ks_kept, s + 1)
                    act.activation(exk[:, par:par + 1], pM[0:NK, NK:NK + 1], ACT.Exp, scale=-1.0).then_inc(exk_done, 1)

                def keep_keys_values(b, g, par):
                    s = b * G + g
                    act.wait_ge(k_full, s + 1)
                    act.activation(kT[:, par, :, 0:NK],
                                   pM[:, P:P + CH * NK].rearrange("p (c k) -> p c k", c=CH),
                                   ACT.Copy).then_inc(k_kept, 1)
                    act.wait_ge(v_full, s + 1)
                    act.wait_ge(kvs_done, s + 1)
                    act.activation(V[0:NK, par, :], pV[0:NK, :], ACT.Copy, scale=kvs[:, par:par + 1]).then_inc(v_kept, 1)

                def first():
                    keep_logits(0, 0)
                    keep_queries(0, 0, 0)
                    exp_scores(0, 0, 0)
                    keep_keys_values(0, 0, 0)

                def step(b, g, has_next):
                    s = b * G + g
                    par = g % 2
                    nb, ng = following(b, g)
                    if has_next:
                        keep_logits(nb, ng)
                    for i in range(TB):
                        act.wait_ge(s_kept, TB * s + i + 2)
                        act.activation(Pr[:, i], Pr[:, i], ACT.Exp).then_inc(e_done, 1)
                        if has_next and i == 0:
                            keep_queries(nb, ng, 1 - par)
                    if has_next:
                        exp_scores(nb, ng, 1 - par)
                    for i in range(TB):
                        act.wait_ge(t_even, TB * s + i + 1)
                        act.activation(PT[:, 0, :, i * P:(i + 1) * P],
                                       pT[0:KK, :].rearrange("p (c q) -> p c q", c=CH), ACT.Copy).then_inc(even_kept, 1)
                        if has_next and i == 0:
                            keep_keys_values(nb, ng, 1 - par)
                    act.wait_ge(o_full, s + 1)
                    act.activation(oT[:, :, :], pQ[:, :, :], ACT.Copy).then_inc(o_kept, 1)

                steps(act, step, first)

            @block.vector
            def _(dve):
                for kept in (s_kept, odd_kept, y_kept):
                    dve.sem_inc(kept, 1)
                FIRST_STEPS = 13
                BATCH_STEPS = G * (2 * TB + FIRST_STEPS + 4) + 4 + 2 * TB

                def route(c, b, g, par):
                    s = b * G + g
                    dve.wait_ge(L_kept, s + 1)
                    for i in range(TB):
                        c.step(dve.tensor_tensor(dg[:, i], Ls[:, :, i * P:(i + 1) * P],
                                                 ident[:, None, :].to_broadcast([P, 2, P]), ALU.mult))
                    dve.tensor_reduce(li[:, par], dg[:, :, :, :], AX_X, ALU.add).then_inc(own_li, 1)
                    dve.wait_ge(own_li, s + 1)
                    for i in range(TB):
                        for r in range(2):
                            own_logit = li[:, par, i, r:r + 1]
                            c.step(dve.tensor_scalar(junk[:, :], Ls[:, r, :], own_logit, 0.0, ALU.is_gt, ALU.add,
                                                     accum_out=later[:, i, r:r + 1]))
                            c.step(dve.scalar_tensor_tensor(junk[:, :], Ls[:, r, :], own_logit, before[:, i, :],
                                                            ALU.is_equal, ALU.mult,
                                                            accum_out=ties[:, i, r:r + 1]))
                    c.step(dve.tensor_tensor(rank[:, :, :], later[:, :, :], ties[:, :, :], ALU.add))
                    c.step(dve.tensor_scalar(mask[:, par, :], rank[:, :, 0], float(NQ), None, ALU.is_lt))
                    dve.tensor_tensor(sel[:, par], ranks[:, None, :].to_broadcast([P, TB, NK]),
                                      rank[:, :, 1:2].to_broadcast([P, TB, NK]), ALU.is_equal).then_inc(routed, 1)

                def weigh(c, b, g, par):
                    s = b * G + g
                    dve.wait_ge(sel_full, s + 1)
                    dve.tensor_copy(ksT[:, par, :], pM[:, 0:NK]).then_inc(ks_kept, 1)
                    dve.wait_ge(exq_done, s + 1)
                    dve.wait_ge(exk_done, s + 1)
                    c.step(dve.tensor_scalar(exk[:, par:par + 1], exk[:, par:par + 1], 1.0, None, ALU.add))
                    dve.reciprocal(kvs[:, par:par + 1], exk[:, par:par + 1]).then_inc(kvs_done, 1)

                def null_key(b, g, par):
                    s = b * G + g
                    dve.wait_ge(k_kept, s + 1)
                    dve.wait_ge(v_kept, s + 1)
                    dve.tensor_copy(V[NK:KK, par, :], nv[NK:KK, g, :])
                    dve.tensor_copy(kT[:, par, :, NK:KK], nk[:, g, :, None]).then_inc(null_in, 1)

                def first():
                    c = Chain(dve, own)
                    dve.wait_ge(const, 3)
                    dve.wait_ge(w_in, 16 * 7)
                    route(c, 0, 0, 0)
                    weigh(c, 0, 0, 0)
                    null_key(0, 0, 0)
                    assert c.n == FIRST_STEPS, c.n

                def step(b, g, has_next):
                    s = b * G + g
                    par = g % 2
                    nb, ng = following(b, g)
                    if g == 0:
                        step.chain = Chain(dve, own, FIRST_STEPS + BATCH_STEPS * b)
                    c = step.chain
                    for i in range(TB):
                        dve.wait_ge(s_full, TB * s + i + 1)
                        v = pS[:, :, 0:CH * KK].rearrange("p e (c k) -> p e c k", c=CH)
                        c.step(dve.tensor_reduce(m8[:, i], v, AX_X, ALU.max))
                        dve.tensor_tensor(Pr[:, i], v, m8[:, i, :, :, None].to_broadcast([P, 2, CH, KK]),
                                          ALU.subtract).then_inc(s_kept, 1)
                    if has_next:
                        route(c, nb, ng, 1 - par)
                    for i in range(TB):
                        dve.wait_ge(e_done, TB * s + i + 1)
                        c.step(dve.tensor_reduce(m8[:, i], Pr[:, i], AX_X, ALU.add))
                        dve.reciprocal(r8[:, i], m8[:, i]).then_inc(r_done, 1)
                    if has_next:
                        weigh(c, nb, ng, 1 - par)
                    c.step(dve.tensor_scalar(exq[:, par, :], exq[:, par, :], 1.0, None, ALU.add))
                    c.step(dve.reciprocal(exq[:, par, :], exq[:, par, :]))
                    c.step(dve.tensor_tensor(qs[:, par, :], exq[:, par, :], mask[:, par, :], ALU.mult))
                    if g == 0:
                        c.step(dve.tensor_copy(cnt[:, :], mask[:, par, :]))
                    else:
                        c.step(dve.tensor_tensor(cnt[:, :], cnt[:, :], mask[:, par, :], ALU.add))
                    for i in range(TB):
                        dve.wait_ge(t_odd, TB * s + i + 1)
                        dve.tensor_copy(PT[:, 1, :, i * P:(i + 1) * P],
                                        pA[0:KK, :].rearrange("p (c q) -> p c q", c=CH)).then_inc(odd_kept, 1)
                    if has_next:
                        null_key(nb, ng, 1 - par)
                    dve.wait_ge(y_full, s + 1)
                    dve.wait_ge(y_kept, TB * s + 1)
                    for i in range(TB):
                        y = pV[:, i * P:(i + 1) * P]
                        if g == 0:
                            dve.tensor_scalar(summed[:, i, :], y, qs[:, par, i:i + 1], None,
                                              ALU.mult).then_inc(y_kept, 1)
                        else:
                            dve.scalar_tensor_tensor(summed[:, i, :], y, qs[:, par, i:i + 1], summed[:, i, :],
                                                     ALU.mult, ALU.add).then_inc(y_kept, 1)
                    if g == G - 1:
                        c.step(dve.tensor_scalar(inv[:, :], cnt[:, :], 1e-5, None, ALU.max))
                        c.step(dve.reciprocal(inv[:, :], inv[:, :]))
                        c.step(dve.tensor_scalar(inv[:, :], inv[:, :], gate, None, ALU.mult))
                        c.step(dve.tensor_scalar(none[:, :], cnt[:, :], 0.0, None, ALU.is_equal))
                        dve.wait_ge(y_kept, TB * (s + 1) + 1)
                        for i in range(TB):
                            xt = x[:, TB * b + i, :]
                            c.step(dve.scalar_tensor_tensor(xt, summed[:, i, :], inv[:, i:i + 1], xt,
                                                            ALU.mult, ALU.add))
                            c.step(dve.scalar_tensor_tensor(xt, null, none[:, i:i + 1], xt, ALU.mult, ALU.add))
                        if has_next:
                            assert c.n == BATCH_STEPS, c.n

                steps(dve, step, first)


def routed_layouts(n, a):
    import numpy as np
    wkv = n["L0_ffn_w_kv"].reshape(G, 2, HR * E, D)
    router = np.stack([n["L0_ffn_w_qr"], n["L0_ffn_w_kvr"]], 1)
    a["r_router"] = np.broadcast_to(router.transpose(2, 0, 1)[:, :, :, None], (D, G, 2, P))
    a["r_wq"] = n["L0_ffn_w_q"].transpose(2, 0, 1)
    a["r_wk"] = wkv[:, 0].transpose(2, 0, 1)
    a["r_wv"] = wkv[:, 1].transpose(2, 0, 1)
    a["r_wo"] = n["L0_ffn_w_out"].reshape(G, D, CH, P).transpose(3, 0, 2, 1)
    nkv = n["L0_ffn_null_kv"].reshape(2, G, HR * E)
    a["r_null_k"] = nkv[0].reshape(G, CH, P).transpose(2, 0, 1)
    a["r_null_v"] = nkv[1][None]


DH = D // H
GH = 4
NG = H // GH
QD = P // GH
VD = DH + 1


def narrow_attention(nc, A, x, xnT, bias, gate, ident):
    MAXIMA = 2 * TB * NC
    VT = 3
    NV = (KT + VT - 1) // VT
    PREP = NG + NG * NC + NV
    FIRST = PREP + NP * MAXIMA + 1
    CARRY = TB + 2
    BATCH = PREP + NP * MAXIMA + 1 + TB * NP + 2
    PER_SLOT = 3
    QSLOTS = (PREP + PER_SLOT - 1) // PER_SLOT
    with ExitStack() as ctx:
        m = Pool_(nc, ctx, "na")
        wq = m.sb("wq", [D, NG, P])
        bq = m.sb("bq", [P, NG])
        wk = m.sb("wk", [C1, NG, P])
        wv = m.sb("wv", [C1, H * VD])
        wo = m.sb("wo", [D, D])
        lows = m.sb("lows", [P, 2])
        fold = m.sb("fold", [P, 2 * VD])
        ctxT = m.sb("ctxT", [C1, T])
        k16 = m.sb("k16", [P, 2, NG, T], F16)
        kh = m.sb("kh", [P, 2, CHUNK[0][1]], F16)
        q16 = m.sb("q16", [P, 2, H * S], F16)
        qa = m.sb("qa", [P, S])
        q_h = m.sb("q_h", [P, S], F16)
        vall = m.sb("vall", [P, 2, KT, H * VD])
        vst = m.sb("vst", [P, 2, KT, 2, QD])
        prob = m.sb("prob", [P, PRING + 1, PAIR])
        acc = m.sb("acc", [P, 2, S])
        mx = m.sb("mx", [P, UNITS * NC])
        mu = m.sb("mu", [P, UNITS])
        shift = m.sb("shift", [UNITS, P], F16)
        att = m.sb("att", [P, TB, H, VD])
        rec = m.sb("rec", [P, TB, H])
        attn = m.sb("attn", [P, TB, D])
        attnT = m.sb("attnT", [D, TB * P])
        scores = m.ps("scores", [P, RING + 1, PAIR])
        helper = m.ps("helper", [P, 2, 512])
        pacc = m.ps("pacc", [P, 2, 512])

        w_in = m.sem("w_in")
        w_ready = m.sem("w_ready")
        ctxT_in = m.sem("ctxT_in")
        v_clear = m.sem("v_clear")
        v_staged = m.sem("v_staged")
        kh_ready = m.sem("kh_ready")
        q_clear = m.sem("q_clear")
        qa_ready = m.sem("qa_ready")
        q_parts = m.sem("q_parts")
        filled = m.sem("helper_filled")
        freed = m.sem("helper_freed")
        prepared = m.sem("prepared")
        mu_ready = m.sem("mu_ready")
        shift_in = m.sem("shift_in")
        scores_ready = m.sem("scores_ready")
        exp_done = m.sem("exp_done")
        pv_done = m.sem("pv_done")
        acc_ready = m.sem("acc_ready")
        out_step = m.sem("out_step")
        attn_ready = m.sem("attn_ready")
        attnT_ready = m.sem("attnT_ready")

        def prep_items(kind, t):
            if kind != "first":
                return range(0)
            return range(PER_SLOT * t, min(PER_SLOT * (t + 1), PREP))

        def maxima(kind, t):
            if kind == "first":
                return range(4 * (t - QSLOTS), 4 * (t - QSLOTS + 1)) if QSLOTS <= t < QSLOTS + 4 else range(0)
            if kind == "middle":
                return range(MAXIMA * t // KT, MAXIMA * (t + 1) // KT)
            return range(2 * t, 2 * t + 2) if kind == "last" and t < 8 else range(0)

        assert QSLOTS + 4 <= KT

        def start_fill(b, p, kind, par):
            if isinstance(p, int) and p == 0:
                carried = 0 if isinstance(b, int) and b == 0 else CARRY
                return FIRST + BATCH * b - carried, (FIRST + BATCH * par) % 2
            if kind == "idle":
                return FIRST + BATCH * b + TB * (p - 1), (FIRST + BATCH * par) % 2
            return (FIRST + BATCH * b + PREP + MAXIMA + (MAXIMA + TB) * (p - 1),
                    (FIRST + BATCH * par + PREP + MAXIMA) % 2)

        def is_p(p, v):
            return isinstance(p, int) and p == v

        with nc.Block() as block:
            @block.sync
            def _(sp):
                for sb_, name in ((wq, "n_wq"), (bq, "n_bq"), (wk, "n_wk"), (wv, "n_wv"), (wo, "n_wo"),
                                  (lows, "n_lows"), (fold, "n_fold")):
                    sp.dma_start(sb_[:], A[name]).then_inc(w_in, 16)

                def load_T(b):
                    if b >= 1:
                        sp.wait_ge(filled, PREP if b == 1 else FIRST + BATCH * (b - 2) + PREP)
                    sp.dma_start(ctxT[:, :], A["ctxT"][b]).then_inc(ctxT_in, 16)

                def put_shift(b):
                    n = FIRST if b == 0 else FIRST + BATCH * b - CARRY
                    sp.wait_ge(freed, n)
                    for i in range(GH):
                        row = QD * i + 3 * DH
                        for g in range(NG):
                            h, u = GH * g + i, 2 * (NG * i + g)
                            sp.dma_start(q16[row:row + 1, b % 2, h * S:(h + 1) * S].rearrange("a (q n) -> a q n", q=TB),
                                         shift[u:u + TB, :]).then_inc(shift_in, 16)

                load_T(0)
                load_T(1)
                put_shift(0)
                for b in range(1, NB):
                    if b + 1 < NB:
                        load_T(b + 1)
                    put_shift(b)

            @block.gpsimd
            def _(pool):
                pool.memset(vall[:, :, KT - 1, :], 0.0).then_inc(v_clear, 1)
                pool.memset(vst[:, :, :, :, :], 0.0).then_inc(v_clear, 1)
                pool.wait_ge(v_clear, 2)

                def batch(b, buf, prepares):
                    with pool.Fori(0, NP // 2) as i:
                        for par in range(2):
                            p = 2 * i + par
                            pool.wait_ge(prepared, b + 1)
                            pool.wait_ge(pv_done, KT * (b * NP + p) + 1)
                            for j in range(2):
                                pool.tensor_copy(vst[:, par, :, j, 0:VD],
                                                 vall[:, buf, :, bass.ds((2 * p + j) * VD, VD)]).then_inc(v_staged, 1)

                over_batches(pool, batch)

            @block.tensor
            def _(pe):
                def fill(f):
                    if not (isinstance(f, int) and f < 2):
                        pe.wait_ge(freed, f - 1)

                def prepare(nb, j, f, bank):
                    fill(f)
                    if j < NG:
                        ins = pe.matmul(helper[:, bank, 0:S], wq[:, j, :], xnT[:, bass.ds(nb * S, S)],
                                        start=True, stop=True)
                    elif j < NG + NG * NC:
                        g, c = divmod(j - NG, NC)
                        c0, w = CHUNK[c]
                        if j == NG:
                            pe.wait_ge(ctxT_in, 16 * nb + 16)
                        ins = pe.matmul(helper[:, bank, 0:w], wk[:, g, :], ctxT[:, c0:c0 + w], start=True, stop=True)
                    else:
                        t0 = VT * (j - NG - NG * NC)
                        for i, t in enumerate(range(t0, min(t0 + VT, KT))):
                            ins = pe.matmul(helper[0:keys(t), bank, i * H * VD:(i + 1) * H * VD],
                                            ctxT[:, t * P:t * P + keys(t)], wv[:, :], start=True, stop=True)
                    ins.then_inc(filled, 1)

                def maximum(buf, p, g, k, f, bank):
                    c0, w = CHUNK[k % NC]
                    fill(f)
                    pe.matmul(helper[:, bank, 0:w], q16[:, buf, bass.ds((4 * p + k // NC) * P, P)],
                              k16[:, buf, g, c0:c0 + w], start=True, stop=True).then_inc(filled, 1)

                def turn_mu(nb, f, bank):
                    pe.wait_ge(mu_ready, nb + 1)
                    fill(f)
                    pe.transpose(helper[0:UNITS, bank, 0:P], mu[:, :], ident[:, :]).then_inc(filled, 1)

                def score(b, p, g, buf, t):
                    n = (b * NP + p) * KT + t
                    if t == 0 and is_p(p, 0):
                        pe.wait_ge(shift_in, 16 * H * (b + 1))
                    pe.wait_ge(exp_done, KT + n - since_last(t, RING) + 1)
                    pe.matmul(scores[0:keys(t), score_slot(t), :], k16[:, buf, g, t * P:t * P + keys(t)],
                              q16[:, buf, bass.ds(p * PAIR, PAIR)], start=True, stop=True).then_inc(scores_ready, 1)

                def attend(p, par, t):
                    for j in range(2):
                        r = QD * (2 * (t % 2) + j)
                        ins = pe.matmul(pacc[r:r + QD, par, 0:S], vst[0:keys(t), par, t, j, :],
                                        prob[0:keys(t), prob_slot(t), j * S:(j + 1) * S],
                                        start=(t < 2), stop=(t >= KT - 2))
                    ins.then_inc(pv_done, 1)

                def project(b, p, par, f, bank):
                    pe.wait_ge(acc_ready, b * NP + p + 3)
                    for i in range(TB):
                        fill(f + i)
                        pe.matmul(helper[:, (bank + i) % 2, 0:2 * VD], acc[:, par, i * P:(i + 1) * P], fold[:, :],
                                  start=True, stop=True).then_inc(filled, 1)

                def turn_out(b, f, bank):
                    pe.wait_ge(attn_ready, b + 1)
                    fill(f)
                    for i in range(TB):
                        ins = pe.transpose(helper[:, bank, i * P:(i + 1) * P], attn[:, i, :], ident[:, :])
                    ins.then_inc(filled, 1)

                def output(b, f, bank):
                    fill(f)
                    pe.wait_ge(attnT_ready, b + 1)
                    for i in range(TB):
                        ins = pe.matmul(helper[:, bank, i * P:(i + 1) * P], attnT[:, i * P:(i + 1) * P],
                                        wo[:, :], start=True, stop=True)
                    ins.then_inc(filled, 1)

                def batch(b, buf, prepares):
                    def pair(p, par, kind, g):
                        f, bank = start_fill(b, p, kind, buf)
                        n = (b * NP + p) * KT
                        k = 0
                        before = pair_before(b, p)
                        gn = g + 1 if par == 1 and not is_p(p, NP - 1) else g
                        for t in range(KT):
                            if t + 2 < KT:
                                score(b, p, g, buf, t + 2)
                            elif kind == "last":
                                score(b + 1, 0, 0, 1 - buf, t + 2 - KT)
                            elif not is_p(p, NP - 1):
                                score(b, p + 1, gn, buf, t + 2 - KT)
                            for i in prep_items(kind, t):
                                prepare(b + 1, i, f + k, (bank + k) % 2)
                                k += 1
                            for i in maxima(kind, t):
                                maximum(1 - buf, p, g, i, f + k, (bank + k) % 2)
                                k += 1
                            if t == 2 and before:
                                project(*before, 1 - par, f + k, (bank + k) % 2)
                                k += TB
                            if t in (5, 7) and before and is_p(p, 0):
                                (turn_out if t == 5 else output)(b - 1, f + k, (bank + k) % 2)
                                k += 1
                            if kind == "last" and t == 9:
                                turn_mu(b + 1, f + k, (bank + k) % 2)
                                k += 1
                            if t == 1:
                                pe.wait_ge(acc_ready, b * NP + p + 1)
                                pe.wait_ge(v_staged, 2 * (b * NP + p + 1))
                            if t % 2 == 1 or t == KT - 1:
                                pe.wait_ge(exp_done, KT + n + t + 1)
                                if t % 2 == 1:
                                    attend(p, par, t - 1)
                                attend(p, par, t)
                        if kind == "idle" and is_p(p, NP - 1):
                            project(b, p, par, f + k, (bank + k) % 2)
                            turn_out(b, f + k + TB, (bank + k) % 2)
                            output(b, f + k + TB + 1, (bank + k + 1) % 2)
                    over_pairs(pe, pair, prepares)

                pe.wait_ge(w_ready, 4)
                for j in range(PREP):
                    prepare(0, j, j, j % 2)
                pe.wait_ge(prepared, 1)
                for p in range(NP):
                    for k in range(MAXIMA):
                        maximum(0, p, p // 2, k, PREP + MAXIMA * p + k, (PREP + k) % 2)
                turn_mu(0, FIRST - 1, (FIRST - 1) % 2)
                for t in range(2):
                    score(0, 0, 0, 0, t)
                over_batches(pe, batch)

            @block.scalar
            def _(act):
                act.sem_inc(exp_done, KT)
                act.sem_inc(acc_ready, 2)

                def keep_k_hi(nb, j, f, bank):
                    w = CHUNK[(j - NG) % NC][1]
                    act.wait_ge(filled, f + 1)
                    act.activation(kh[:, bank, 0:w], helper[:, bank, 0:w], ACT.Copy).then_inc(kh_ready, 1)

                def keep_q(nb, j, f, bank):
                    act.wait_ge(filled, f + 1)
                    act.wait_ge(q_parts, GH * (NG * nb + j) + 1)
                    act.activation(qa[:, :], helper[:, bank, 0:S], ACT.Identity, bias=bq[:, j:j + 1]).then_inc(qa_ready, 1)
                    act.wait_ge(qa_ready, 2 * (NG * nb + j) + 1)
                    act.activation(q_h[:, :], qa[:, :], ACT.Copy).then_inc(qa_ready, 1)

                def keep_acc(b, p, par):
                    act.wait_ge(pv_done, KT * (b * NP + p + 2))
                    act.activation(acc[:, par, :], pacc[:, par, 0:S], ACT.Copy).then_inc(acc_ready, 1)

                def batch(b, buf, prepares):
                    def pair(p, par, kind, _):
                        f, bank = start_fill(b, p, kind, buf)
                        before = pair_before(b, p)
                        n = (b * NP + p) * KT
                        k = 0
                        for t in range(KT):
                            act.wait_ge(scores_ready, n + t + 1)
                            act.wait_ge(pv_done, KT + n + t - since_last(t, PRING) + 1)
                            act.activation(prob[0:keys(t), prob_slot(t), :],
                                           scores[0:keys(t), score_slot(t), :], ACT.Exp,
                                           scale=UNSPLIT).then_inc(exp_done, 1)
                            if t == 0 and before:
                                keep_acc(*before, 1 - par)
                            for i in prep_items(kind, t):
                                if i < NG:
                                    keep_q(b + 1, i, f + k, (bank + k) % 2)
                                elif i < NG + NG * NC:
                                    keep_k_hi(b + 1, i, f + k, (bank + k) % 2)
                                k += 1
                            if t == 2 and before:
                                k += TB
                            if t in (5, 7) and before and is_p(p, 0):
                                k += 1
                        if kind == "idle" and is_p(p, NP - 1):
                            keep_acc(b, p, par)
                    over_pairs(act, pair, prepares)

                act.wait_ge(w_ready, 4)
                for j in range(NG + NG * NC):
                    (keep_q if j < NG else keep_k_hi)(0, j, j, j % 2)
                over_batches(act, batch)

            @block.vector
            def _(dve):
                dve.sem_inc(pv_done, KT)
                dve.sem_inc(q_parts, 1)
                dve.memset(q16[:, :, :], 0.0).then_inc(q_clear, 1)
                dve.tensor_tensor(x[:, :, :], x[:, :, :], bias[:, None, :].to_broadcast([P, NT, D]),
                                  ALU.add).then_inc(q_clear, 1)
                dve.wait_ge(w_in, 16 * 7)
                dve.tensor_scalar(wk[:, :, :], wk[:, :, :], SPLIT, None, ALU.mult).then_inc(w_ready, 1)
                dve.tensor_scalar(wq[:, :, :], wq[:, :, :], SPLIT * DH ** -0.5, None, ALU.mult).then_inc(w_ready, 1)
                dve.tensor_scalar(bq[:, :], bq[:, :], SPLIT * DH ** -0.5, None, ALU.mult).then_inc(w_ready, 1)
                dve.tensor_scalar(wo[:, :], wo[:, :], gate, None, ALU.mult).then_inc(w_ready, 1)
                dve.wait_ge(w_ready, 4)
                dve.wait_ge(q_clear, 2)
                dve.wait_ge(v_clear, 2)

                def prepare(nb, buf, j, f, bank):
                    dve.wait_ge(filled, f + 1)
                    if j < NG:
                        dve.wait_ge(qa_ready, 2 * (NG * nb + j) + 2)
                        for i in range(GH):
                            r = slice(QD * i, QD * (i + 1))
                            h = GH * j + i
                            dve.scalar_tensor_tensor(q16[r, buf, h * S:(h + 1) * S], q_h[r, :], lows[r, 1:2],
                                                     qa[r, :], ALU.mult, ALU.add).then_inc(q_parts, 1)
                        dve.sem_inc(freed, 1)
                    elif j < NG + NG * NC:
                        g, c = divmod(j - NG, NC)
                        c0, w = CHUNK[c]
                        dve.wait_ge(kh_ready, NG * NC * nb + j - NG + 1)
                        dve.scalar_tensor_tensor(k16[:, buf, g, c0:c0 + w], kh[:, bank, 0:w], lows[:, 0:1],
                                                 helper[:, bank, 0:w], ALU.mult, ALU.add).then_inc(freed, 1)
                    else:
                        t0 = VT * (j - NG - NG * NC)
                        n = min(VT, KT - t0)
                        k = keys(t0 + n - 1)
                        assert n == 1 or k == P
                        dve.tensor_copy(vall[0:k, buf, t0:t0 + n, :].rearrange("p t v -> p (t v)"),
                                        helper[0:k, bank, 0:n * H * VD]).then_inc(freed, 1)
                        if j == PREP - 1:
                            dve.wait_ge(freed, f + 1)
                            dve.wait_ge(q_parts, GH * NG * (nb + 1) + 1)
                            dve.sem_inc(prepared, 1)

                def maximum(p, k, f, bank):
                    w = CHUNK[k % NC][1]
                    dve.wait_ge(filled, f + 1)
                    dve.tensor_reduce(mx[:, bass.ds(MAXIMA * p + k, 1)], helper[:, bank, 0:w], AX_X,
                                      ALU.max).then_inc(freed, 1)

                def gather_mu(nb, f):
                    dve.wait_ge(freed, f)
                    v = mx[:, :].rearrange("p (g i q c) -> p i g q c", g=NG, i=GH, q=TB)
                    for i in range(GH):
                        ins = dve.tensor_reduce(mu[:, 2 * NG * i:2 * NG * (i + 1)].rearrange("p (g q) -> p g q", g=NG),
                                                v[:, i], AX_X, ALU.max)
                    ins.then_inc(mu_ready, 1)

                def keep_shift(nb, f, bank):
                    dve.wait_ge(filled, f + 1)
                    if not (isinstance(nb, int) and nb == 0):
                        dve.wait_ge(shift_in, 16 * H * nb)
                    dve.tensor_scalar(shift[:, :], helper[0:UNITS, bank, 0:P], -1.0 / SPLIT, None,
                                      ALU.mult).then_inc(freed, 1)

                def keep_out(b, p, f, bank):
                    for i in range(TB):
                        dve.wait_ge(filled, f + i + 1)
                        dve.tensor_copy(att[:, i].rearrange("p h v -> p (h v)")[:, bass.ds(2 * VD * p, 2 * VD)],
                                        helper[:, (bank + i) % 2, 0:2 * VD]).then_inc(freed, 1)

                def normalise(b, f):
                    dve.wait_ge(freed, f)
                    dve.reciprocal(rec[:, :, :], att[:, :, :, DH]).then_inc(out_step, 1)
                    dve.wait_ge(out_step, 2 * b + 1)
                    for i in range(TB):
                        ins = dve.tensor_tensor(attn[:, i, :].rearrange("p (h v) -> p h v", h=H), att[:, i, :, 0:DH],
                                                rec[:, i, :, None].to_broadcast([P, H, DH]), ALU.mult)
                    ins.then_inc(attn_ready, 1)

                def keep_attnT(b, f, bank):
                    dve.wait_ge(filled, f + 1)
                    dve.tensor_copy(attnT[:, :], helper[:, bank, 0:TB * P]).then_inc(freed, 1)
                    dve.wait_ge(freed, f + 1)
                    dve.sem_inc(attnT_ready, 1)

                def add_out(b, f, bank):
                    dve.wait_ge(filled, f + 1)
                    for i in range(TB):
                        xt = x[:, TB * b + i, :]
                        ins = dve.tensor_tensor(xt, xt, helper[:, bank, i * P:(i + 1) * P], ALU.add)
                        ins.then_inc(out_step if i == 0 else freed, 1)

                def batch(b, buf, prepares):
                    def pair(p, par, kind, _):
                        f, bank = start_fill(b, p, kind, buf)
                        before = pair_before(b, p)
                        k = 0
                        for t in range(KT):
                            for i in prep_items(kind, t):
                                prepare(b + 1, 1 - buf, i, f + k, (bank + k) % 2)
                                k += 1
                            for i in maxima(kind, t):
                                maximum(p, i, f + k, (bank + k) % 2)
                                k += 1
                            if t == 2 and before:
                                keep_out(*before, f + k, (bank + k) % 2)
                                k += TB
                                if is_p(p, 0):
                                    normalise(b - 1, f + k)
                            if t in (5, 7) and before and is_p(p, 0):
                                (keep_attnT if t == 5 else add_out)(b - 1, f + k, (bank + k) % 2)
                                k += 1
                            if kind == "last" and t == 8:
                                gather_mu(b + 1, f + k)
                            if kind == "last" and t == 9:
                                keep_shift(b + 1, f + k, (bank + k) % 2)
                                k += 1
                        if kind == "idle" and is_p(p, NP - 1):
                            keep_out(b, p, f + k, (bank + k) % 2)
                            k += TB
                            normalise(b, f + k)
                            keep_attnT(b, f + k, (bank + k) % 2)
                            add_out(b, f + k + 1, (bank + k + 1) % 2)
                    over_pairs(dve, pair, prepares)

                for j in range(PREP):
                    prepare(0, 0, j, j, j % 2)
                for p in range(NP):
                    for k in range(MAXIMA):
                        maximum(p, k, PREP + MAXIMA * p + k, (PREP + k) % 2)
                gather_mu(0, FIRST - 1)
                keep_shift(0, FIRST - 1, (FIRST - 1) % 2)
                over_batches(dve, batch)


def narrow_layouts(n, a):
    import numpy as np
    f = np.float32
    wq = n["L1_xattn_Wq"].reshape(NG, GH, DH, D)
    bq = n["L1_xattn_bq"].reshape(NG, GH, DH)
    wkv = np.concatenate([n["L1_xattn_Wkv"], n["L1_xattn_bkv"][:, None]], 1).reshape(H, 2, DH, C1)
    wk = wkv[:, 0].reshape(NG, GH, DH, C1)
    q = np.zeros((D, NG, GH, QD), f)
    qb = np.zeros((GH, QD, NG), f)
    k = np.zeros((C1, NG, GH, QD), f)
    lows = np.zeros((GH, QD, 2), f)
    for r in range(3):
        part = slice(r * DH, (r + 1) * DH)
        q[..., part] = wq.transpose(3, 0, 1, 2)
        qb[:, part] = bq.transpose(1, 2, 0)
        k[..., part] = wk.transpose(3, 0, 1, 2)
    k[C, :, :, 3 * DH] = 1.0
    lows[:, DH:2 * DH, 0] = -1.0
    lows[:, 2 * DH:3 * DH, 1] = -1.0
    v = np.zeros((C1, H, VD), f)
    v[..., 0:DH] = wkv[:, 1].transpose(2, 0, 1)
    v[C, :, DH] = 1.0
    fold = np.zeros((2, 2, QD, 2, VD), f)
    for j in range(2):
        fold[:, j, 0:VD, j, :] = np.eye(VD, dtype=f)
    a["n_wq"] = q.reshape(D, NG, P)
    a["n_bq"] = qb.reshape(P, NG)
    a["n_wk"] = k.reshape(C1, NG, P)
    a["n_wv"] = v.reshape(C1, H * VD)
    a["n_wo"] = n["L1_xattn_Wo"].T
    a["n_lows"] = lows.reshape(P, 2)
    a["n_fold"] = fold.reshape(P, 2 * VD)


NE, HRT, HSH, TAU = 12, 384, 256, 1.5
RC, SC = HRT // P, HSH // P
BLK = 512
NBLK = NB * S // BLK
BT = BLK // P


def experts(nc, A, x, xnT, bias, gate, ident):
    CHUNKS = SC + NE * RC
    with ExitStack() as ctx:
        m = Pool_(nc, ctx, "ex")
        w1 = m.sb("w1", [D, NE, 2 * HRT])
        w2 = m.sb("w2", [P, NE, RC, D])
        ws1 = m.sb("ws1", [D, 2 * HSH])
        ws2 = m.sb("ws2", [P, SC, D])
        b1 = m.sb("b1", [P, NE, 2 * RC])
        bs1 = m.sb("bs1", [P, 2 * SC])
        b2 = m.sb("b2", [NE, D])
        wr = m.sb("wr", [D, NE])
        br = m.sb("br", [P, NE])
        tri = m.sb("tri", [P, NE, NE])
        L = m.sb("logits", [P, NT, NE])
        gt = m.sb("larger", [P, NT, NE, NE])
        eq = m.sb("ties", [P, NT, NE, NE])
        rank = m.sb("rank", [P, NT, NE])
        top = m.sb("top", [P, NT])
        ex = m.sb("ex", [P, NT, NE])
        den = m.sb("den", [P, NT])
        wgt = m.sb("weight", [P, NT, NE])
        wgt_g = m.sb("gated_weight", [P, NT, NE])
        wT = m.sb("wT", [NE, NT * P])
        wTb = m.sb("wT_block", [NE, BLK])
        gl = m.sb("gelu", [P, 2, BLK])
        hidden = m.sb("hidden", [P, 2, RC, BLK])
        pa = m.ps("a", [P, 2, BLK])
        pg = m.ps("g", [P, 2, BLK])
        py = m.ps("y", [P, 2, BT, D])
        pr = m.ps("route", [P, 2, 512])

        small_in = m.sem("small_in")
        w_in = [m.sem(f"w_in{e}") for e in range(NE + 1)]
        tri_ready = m.sem("tri_ready")
        own = m.sem("own")
        logits_full = m.sem("logits_full")
        shifted = m.sem("shifted")
        ex_done = m.sem("ex_done")
        wgt_ready = m.sem("wgt_ready")
        wT_full = m.sem("wT_full")
        wT_kept = m.sem("wT_kept")
        wTb_ready = m.sem("wTb_ready")
        up_full = m.sem("up_full")
        gelu_done = m.sem("gelu_done")
        up_kept = m.sem("up_kept")
        y_full = m.sem("y_full")
        y_kept = m.sem("y_kept")

        def chunks(e):
            return SC if e == 0 else RC

        def chunk_index(e):
            return 0 if e == 0 else SC + RC * (e - 1)

        with nc.Block() as block:
            @block.sync
            def _(sp):
                for sb_, name in ((wr, "e_wr"), (br, "e_br"), (b2, "e_b2"), (b1, "e_b1"), (bs1, "e_bs1")):
                    sp.dma_start(sb_[:], A[name]).then_inc(small_in, 16)
                sp.dma_start(ws1[:, :], A["e_ws1"]).then_inc(w_in[0], 16)
                sp.dma_start(ws2[:, :, :], A["e_ws2"]).then_inc(w_in[0], 16)
                for e in range(NE):
                    sp.dma_start(w1[:, e, :], A["e_w1"][:, e, :]).then_inc(w_in[e + 1], 16)
                    sp.dma_start(w2[:, e, :, :], A["e_w2"][:, e, :, :]).then_inc(w_in[e + 1], 16)

            @block.gpsimd
            def _(pool):
                pool.memset(tri[:, :, :], 1.0).then_inc(tri_ready, 1)
                pool.wait_ge(tri_ready, 1)
                pool.affine_select(out=tri[:, :, :], in_=tri[:, :, :], compare_op=ALU.is_gt, fill=0.0, base=0,
                                   pattern=[[1, NE], [-1, NE]], channel_multiplier=0).then_inc(tri_ready, 1)
                pool.wait_ge(wT_kept, NT // 4)
                with pool.Fori(0, NBLK) as tb:
                    pool.wait_ge(wT_kept, NT // 4)
                    pool.wait_ge(y_full, tb * (NE + 1) + 1)
                    pool.tensor_copy(wTb[:, :], wT[:, bass.ds(tb * BLK, BLK)]).then_inc(wTb_ready, 1)

            @block.tensor
            def _(pe):
                def up(tb, e):
                    for c in range(chunks(e)):
                        k = chunk_index(e) + c
                        pe.wait_ge(up_kept, tb * CHUNKS + k + 1)
                        if c == 0 and isinstance(tb, int) and tb == 0:
                            pe.wait_ge(w_in[e], 32)
                        for bank, half in ((pa, 0), (pg, 1)):
                            if e == 0:
                                w = ws1[:, half * HSH + c * P:half * HSH + (c + 1) * P]
                            else:
                                w = w1[:, e - 1, half * HRT + c * P:half * HRT + (c + 1) * P]
                            ins = pe.matmul(bank[:, k % 2, :], w, xnT[:, bass.ds(tb * BLK, BLK)],
                                            start=True, stop=True)
                        ins.then_inc(up_full, 1)

                def down(tb, e):
                    n = tb * (NE + 1) + e
                    pe.wait_ge(up_kept, 2 + tb * CHUNKS + chunk_index(e) + chunks(e))
                    pe.wait_ge(y_kept, n + 2 if e == 0 else n + 1)
                    if e == 0:
                        pe.wait_ge(wTb_ready, tb + 1)
                    for t in range(BT):
                        if e == 0:
                            pe.matmul(py[:, 0, t, :], wTb[:, t * P:(t + 1) * P], b2[:, :], start=True, stop=False)
                        for c in range(chunks(e)):
                            w = ws2[:, c, :] if e == 0 else w2[:, e - 1, c, :]
                            ins = pe.matmul(py[:, e % 2, t, :], hidden[:, e % 2, c, t * P:(t + 1) * P], w,
                                            start=(c == 0 and e > 0), stop=(c == chunks(e) - 1))
                    ins.then_inc(y_full, 1)

                def token_block(tb):
                    for e in range(NE + 2):
                        if e <= NE:
                            up(tb, e)
                        if e >= 1:
                            down(tb, e - 1)

                pe.wait_ge(small_in, 16 * 5)
                for t in range(NT):
                    ins = pe.matmul(pr[:, 0, t * NE:(t + 1) * NE], xnT[:, t * P:(t + 1) * P], wr[:, :],
                                    start=True, stop=True)
                ins.then_inc(logits_full, 1)
                pe.wait_ge(wgt_ready, 1)
                for t in range(NT):
                    if t % 4 == 0 and t >= 8:
                        pe.wait_ge(wT_kept, t // 4 - 1)
                    ins = pe.transpose(pr[0:NE, t // 4 % 2, t % 4 * P:(t % 4 + 1) * P], wgt[:, t, :], ident[:, :])
                    if t % 4 == 3:
                        ins.then_inc(wT_full, 1)
                token_block(0)
                with pe.Fori(1, NBLK) as tb:
                    token_block(tb)

            @block.scalar
            def _(act):
                act.wait_ge(shifted, 1)
                act.activation(ex[:, :, :], ex[:, :, :], ACT.Exp).then_inc(ex_done, 1)
                for q in range(NT // 4):
                    act.wait_ge(wT_full, q + 1)
                    act.activation(wT[:, 4 * q * P:4 * (q + 1) * P], pr[0:NE, q % 2, :], ACT.Copy).then_inc(wT_kept, 1)
                with act.Fori(0, NBLK) as tb:
                    for e in range(NE + 1):
                        for c in range(chunks(e)):
                            k = chunk_index(e) + c
                            act.wait_ge(up_full, tb * CHUNKS + k + 1)
                            act.wait_ge(up_kept, tb * CHUNKS + k + 1)
                            b = bs1[:, SC + c:SC + c + 1] if e == 0 else b1[:, e - 1, RC + c:RC + c + 1]
                            act.activation(gl[:, k % 2, :], pg[:, k % 2, :], ACT.Gelu, bias=b).then_inc(gelu_done, 1)

            @block.vector
            def _(dve):
                c = Chain(dve, own)
                dve.sem_inc(up_kept, 2)
                dve.sem_inc(y_kept, 2)
                dve.sem_inc(y_full, 2)
                dve.tensor_tensor(x[:, :, :], x[:, :, :], bias[:, None, :].to_broadcast([P, NT, D]), ALU.add)
                dve.wait_ge(small_in, 16 * 5)
                dve.wait_ge(tri_ready, 2)
                dve.wait_ge(logits_full, 1)
                c.step(dve.tensor_tensor(L[:, :, :], pr[:, 0, 0:NT * NE].rearrange("p (t e) -> p t e", t=NT),
                                         br[:, None, :].to_broadcast([P, NT, NE]), ALU.add))
                c.step(dve.tensor_scalar(L[:, :, :], L[:, :, :], 1.0 / TAU, None, ALU.mult))
                other = L[:, :, None, :].to_broadcast([P, NT, NE, NE])
                mine = L[:, :, :, None].to_broadcast([P, NT, NE, NE])
                c.step(dve.tensor_tensor(gt[:, :, :, :], other, mine, ALU.is_gt))
                c.step(dve.tensor_tensor(eq[:, :, :, :], other, mine, ALU.is_equal))
                for t in range(NT):
                    ins = dve.tensor_tensor(eq[:, t, :, :], eq[:, t, :, :], tri[:, :, :], ALU.mult)
                c.step(ins)
                c.step(dve.tensor_tensor(gt[:, :, :, :], gt[:, :, :, :], eq[:, :, :, :], ALU.add))
                c.step(dve.tensor_reduce(rank[:, :, :], gt[:, :, :, :], AX_X, ALU.add))
                c.step(dve.tensor_reduce(top[:, :], L[:, :, :], AX_X, ALU.max))
                dve.tensor_tensor(ex[:, :, :], L[:, :, :], top[:, :, None].to_broadcast([P, NT, NE]),
                                  ALU.subtract).then_inc(shifted, 1)
                c.step(dve.tensor_scalar(rank[:, :, :], rank[:, :, :], 2.0, None, ALU.is_lt))
                dve.wait_ge(ex_done, 1)
                c.step(dve.tensor_tensor(ex[:, :, :], ex[:, :, :], rank[:, :, :], ALU.mult))
                c.step(dve.tensor_reduce(den[:, :], ex[:, :, :], AX_X, ALU.add))
                c.step(dve.reciprocal(den[:, :], den[:, :]))
                dve.tensor_tensor(wgt[:, :, :], ex[:, :, :], den[:, :, None].to_broadcast([P, NT, NE]),
                                  ALU.mult).then_inc(wgt_ready, 1)
                dve.wait_ge(wgt_ready, 1)
                c.step(dve.tensor_scalar(wgt_g[:, :, :], wgt[:, :, :], gate, None, ALU.mult))

                def hide(tb, e):
                    n = tb * (NE + 1) + e
                    dve.wait_ge(y_full, n + 2 if e == 0 else n if e == 1 else n + 1)
                    for c in range(chunks(e)):
                        k = chunk_index(e) + c
                        dve.wait_ge(gelu_done, tb * CHUNKS + k + 1)
                        b = bs1[:, c:c + 1] if e == 0 else b1[:, e - 1, c:c + 1]
                        dve.scalar_tensor_tensor(hidden[:, e % 2, c, :], pa[:, k % 2, :], b, gl[:, k % 2, :],
                                                 ALU.add, ALU.mult).then_inc(up_kept, 1)

                def add(tb, e):
                    n = tb * (NE + 1) + e
                    dve.wait_ge(y_full, n + 3)
                    dve.wait_ge(y_kept, n + 2)
                    for t in range(BT):
                        xt = x[:, tb * BT + t, :]
                        w = gate if e == 0 else wgt_g[:, bass.ds(tb * BT + t, 1), e - 1]
                        ins = dve.scalar_tensor_tensor(xt, py[:, e % 2, t, :], w, xt, ALU.mult, ALU.add)
                    ins.then_inc(y_kept, 1)

                with dve.Fori(0, NBLK) as tb:
                    for e in range(NE + 2):
                        if e <= NE:
                            hide(tb, e)
                        if e >= 1:
                            add(tb, e - 1)


def expert_layouts(n, a):
    import numpy as np
    a["e_w1"] = n["L1_ffn_We1"].transpose(1, 0, 2)
    a["e_w2"] = n["L1_ffn_We2"].reshape(NE, RC, P, D).transpose(2, 0, 1, 3)
    a["e_ws1"] = n["L1_ffn_Ws1"]
    a["e_ws2"] = n["L1_ffn_Ws2"].reshape(SC, P, D).transpose(1, 0, 2)
    a["e_b1"] = n["L1_ffn_be1"].reshape(NE, 2 * RC, P).transpose(2, 0, 1)
    a["e_bs1"] = n["L1_ffn_bs1"].reshape(2 * SC, P).T
    a["e_b2"] = n["L1_ffn_be2"]
    a["e_wr"] = n["L1_ffn_Wr"]
    a["e_br"] = np.tile(n["L1_ffn_br"].reshape(1, NE), (P, 1))


def setup(nc, A, x, ident, gate, rowvec, ROWVECS):
    with ExitStack() as ctx:
        m = Pool_(nc, ctx, "su")
        raw = m.sb("raw_gate", [P, 4])
        x_in = m.sem("x_in")
        gate_in = m.sem("gate_in")
        zeroed = m.sem("zeroed")
        gate_ready = m.sem("gate_ready")
        with nc.Block() as block:
            @block.sync
            def _(sp):
                sp.dma_start(raw[:, :], A["gates"]).then_inc(gate_in, 16)
                sp.dma_start(rowvec[:, :, :], A["rowvecs"]).then_inc(gate_in, 16)
                sp.dma_start(x[:, :, :], A["x"]).then_inc(x_in, 16)
                sp.wait_ge(x_in, 16)

            @block.gpsimd
            def _(pool):
                pool.memset(ident[:, :], 0.0).then_inc(zeroed, 1)
                pool.wait_ge(zeroed, 1)
                pool.affine_select(out=ident[:, :], in_=ident[:, :], compare_op=ALU.not_equal, fill=1.0,
                                   base=0, pattern=[[-1, P]], channel_multiplier=1)

            @block.scalar
            def _(act):
                act.wait_ge(gate_in, 32)
                act.activation(gate[:, :], raw[:, :], ACT.Tanh).then_inc(gate_ready, 1)

            @block.vector
            def _(dve):
                dve.wait_ge(gate_ready, 1)
                for i, g in enumerate(ROWVECS):
                    if g is not None:
                        dve.tensor_scalar(rowvec[:, i, :], rowvec[:, i, :], gate[:, g:g + 1], None, ALU.mult)


def store(nc, x, out):
    with nc.semaphore("stored") as stored, nc.Block() as block:
        @block.sync
        def _(sp):
            sp.dma_start(out, x[:, :, :]).then_inc(stored, 16)
            sp.wait_ge(stored, 16)


G_XATTN0, G_XATTN1, G_FFN0, G_FFN1 = range(4)
ROWVECS = [G_XATTN0, G_FFN0, G_XATTN1, G_FFN1]


def build(nc, A, out, stages=5, start=0):
    with ExitStack() as ctx:
        m = Pool_(nc, ctx, "all")
        x = m.sb("x", [P, NT, D])
        xn = m.sb("xn", [P, NT, D])
        xnT = m.sb("xnT", [D, NT * P])
        ident = m.sb("ident", [P, P])
        gate = m.sb("gate", [P, 4])
        rowvec = m.sb("rowvec", [P, len(ROWVECS), D])
        setup(nc, A, x, ident, gate, rowvec, ROWVECS)
        if stages >= 1 > start:
            with ExitStack() as own:
                w = Pool_(nc, own, "w")
                wide_M = w.sb("M", [D, H, C])
                wide_VO = w.sb("VO", [C1, H, D + 1])
                wide_setup(nc, A, wide_M, wide_VO, gate[:, G_XATTN0:G_XATTN0 + 1])
                layernorm(nc, "ln0", x, xn, xnT, ident)
                wide_attention(nc, A, x, xnT, wide_M, wide_VO, rowvec[:, 0, :], ident)
        if stages >= 2 > start:
            layernorm(nc, "ln1", x, xn, xnT, ident)
            routed_attention(nc, A, x, xn, xnT, rowvec[:, 1, :], gate[:, G_FFN0:G_FFN0 + 1], ident)
        if stages >= 3 > start:
            layernorm(nc, "ln2", x, xn, xnT, ident)
            narrow_attention(nc, A, x, xnT, rowvec[:, 2, :], gate[:, G_XATTN1:G_XATTN1 + 1], ident)
        if stages >= 4 > start:
            layernorm(nc, "ln3", x, xn, xnT, ident)
            experts(nc, A, x, xnT, rowvec[:, 3, :], gate[:, G_FFN1:G_FFN1 + 1], ident)
        store(nc, x, out)


def laid_out(i):
    import numpy as np
    f = np.float32
    B, T_, C_ = i["ctx_768"].shape
    ctx = np.asarray(i["ctx_768"])
    ctx1 = np.concatenate([ctx, np.ones((B, T_, 1), f)], 2)
    padded = np.concatenate([ctx1, np.zeros((B, KT * P - T_, C1), f)], 1)
    tile = lambda v: np.tile(np.asarray(v).reshape(1, -1), (P, 1))
    gx, gf = np.asarray(i["g_xattn"]), np.asarray(i["g_ffn"])
    a = {
        "x": np.asarray(i["x"]).reshape(NT, P, D).transpose(1, 0, 2),
        "ctxT": ctx1.transpose(0, 2, 1),
        "ctx_rows": padded.reshape(B, KT, P, C1).transpose(0, 2, 1, 3),
        "gates": tile(np.concatenate([gx, gf])),
        "rowvecs": np.stack([tile(i["L0_xattn_bo"]), tile(i["L0_ffn_null_token"]),
                             tile(i["L1_xattn_bo"]), tile(i["L1_ffn_bs2"])], 1),
        "a_wq": np.asarray(i["L0_xattn_Wq"]).reshape(D, H, E0).transpose(2, 1, 0),
        "a_wk": np.asarray(i["L0_xattn_Wk"]).reshape(C, H, E0).transpose(2, 1, 0),
        "a_wv": np.asarray(i["L0_xattn_Wv"]).reshape(C, H, E0).transpose(2, 1, 0),
        "a_wo": np.asarray(i["L0_xattn_Wo"]).reshape(H, E0, D).transpose(1, 0, 2),
    }
    n = {k: np.asarray(v) for k, v in i.items()}
    for layouts in (routed_layouts, narrow_layouts, expert_layouts):
        layouts(n, a)
    return {k: np.ascontiguousarray(v) for k, v in a.items()}


def kernel(**inputs):
    import numpy as np
    import concourse.bacc as bacc
    from concourse.bass_utils import run_bass_kernel_spmd

    nc = bacc.Bacc("TRN2", target_bir_lowering=False, num_devices=1)
    arrays = laid_out(inputs)
    A = {k: nc.dram_tensor(k, v.shape, F32, kind="ExternalInput").ap() for k, v in arrays.items()}
    out = nc.dram_tensor("out", (P, NT, D), F32, kind="ExternalOutput").ap()
    build(nc, A, out)
    r = run_bass_kernel_spmd(nc, [arrays], core_ids=[0])
    y = r.results[0]["out"]
    return np.ascontiguousarray(y.transpose(1, 0, 2).reshape(NB, S, D))
```

```python
import math
from contextlib import ExitStack

import concourse.bass as bass
from concourse import mybir

P = 128
F32 = mybir.dt.float32
F16 = mybir.dt.float16
ALU = mybir.AluOpType
ACT = mybir.ActivationFunctionType
AX_X = mybir.AxisListType.X

NB, S, D = 8, 256, 128
NT = NB * S // P
TB = S // P
C, T = 96, 1601
C1 = C + 1
H = 16
NP = H // 2
KT = (T + P - 1) // P
KLAST = T - (KT - 1) * P
E0 = 64
EPS = 1e-5
SPLIT = 64.0
UNSPLIT = 1.0 / (SPLIT * SPLIT)
CHUNK = [(400 * i, T - 1200) for i in range(4)]
NC = len(CHUNK)
UNITS = H * TB


def keys(t):
    return P if t < KT - 1 else KLAST


class Chain:

    def __init__(self, eng, sem, base=0):
        self.eng, self.sem, self.base, self.n = eng, sem, base, 0

    def step(self, ins):
        ins.then_inc(self.sem, 1)
        self.n += 1
        self.eng.wait_ge(self.sem, self.base + self.n)


class Pool_:

    def __init__(self, nc, ctx, tag):
        self.nc, self.ctx, self.tag = nc, ctx, tag

    def sb(self, name, shape, dt=F32):
        return self.ctx.enter_context(self.nc.sbuf_tensor(f"{self.tag}_{name}", shape, dt))

    def ps(self, name, shape, dt=F32):
        return self.ctx.enter_context(self.nc.psum_tensor(f"{self.tag}_{name}", shape, dt))

    def sem(self, name):
        return self.ctx.enter_context(self.nc.semaphore(f"{self.tag}_{name}"))


def layernorm(nc, tag, x, xn, xnT, ident):
    with ExitStack() as ctx:
        m = Pool_(nc, ctx, tag)
        stats = m.sb("stats", [P, NT, 6])
        mv = m.sb("mv", [P, NT, 2])
        var = m.sb("var", [P, NT])
        std = m.sb("std", [P, NT])
        r = m.sb("r", [P, NT])
        e = m.sb("e", [P, NT])
        pt = m.ps("pt", [P, 4, 4 * P])
        own = m.sem("own")
        var_ready = m.sem("var_ready")
        std_ready = m.sem("std_ready")
        xn_ready = m.sem("xn_ready")
        turned = m.sem("turned")
        xnt_ready = m.sem("xnt_ready")
        stat_ready = m.sem("stat_ready")
        with nc.Block() as block:
            @block.vector
            def _(dve):
                for t in range(NT):
                    dve.bn_stats(stats[:, t, :], x[:, t, :]).then_inc(stat_ready, 1)
                for t in range(NT):
                    dve.wait_ge(stat_ready, t + 1)
                    dve.bn_aggr(mv[:, t, :], stats[:, t, :]).then_inc(stat_ready, 1)
                dve.wait_ge(stat_ready, 2 * NT)
                dve.tensor_scalar(var[:, :], mv[:, :, 1], EPS, None, ALU.add).then_inc(var_ready, 1)
                dve.wait_ge(std_ready, 1)
                c = Chain(dve, own)
                c.step(dve.reciprocal(r[:, :], std[:, :]))
                c.step(dve.tensor_tensor(e[:, :], r[:, :], r[:, :], ALU.mult))
                c.step(dve.tensor_tensor(e[:, :], e[:, :], var[:, :], ALU.mult))
                c.step(dve.tensor_scalar(e[:, :], e[:, :], -0.5, 1.5, ALU.mult, ALU.add))
                c.step(dve.tensor_tensor(r[:, :], r[:, :], e[:, :], ALU.mult))
                for t in range(NT):
                    dve.tensor_scalar(xn[:, t, :], x[:, t, :], mv[:, t, 0:1], r[:, t:t + 1],
                                      ALU.subtract, ALU.mult).then_inc(xn_ready, 1)

            @block.tensor
            def _(pe):
                for t in range(NT):
                    pe.wait_ge(xn_ready, t + 1)
                    pe.transpose(pt[:, t // 4, (t % 4) * P:(t % 4 + 1) * P], xn[:, t, :],
                                 ident[:, :]).then_inc(turned, 1)

            @block.scalar
            def _(act):
                act.wait_ge(var_ready, 1)
                act.activation(std[:, :], var[:, :], ACT.Sqrt).then_inc(std_ready, 1)
                for g in range(NT // 4):
                    act.wait_ge(turned, 4 * g + 4)
                    act.activation(xnT[:, 4 * g * P:4 * (g + 1) * P], pt[:, g, :],
                                   ACT.Copy).then_inc(xnt_ready, 1)


def wide_setup(nc, A, wide_M, wide_VO, gate):
    HB = 4
    with ExitStack() as ctx:
        m = Pool_(nc, ctx, "ws")
        wq = m.sb("wq", [E0, H, D])
        wk = m.sb("wk", [E0, H, C])
        wv = m.sb("wv", [E0, H, C])
        wo = m.sb("wo", [E0, H, D])
        pm = m.ps("pm", [P, 2, HB, 128])
        pv = m.ps("pv", [P, 2, HB, 128])
        loaded = m.sem("loaded")
        product = m.sem("product")
        kept = m.sem("kept")
        cleared = m.sem("cleared")
        with nc.Block() as block:
            @block.sync
            def _(sp):
                for sb_, dram in ((wq, A["a_wq"]), (wk, A["a_wk"]), (wv, A["a_wv"]), (wo, A["a_wo"])):
                    sp.dma_start(sb_[:, :, :], dram).then_inc(loaded, 16)

            @block.tensor
            def _(pe):
                pe.wait_ge(loaded, 64)
                for g in range(H // HB):
                    if g >= 2:
                        pe.wait_ge(kept, 2 * (g - 1))
                    for j in range(HB):
                        h = g * HB + j
                        pe.matmul(pm[:, g % 2, j, 0:C], wq[:, h, :], wk[:, h, :], start=True, stop=True)
                        ins = pe.matmul(pv[0:C, g % 2, j, :], wv[:, h, :], wo[:, h, :], start=True, stop=True)
                    ins.then_inc(product, 1)

            @block.vector
            def _(dve):
                dve.memset(wide_VO[:, :, :], 0.0).then_inc(cleared, 1)
                dve.wait_ge(cleared, 1)
                dve.memset(wide_VO[C:C1, :, D:D + 1], 1.0)
                for g in range(H // HB):
                    dve.wait_ge(product, g + 1)
                    dve.tensor_scalar(wide_M[:, g * HB:(g + 1) * HB, :], pm[:, g % 2, :, 0:C],
                                      SPLIT * E0 ** -0.5, None, ALU.mult).then_inc(kept, 1)
                    dve.tensor_scalar(wide_VO[0:C, g * HB:(g + 1) * HB, 0:D], pv[0:C, g % 2, :, :],
                                      gate[0:C, 0:1], None, ALU.mult).then_inc(kept, 1)


RING = 3
PRING = 4
WRING = 2
LIFT = 10 * math.log(2.0)
PAIR = 2 * S

OUT_SLOTS = (2, 3)


def score_slot(t):
    return t % RING if t < KT - 1 else RING


def prob_slot(t, ring=PRING):
    return t % ring if t < KT - 1 else ring


def since_last(t, ring):
    if t == KT - 1:
        return KT
    return ring if t >= ring else ring + 1


def over_batches(eng, batch):
    batch(0, 0, True)
    with eng.Fori(0, NB // 2 - 1) as i:
        batch(2 * i + 1, 1, True)
        batch(2 * i + 2, 0, True)
    batch(NB - 1, 1, False)


def pair_before(b, p):
    if isinstance(p, int) and p == 0:
        return None if isinstance(b, int) and b == 0 else (b - 1, NP - 1)
    return b, p - 1


def over_pairs(eng, pair, prepares):
    first, middle, last = ("first", "middle", "last") if prepares else ("idle",) * 3
    pair(0, 0, first, 0)
    with eng.Fori(0, NP // 2 - 1) as i:
        pair(2 * i + 1, 1, middle, i)
        pair(2 * i + 2, 0, middle, i + 1)
    pair(NP - 1, 1, last, NP // 2 - 1)


def wide_attention(nc, A, x, xnT, wide_M, wide_VO, bias, ident):
    MAXIMA = 2 * TB * NC
    FIRST = NP + 1
    BATCH = NP + NP * MAXIMA + 1 + TB * NP
    with ExitStack() as ctx:
        m = Pool_(nc, ctx, "wa")
        ctxT = m.sb("ctxT", [C1, T])
        ch = m.sb("ctx_hi", [C1, 2, T], F16)
        cl = m.sb("ctx_lo", [C1, 2, T], F16)
        rows = m.sb("ctx_rows", [P, KT, C1])
        rh = m.sb("rows_hi", [P, 2, KT, C1], F16)
        rl = m.sb("rows_lo", [P, 2, KT, C1], F16)
        qh = m.sb("q_hi", [C1, 2, H * S], F16)
        ql = m.sb("q_lo", [C1, 2, H * S], F16)
        prob = m.sb("prob", [P, WRING + 1, PAIR])
        prob_hi = m.sb("prob_hi", [P, PRING + 1, PAIR], F16)
        prob_lo = m.sb("prob_lo", [P, PRING + 1, PAIR], F16)
        lift = m.sb("lift", [P, 1])
        acc = m.sb("acc", [C1, 2, PAIR])
        mx = m.sb("mx", [P, UNITS * NC])
        mu = m.sb("mu", [P, UNITS])
        shift = m.sb("shift", [UNITS, P], F16)
        rec = m.sb("rec", [P, 2])
        scores = m.ps("scores", [P, RING + 1, PAIR])
        helper = m.ps("helper", [P, 2, 512])
        pacc = m.ps("pacc", [P, 2, PAIR])

        ctxT_in = m.sem("ctxT_in")
        rows_in = m.sem("rows_in")
        scaled = m.sem("scaled")
        hi_ready = m.sem("hi_ready")
        split = m.sem("split")
        rows_scaled = m.sem("rows_scaled")
        rows_split = m.sem("rows_split")
        lift_ready = m.sem("lift_ready")
        q_hi_ready = m.sem("q_hi_ready")
        filled = m.sem("helper_filled")
        freed = m.sem("helper_freed")
        max_filled = m.sem("max_filled")
        max_freed = m.sem("max_freed")
        mu_ready = m.sem("mu_ready")
        shift_in = m.sem("shift_in")
        scores_ready = m.sem("scores_ready")
        exp_done = m.sem("exp_done")
        lo_done = m.sem("prob_lo_done")
        pv_done = m.sem("pv_done")
        acc_ready = m.sem("acc_ready")
        x_step = m.sem("x_step")

        def maxima(kind, t):
            if kind == "first":
                n = KT - NP
                return range(MAXIMA * (t - NP) // n, MAXIMA * (t - NP + 1) // n) if t >= NP else range(0)
            if kind == "middle":
                return range(MAXIMA * t // KT, MAXIMA * (t + 1) // KT)
            return range(2 * t, 2 * t + 2) if kind == "last" and t < 8 else range(0)

        def fills_before(p, kind):
            if kind == "idle":
                return TB * (p - 1)
            return NP + MAXIMA + (MAXIMA + TB) * (p - 1)

        def start_fill(b, p, kind, par):
            if isinstance(p, int) and p == 0:
                off = 0 if isinstance(b, int) and b == 0 else -TB
            else:
                off = fills_before(p, kind)
            even = NP + MAXIMA if kind not in ("idle",) else 0
            even = 0 if isinstance(p, int) and p == 0 else even
            return FIRST + BATCH * b + off, (FIRST + BATCH * par + even) % 2

        with nc.Block() as block:
            @block.sync
            def _(sp):
                def load_T(b):
                    if b >= 1:
                        sp.wait_ge(split, b)
                    sp.dma_start(ctxT[:, :], A["ctxT"][b]).then_inc(ctxT_in, 16)

                def load_rows(b):
                    if b >= 1:
                        sp.wait_ge(rows_split, b)
                    sp.dma_start(rows[:, :, :], A["ctx_rows"][b]).then_inc(rows_in, 16)

                def put_shift(b):
                    n = FIRST if b == 0 else FIRST + BATCH * b - TB
                    sp.wait_ge(freed, n)
                    sp.dma_start(qh[C:C1, b % 2, :].rearrange("a (u q) -> a u q", u=UNITS),
                                 shift[:, :]).then_inc(shift_in, 16)

                load_T(0)
                load_rows(0)
                load_T(1)
                load_rows(1)
                put_shift(0)
                for b in range(1, NB):
                    if b + 1 < NB:
                        load_T(b + 1)
                    put_shift(b)
                    if b + 1 < NB:
                        load_rows(b + 1)

            @block.gpsimd
            def _(pool):
                def split_rows(b):
                    pool.wait_ge(rows_in, 16 * (b + 1))
                    pool.tensor_scalar(rows[:, :, :], rows[:, :, :], SPLIT, None, ALU.mult).then_inc(rows_scaled, 1)
                    if b >= 2:
                        pool.wait_ge(pv_done, KT + (b - 1) * NP * KT)
                    pool.wait_ge(rows_scaled, 2 * b + 1)
                    pool.tensor_copy(rh[:, b % 2], rows[:, :, :]).then_inc(rows_scaled, 1)
                    pool.wait_ge(rows_scaled, 2 * b + 2)
                    pool.tensor_tensor(rl[:, b % 2], rows[:, :, :], rh[:, b % 2],
                                       ALU.subtract).then_inc(rows_split, 1)

                pool.memset(lift[:, :], LIFT).then_inc(lift_ready, 1)
                split_rows(0)
                pool.tensor_tensor(x[:, :, :], x[:, :, :], bias[:, None, :].to_broadcast([P, NT, D]),
                                   ALU.add).then_inc(x_step, 1)
                for b in range(1, NB):
                    pool.wait_ge(ctxT_in, 16 * (b + 1))
                    pool.tensor_scalar(ctxT[:, :], ctxT[:, :], SPLIT, None, ALU.mult).then_inc(scaled, 1)
                    if b >= 2:
                        pool.wait_ge(scores_ready, (b - 1) * NP * KT)
                    pool.wait_ge(scaled, 2 * b - 1)
                    pool.tensor_copy(ch[:, b % 2, :], ctxT[:, :]).then_inc(scaled, 1)
                    pool.wait_ge(scaled, 2 * b)
                    pool.tensor_tensor(cl[:, b % 2, :], ctxT[:, :], ch[:, b % 2, :],
                                       ALU.subtract).then_inc(split, 1)
                    split_rows(b)

            @block.tensor
            def _(pe):
                def fill(f):
                    if not (isinstance(f, int) and f < 2):
                        pe.wait_ge(freed, f - 1)

                def q_product(nb, j, f, bank):
                    fill(f)
                    for i in range(2):
                        ins = pe.matmul(helper[0:C, bank, i * S:(i + 1) * S], wide_M[:, 2 * j + i, :],
                                        xnT[:, bass.ds(nb * S, S)], start=True, stop=True)
                    ins.then_inc(filled, 1)

                def maximum(buf, p, k, f, bank):
                    c0, w = CHUNK[k % NC]
                    fill(f)
                    pe.matmul(helper[:, bank, 0:w], qh[0:C, buf, bass.ds((4 * p + k // NC) * P, P)],
                              ch[0:C, buf, c0:c0 + w], start=True, stop=True).then_inc(filled, 1)

                def turn_mu(nb, f, bank):
                    pe.wait_ge(mu_ready, nb + 1)
                    fill(f)
                    pe.transpose(helper[0:UNITS, bank, 0:P], mu[:, :], ident[:, :]).then_inc(filled, 1)

                def score(b, p, buf, t):
                    n = (b * NP + p) * KT + t
                    if t == 0 and isinstance(p, int) and p == 0:
                        pe.wait_ge(shift_in, 16 * b + 16)
                    pe.wait_ge(exp_done, KT + n - since_last(t, RING) + 1)
                    out = scores[0:keys(t), score_slot(t), :]
                    kk = slice(t * P, t * P + keys(t))
                    qq = bass.ds(p * PAIR, PAIR)
                    pe.matmul(out, ch[:, buf, kk], qh[:, buf, qq], start=True, stop=False)
                    pe.matmul(out, ch[0:C, buf, kk], ql[0:C, buf, qq], start=False, stop=False)
                    pe.matmul(out, cl[0:C, buf, kk], qh[0:C, buf, qq],
                              start=False, stop=True).then_inc(scores_ready, 1)

                def project(b, p, par, i, f, bank):
                    if i == 0:
                        pe.wait_ge(acc_ready, b * NP + p + 3)
                    fill(f)
                    for j in range(2):
                        ins = pe.matmul(helper[:, bank, j * (D + 1):(j + 1) * (D + 1)],
                                        acc[:, par, j * S + i * P:j * S + (i + 1) * P],
                                        wide_VO[:, 2 * p + j, :], start=True, stop=True)
                    ins.then_inc(filled, 1)

                def batch(b, buf, prepares):
                    def pair(p, par, kind, _):
                        f, bank = start_fill(b, p, kind, buf)
                        n = (b * NP + p) * KT
                        before = pair_before(b, p)
                        k = 0
                        for t in range(KT):
                            if t + 2 < KT:
                                score(b, p, buf, t + 2)
                            elif kind == "last":
                                score(b + 1, 0, 1 - buf, t + 2 - KT)
                            elif not (isinstance(p, int) and p == NP - 1):
                                score(b, p + 1, buf, t + 2 - KT)
                            if kind == "first" and t < NP:
                                q_product(b + 1, t, f + k, (bank + k) % 2)
                                k += 1
                            for i in maxima(kind, t):
                                if i == 0:
                                    pe.wait_ge(q_hi_ready, NP * (b + 1) + p + 1)
                                if i == 0 and kind == "first":
                                    pe.wait_ge(split, b + 2)
                                maximum(1 - buf, p, i, f + k, (bank + k) % 2)
                                k += 1
                            if t in OUT_SLOTS and before:
                                project(*before, 1 - par, t - OUT_SLOTS[0], f + k, (bank + k) % 2)
                                k += 1
                            if kind == "last" and t == NP + 1:
                                turn_mu(b + 1, f + k, (bank + k) % 2)
                                k += 1
                            if t == 0:
                                pe.wait_ge(acc_ready, b * NP + p + 1)
                                if isinstance(p, int) and p == 0:
                                    pe.wait_ge(rows_split, b + 1)
                            pe.wait_ge(exp_done, KT + n + t + 1)
                            ks, slot = slice(0, keys(t)), prob_slot(t)
                            pe.matmul(pacc[0:C1, par, :], rh[ks, buf, t, :], prob_hi[ks, slot, :],
                                      start=(t == 0), stop=False)
                            pe.matmul(pacc[0:C1, par, :], rl[ks, buf, t, :], prob_hi[ks, slot, :],
                                      start=False, stop=False)
                            pe.wait_ge(lo_done, KT + n + t + 1)
                            pe.matmul(pacc[0:C1, par, :], rh[ks, buf, t, :], prob_lo[ks, slot, :],
                                      start=False, stop=(t == KT - 1)).then_inc(pv_done, 1)
                        if kind == "idle" and isinstance(p, int) and p == NP - 1:
                            for i in range(TB):
                                project(b, p, par, i, f + k + i, (bank + k + i) % 2)
                    over_pairs(pe, pair, prepares)

                pe.wait_ge(split, 1)
                for j in range(NP):
                    q_product(0, j, j, j % 2)
                pe.wait_ge(q_hi_ready, NP)
                with pe.Fori(0, NP) as p:
                    for k in range(MAXIMA // 2):
                        half = 2 * (k % 2)
                        pe.wait_ge(max_freed, MAXIMA // 2 * p + k + 1)
                        for i in range(2):
                            c0, w = CHUNK[(2 * k + i) % NC]
                            ins = pe.matmul(scores[:, half + i, 0:w],
                                            qh[0:C, 0, bass.ds((4 * p + 2 * k // NC) * P, P)],
                                            ch[0:C, 0, c0:c0 + w], start=True, stop=True)
                        ins.then_inc(max_filled, 1)
                turn_mu(0, FIRST - 1, (FIRST - 1) % 2)
                for t in range(2):
                    score(0, 0, 0, t)
                over_batches(pe, batch)

            @block.scalar
            def _(act):
                act.sem_inc(exp_done, KT)
                act.sem_inc(acc_ready, 2)
                act.wait_ge(lift_ready, 1)
                act.wait_ge(ctxT_in, 16)
                act.activation(ch[:, 0, :], ctxT[:, :], ACT.Copy, scale=SPLIT).then_inc(hi_ready, 1)

                def keep_q_hi(nb, buf, j, f, bank):
                    act.wait_ge(filled, f + 1)
                    act.activation(qh[0:C, buf, j * PAIR:(j + 1) * PAIR], helper[0:C, bank, :],
                                   ACT.Copy).then_inc(q_hi_ready, 1)

                def keep_acc(b, p, par):
                    act.wait_ge(pv_done, KT * (b * NP + p + 2))
                    act.activation(acc[:, par, :], pacc[0:C1, par, :], ACT.Copy).then_inc(acc_ready, 1)

                def batch(b, buf, prepares):
                    def pair(p, par, kind, _):
                        f, bank = start_fill(b, p, kind, buf)
                        before = pair_before(b, p)
                        n = (b * NP + p) * KT
                        for t in range(KT):
                            act.wait_ge(scores_ready, n + t + 1)
                            act.wait_ge(pv_done, KT + n + t - since_last(t, PRING) + 1)
                            act.wait_ge(lo_done, n + t - since_last(t, WRING) + 1 + KT)
                            for out in (prob[0:keys(t), prob_slot(t, WRING), :], prob_hi[0:keys(t), prob_slot(t), :]):
                                ins = act.activation(out, scores[0:keys(t), score_slot(t), :], ACT.Exp,
                                                     scale=UNSPLIT, bias=lift[0:keys(t), :])
                            ins.then_inc(exp_done, 1)
                            if t == 0 and before:
                                keep_acc(*before, 1 - par)
                            if kind == "first" and t < NP:
                                k = t + (sum(o < t for o in OUT_SLOTS) if before else 0)
                                keep_q_hi(b + 1, 1 - buf, t, f + k, (bank + k) % 2)
                        if kind == "idle" and isinstance(p, int) and p == NP - 1:
                            keep_acc(b, p, par)
                    over_pairs(act, pair, prepares)

                for j in range(NP):
                    keep_q_hi(0, 0, j, j, j % 2)
                over_batches(act, batch)

            @block.vector
            def _(dve):
                dve.sem_inc(pv_done, KT)
                dve.sem_inc(lo_done, KT)
                dve.sem_inc(max_freed, 2)
                dve.wait_ge(hi_ready, 1)
                dve.scalar_tensor_tensor(cl[:, 0, :], ctxT[:, :], SPLIT, ch[:, 0, :], ALU.mult,
                                         ALU.subtract).then_inc(split, 1)

                def keep_q_lo(nb, buf, j, f, bank):
                    dve.wait_ge(q_hi_ready, NP * nb + j + 1)
                    cols = slice(j * PAIR, (j + 1) * PAIR)
                    dve.tensor_tensor(ql[0:C, buf, cols], helper[0:C, bank, :], qh[0:C, buf, cols],
                                      ALU.subtract).then_inc(freed, 1)

                def maximum(p, k, f, bank):
                    w = CHUNK[k % NC][1]
                    dve.wait_ge(filled, f + 1)
                    dve.tensor_reduce(mx[:, bass.ds(MAXIMA * p + k, 1)], helper[:, bank, 0:w], AX_X,
                                      ALU.max).then_inc(freed, 1)

                def gather_mu(f):
                    dve.wait_ge(freed, f)
                    dve.tensor_reduce(mu[:, :], mx[:, :].rearrange("p (u c) -> p u c", c=NC), AX_X,
                                      ALU.max).then_inc(mu_ready, 1)

                def keep_shift(nb, f, bank):
                    dve.wait_ge(filled, f + 1)
                    if not (isinstance(nb, int) and nb == 0):
                        dve.wait_ge(shift_in, 16 * nb)
                    dve.tensor_scalar(shift[:, :], helper[0:UNITS, bank, 0:P], -1.0 / SPLIT, None,
                                      ALU.mult).then_inc(freed, 1)

                def add_out(b, p, i, f, bank):
                    v = helper[:, bank, 0:2 * (D + 1)].rearrange("p (a c) -> p a c", c=D + 1)
                    xt = x[:, TB * b + i, :]
                    s = 2 * (TB * (b * NP + p) + i) + 1
                    dve.wait_ge(filled, f + 1)
                    dve.wait_ge(freed, f)
                    dve.reciprocal(rec[:, :], v[:, :, D]).then_inc(x_step, 1)
                    dve.wait_ge(x_step, s + 1)
                    dve.scalar_tensor_tensor(xt, v[:, 0, 0:D], rec[:, 0:1], xt, ALU.mult,
                                             ALU.add).then_inc(x_step, 1)
                    dve.wait_ge(x_step, s + 2)
                    dve.scalar_tensor_tensor(xt, v[:, 1, 0:D], rec[:, 1:2], xt, ALU.mult,
                                             ALU.add).then_inc(freed, 1)

                def keep_lo(n, t):
                    ks = slice(0, keys(t))
                    dve.wait_ge(exp_done, KT + n + t + 1)
                    dve.wait_ge(pv_done, KT + n + t - since_last(t, PRING) + 1)
                    dve.tensor_tensor(prob_lo[ks, prob_slot(t), :], prob[ks, prob_slot(t, WRING), :],
                                      prob_hi[ks, prob_slot(t), :], ALU.subtract).then_inc(lo_done, 1)

                def batch(b, buf, prepares):
                    def pair(p, par, kind, _):
                        f, bank = start_fill(b, p, kind, buf)
                        before = pair_before(b, p)
                        k = 0
                        for t in range(KT):
                            keep_lo((b * NP + p) * KT, t)
                            if kind == "first" and t < NP:
                                keep_q_lo(b + 1, 1 - buf, t, f + k, (bank + k) % 2)
                                k += 1
                            for i in maxima(kind, t):
                                maximum(p, i, f + k, (bank + k) % 2)
                                k += 1
                            if t in OUT_SLOTS and before:
                                add_out(*before, t - OUT_SLOTS[0], f + k, (bank + k) % 2)
                                k += 1
                            if kind == "last" and t == NP:
                                gather_mu(f + k)
                            if kind == "last" and t == NP + 1:
                                keep_shift(b + 1, f + k, (bank + k) % 2)
                                k += 1
                        if kind == "idle" and isinstance(p, int) and p == NP - 1:
                            for i in range(TB):
                                add_out(b, p, i, f + k + i, (bank + k + i) % 2)
                    over_pairs(dve, pair, prepares)

                for j in range(NP):
                    keep_q_lo(0, 0, j, j, j % 2)
                with dve.Fori(0, NP) as p:
                    for k in range(MAXIMA // 2):
                        n, half = MAXIMA // 2 * p + k, 2 * (k % 2)
                        dve.wait_ge(max_filled, n + 1)
                        dve.tensor_reduce(mx[:, bass.ds(2 * n, 2)], scores[:, half:half + 2, 0:CHUNK[0][1]], AX_X,
                                          ALU.max).then_inc(max_freed, 1)
                dve.wait_ge(max_freed, NP * MAXIMA // 2 + 2)
                dve.wait_ge(x_step, 1)
                gather_mu(FIRST - 1)
                keep_shift(0, FIRST - 1, (FIRST - 1) % 2)
                over_batches(dve, batch)


G, NQ, NK, HR, E = 4, 128, 64, 8, 64
KK = NK + 1
CH = HR * E // P


def routed_attention(nc, A, x, xn, xnT, null, gate, ident):
    with ExitStack() as ctx:
        m = Pool_(nc, ctx, "ra")
        wq = m.sb("wq", [D, G, HR * E])
        wk = m.sb("wk", [D, G, HR * E])
        wv = m.sb("wv", [D, G, HR * E])
        wo = m.sb("wo", [P, G, CH, D])
        wr = m.sb("router", [D, G, 2, P])
        before = m.sb("before", [P, TB, S])
        ranks = m.sb("ranks", [P, NK])
        xb = m.sb("xb", [P, TB, D])
        Ls = m.sb("logits", [P, 2, S])
        dg = m.sb("diag", [P, TB, 2, P])
        junk = m.sb("junk", [P, S])
        li = m.sb("own_logit", [P, 2, TB, 2])
        later = m.sb("larger", [P, TB, 2])
        ties = m.sb("ties", [P, TB, 2])
        rank = m.sb("rank", [P, TB, 2])
        sel = m.sb("sel", [P, 2, TB, NK])
        mask = m.sb("mask", [P, G, TB])
        exq = m.sb("exq", [P, G, TB])
        qs = m.sb("q_score", [P, G, TB])
        cnt = m.sb("count", [P, TB])
        inv = m.sb("inverse", [P, TB])
        none = m.sb("none", [P, TB])
        ksT = m.sb("keysT", [D, 2, NK])
        exk = m.sb("exk", [NK, 2])
        kvs = m.sb("kv_score", [NK, 2])
        kT = m.sb("kT", [P, 2, CH, KK])
        V = m.sb("V", [KK, 2, HR * E])
        nk = m.sb("null_k", [P, G, CH])
        nv = m.sb("null_v", [KK, G, HR * E])
        qT = m.sb("qT", [P, 2, CH, S])
        Pr = m.sb("prob", [P, 2, TB, 2, CH, KK])
        m8 = m.sb("m8", [P, 2, TB, 2, CH])
        r8 = m.sb("r8", [P, 2, TB, 2, CH])
        PT = m.sb("PT", [KK, 2, CH, S])
        oT = m.sb("oT", [P, CH, S])
        summed = m.sb("summed", [P, TB, D])
        pA = m.ps("bank_logits", [P, 512])
        pM = m.ps("bank_keys", [P, 512])
        pV = m.ps("bank_values", [P, 512])
        pQ = m.ps("bank_q", [P, CH, S])
        pS = m.ps("bank_scores", [P, 2, 512])
        pT = m.ps("bank_turn", [P, 512])

        w_in = m.sem("w_in")
        const = m.sem("const")
        xb_ready = m.sem("xb_ready")
        L_full = m.sem("L_full")
        L_kept = m.sem("L_kept")
        own = m.sem("own")
        diag_ready = m.sem("diag_ready")
        own_li = m.sem("li_ready")
        routed = m.sem("routed")
        exq_done = m.sem("exq_done")
        sel_full = m.sem("sel_full")
        ks_kept = m.sem("ks_kept")
        exk_done = m.sem("exk_done")
        kvs_done = m.sem("kvs_done")
        k_full = m.sem("k_full")
        v_full = m.sem("v_full")
        k_kept = m.sem("k_kept")
        null_in = m.sem("null_in")
        v_kept = m.sem("v_kept")
        q_full = m.sem("q_full")
        q_kept = m.sem("q_kept")
        s_full = m.sem("s_full")
        s_kept = m.sem("s_kept")
        e_done = m.sem("e_done")
        r_done = m.sem("r_done")
        p_ready = m.sem("p_ready")
        t_even = m.sem("t_even")
        t_odd = m.sem("t_odd")
        even_kept = m.sem("even_kept")
        odd_kept = m.sem("odd_kept")
        o_full = m.sem("o_full")
        o_kept = m.sem("o_kept")
        y_full = m.sem("y_full")
        y_kept = m.sem("y_kept")

        def steps(eng, step, first):
            first()
            with eng.Fori(0, NB - 1) as b:
                for g in range(G):
                    step(b, g, 3)
            for g in range(G):
                step(NB - 1, g, min(G - 1 - g, 3))

        def following(b, g, k):
            return (b, g + k) if g + k < G else (b + 1, g + k - G)

        with nc.Block() as block:
            @block.sync
            def _(sp):
                for sb_, name in ((wr, "r_router"), (wq, "r_wq"), (wk, "r_wk"), (wv, "r_wv"), (wo, "r_wo"),
                                  (nk, "r_null_k")):
                    sp.dma_start(sb_[:], A[name]).then_inc(w_in, 16)
                sp.dma_start(nv[NK:KK, :, :], A["r_null_v"]).then_inc(w_in, 16)

            @block.gpsimd
            def _(pool):
                pool.iota(ranks[:, :], pattern=[[1, NK]], base=0, channel_multiplier=0,
                          allow_small_or_imprecise_dtypes=True).then_inc(const, 1)
                pool.memset(before[:, :, :], 1.0).then_inc(const, 1)
                pool.wait_ge(const, 2)
                pool.affine_select(out=before[:, :, :], in_=before[:, :, :], compare_op=ALU.is_gt, fill=0.0,
                                   base=0, pattern=[[P, TB], [-1, S]], channel_multiplier=1).then_inc(const, 1)

                def stage_x(b):
                    pool.tensor_copy(xb[:, :, :], xn[:, bass.ds(b * TB, TB), :]).then_inc(xb_ready, 1)

                def normalise(b, g, par):
                    s = b * G + g
                    for i in range(TB):
                        pool.wait_ge(r_done, TB * s + i + 1)
                        pool.tensor_tensor(Pr[:, par, i].rearrange("p e c k -> p (e c) k"),
                                           Pr[:, par, i].rearrange("p e c k -> p (e c) k"),
                                           r8[:, par, i].rearrange("p e c -> p (e c)")[:, :, None].to_broadcast([P, HR, KK]),
                                           ALU.mult).then_inc(p_ready, 1)

                def diagonal(b, g):
                    s = b * G + g
                    pool.wait_ge(L_kept, s + 1)
                    if not (isinstance(s, int) and s == 0):
                        pool.wait_ge(own_li, s)
                    for i in range(TB):
                        pool.tensor_tensor(dg[:, i], Ls[:, :, i * P:(i + 1) * P],
                                           ident[:, None, :].to_broadcast([P, 2, P]), ALU.mult).then_inc(diag_ready, 1)

                def first():
                    stage_x(0)
                    for g in range(3):
                        diagonal(0, g)
                    normalise(0, 0, 0)

                def step(b, g, more):
                    if more >= 1:
                        normalise(*following(b, g, 1), (g + 1) % 2)
                    if g + 2 == G - 1 and more >= 3:
                        pool.wait_ge(const, 3)
                        pool.wait_ge(sel_full, b * G + G)
                        stage_x(b + 1)
                    if more >= 3:
                        diagonal(*following(b, g, 3))

                steps(pool, step, first)

            @block.tensor
            def _(pe):
                def logits(b, g):
                    s = b * G + g
                    pe.wait_ge(L_kept, s)
                    if not (isinstance(s, int) and s < 3):
                        pe.wait_ge(odd_kept, TB * (s - 2) + 1)
                    for r in range(2):
                        ins = pe.matmul(pA[:, r * S:(r + 1) * S], wr[:, g, r, :], xnT[:, bass.ds(b * S, S)],
                                        start=True, stop=True)
                    ins.then_inc(L_full, 1)

                def queries(b, g):
                    s = b * G + g
                    pe.wait_ge(q_kept, s)
                    if not (isinstance(s, int) and s < 3):
                        pe.wait_ge(o_kept, s - 1)
                    for c in range(CH):
                        ins = pe.matmul(pQ[:, c, :], wq[:, g, c * P:(c + 1) * P], xnT[:, bass.ds(b * S, S)],
                                        start=True, stop=True)
                    ins.then_inc(q_full, 1)

                def gather(b, g, par):
                    s = b * G + g
                    pe.wait_ge(routed, s + 1)
                    pe.wait_ge(xb_ready, b + 1)
                    pe.wait_ge(k_kept, s)
                    for i in range(TB):
                        pe.matmul(pM[:, 0:NK], xb[:, i, :], sel[:, par, i, :], start=(i == 0), stop=(i == TB - 1))
                    for i in range(TB):
                        ins = pe.matmul(pM[0:NK, NK:NK + 1], sel[:, par, i, :], li[:, par, i, 1:2],
                                        start=(i == 0), stop=(i == TB - 1))
                    ins.then_inc(sel_full, 1)

                def keys_values(b, g, par):
                    s = b * G + g
                    pe.wait_ge(ks_kept, s + 1)
                    pe.wait_ge(exk_done, s + 1)
                    for c in range(CH):
                        ins = pe.matmul(pM[:, P + c * NK:P + (c + 1) * NK], wk[:, g, c * P:(c + 1) * P],
                                        ksT[:, par, :], start=True, stop=True)
                    ins.then_inc(k_full, 1)
                    pe.wait_ge(v_kept, s)
                    if not (isinstance(s, int) and s < 3):
                        pe.wait_ge(y_kept, TB * (s - 2) + 1)
                    pe.matmul(pV[0:NK, :], ksT[:, par, :], wv[:, g, :], start=True, stop=True).then_inc(v_full, 1)

                def scores(b, g, par, i):
                    s = b * G + g
                    if i == 0:
                        pe.wait_ge(q_kept, s + 1)
                        pe.wait_ge(k_kept, s + 1)
                        pe.wait_ge(null_in, s + 1)
                    pe.wait_ge(s_kept, TB * s + i + 1)
                    for c in range(CH):
                        for e in range(2):
                            ins = pe.matmul(pS[:, e, c * KK:(c + 1) * KK],
                                            qT[e * E:(e + 1) * E, par, c, i * P:(i + 1) * P],
                                            kT[e * E:(e + 1) * E, par, c, :], start=True, stop=True)
                    ins.then_inc(s_full, 1)

                def turn(b, g, par, i, more):
                    s = b * G + g
                    pe.wait_ge(p_ready, TB * s + i + 1)
                    if i == 0:
                        pe.wait_ge(L_kept, s + 3 if more >= 2 else NB * G)
                    for e, (bank, kept, done) in enumerate(((pT, even_kept, t_even), (pA, odd_kept, t_odd))):
                        pe.wait_ge(kept, TB * s + i + 1)
                        for c in range(CH):
                            ins = pe.transpose(bank[0:KK, c * P:(c + 1) * P], Pr[:, par, i, e, c, :], ident[:, :])
                        ins.then_inc(done, 1)

                def values_product(b, g, par, more):
                    s = b * G + g
                    if more >= 2:
                        pe.wait_ge(q_kept, s + 3)
                    pe.wait_ge(even_kept, TB * (s + 1) + 1)
                    pe.wait_ge(odd_kept, TB * (s + 1) + 1)
                    pe.wait_ge(v_kept, s + 1)
                    for c in range(CH):
                        for e in range(2):
                            h = 2 * c + e
                            ins = pe.matmul(pQ[e * E:(e + 1) * E, c, :], V[:, par, h * E:(h + 1) * E],
                                            PT[:, e, c, :], start=True, stop=True)
                    ins.then_inc(o_full, 1)

                def output(b, g, more):
                    s = b * G + g
                    pe.wait_ge(o_kept, s + 2)
                    if more >= 2:
                        pe.wait_ge(v_kept, s + 3)
                    else:
                        pe.wait_ge(y_kept, TB * s + 1)
                    for i in range(TB):
                        for c in range(CH):
                            ins = pe.matmul(pV[:, i * P:(i + 1) * P], oT[:, c, i * P:(i + 1) * P], wo[:, g, c, :],
                                            start=(c == 0), stop=(c == CH - 1))
                    ins.then_inc(y_full, 1)

                def first():
                    pe.wait_ge(w_in, 16 * 7)
                    logits(0, 0)
                    queries(0, 0)
                    gather(0, 0, 0)
                    logits(0, 1)
                    keys_values(0, 0, 0)
                    queries(0, 1)
                    scores(0, 0, 0, 0)
                    gather(0, 1, 1)
                    logits(0, 2)
                    scores(0, 0, 0, 1)
                    keys_values(0, 1, 1)

                def step(b, g, more):
                    par = g % 2
                    n1, n2, n3 = (following(b, g, k) for k in (1, 2, 3))
                    if more >= 1:
                        scores(*n1, 1 - par, 0)
                    turn(b, g, par, 0, more)
                    if more >= 2:
                        queries(*n2)
                    if more >= 1:
                        scores(*n1, 1 - par, 1)
                    turn(b, g, par, 1, more)
                    if more >= 2:
                        gather(*n2, par)
                    if more >= 3:
                        logits(*n3)
                    values_product(b, g, par, more)
                    if more >= 2:
                        keys_values(*n2, par)
                    output(b, g, more)

                steps(pe, step, first)

            @block.scalar
            def _(act):
                act.sem_inc(even_kept, 1)
                act.sem_inc(o_kept, 1)

                def keep_logits(b, g):
                    s = b * G + g
                    act.wait_ge(L_full, s + 1)
                    act.wait_ge(routed, s)
                    act.activation(Ls[:, :, :].rearrange("p r n -> p (r n)"), pA[:, :], ACT.Copy).then_inc(L_kept, 1)

                def keep_queries(b, g, par):
                    s = b * G + g
                    act.wait_ge(q_full, s + 1)
                    act.activation(qT[:, par, :, :], pQ[:, :, :], ACT.Copy, scale=E ** -0.5).then_inc(q_kept, 1)

                def exp_logits(b, g, par):
                    s = b * G + g
                    act.wait_ge(own_li, s + 1)
                    act.activation(exq[:, g, :], li[:, par, :, 0], ACT.Exp, scale=-1.0).then_inc(exq_done, 1)
                    act.wait_ge(ks_kept, s + 1)
                    act.activation(exk[:, par:par + 1], pM[0:NK, NK:NK + 1], ACT.Exp, scale=-1.0).then_inc(exk_done, 1)

                def keep_keys_values(b, g, par):
                    s = b * G + g
                    act.wait_ge(k_full, s + 1)
                    act.activation(kT[:, par, :, 0:NK],
                                   pM[:, P:P + CH * NK].rearrange("p (c k) -> p c k", c=CH),
                                   ACT.Copy).then_inc(k_kept, 1)
                    act.wait_ge(v_full, s + 1)
                    act.wait_ge(kvs_done, s + 1)
                    act.activation(V[0:NK, par, :], pV[0:NK, :], ACT.Copy, scale=kvs[:, par:par + 1]).then_inc(v_kept, 1)

                def exp_scores(b, g, par, i):
                    act.wait_ge(s_kept, TB * (b * G + g) + i + 2)
                    act.activation(Pr[:, par, i], Pr[:, par, i], ACT.Exp).then_inc(e_done, 1)

                def keep_even(b, g, i):
                    act.wait_ge(t_even, TB * (b * G + g) + i + 1)
                    act.activation(PT[:, 0, :, i * P:(i + 1) * P],
                                   pT[0:KK, :].rearrange("p (c q) -> p c q", c=CH), ACT.Copy).then_inc(even_kept, 1)

                def keep_heads(b, g):
                    act.wait_ge(o_full, b * G + g + 1)
                    act.activation(oT[:, :, :], pQ[:, :, :], ACT.Copy).then_inc(o_kept, 1)

                def first():
                    keep_logits(0, 0)
                    keep_queries(0, 0, 0)
                    exp_logits(0, 0, 0)
                    keep_logits(0, 1)
                    keep_keys_values(0, 0, 0)
                    keep_queries(0, 1, 1)
                    exp_scores(0, 0, 0, 0)
                    exp_logits(0, 1, 1)
                    keep_logits(0, 2)
                    exp_scores(0, 0, 0, 1)
                    keep_keys_values(0, 1, 1)

                def step(b, g, more):
                    par = g % 2
                    n1, n2, n3 = (following(b, g, k) for k in (1, 2, 3))
                    if more >= 1:
                        exp_scores(*n1, 1 - par, 0)
                    keep_even(b, g, 0)
                    if more >= 2:
                        keep_queries(*n2, par)
                    if more >= 1:
                        exp_scores(*n1, 1 - par, 1)
                    keep_even(b, g, 1)
                    if more >= 2:
                        exp_logits(*n2, par)
                    if more >= 3:
                        keep_logits(*n3)
                    keep_heads(b, g)
                    if more >= 2:
                        keep_keys_values(*n2, par)

                steps(act, step, first)

            @block.vector
            def _(dve):
                for kept in (s_kept, odd_kept, y_kept):
                    dve.sem_inc(kept, 1)
                FIRST_STEPS = 2 * 11 + 2 * TB + 4
                BATCH_STEPS = G * (2 * TB + 11 + 4) + 4 + 2 * TB

                def own_logits(b, g, par):
                    s = b * G + g
                    dve.wait_ge(diag_ready, TB * (s + 1))
                    dve.tensor_reduce(li[:, par], dg[:, :, :, :], AX_X, ALU.add).then_inc(own_li, 1)
                    dve.wait_ge(own_li, s + 1)

                def rank_tile(c, par, i):
                    for r in range(2):
                        own_logit = li[:, par, i, r:r + 1]
                        c.step(dve.tensor_scalar(junk[:, :], Ls[:, r, :], own_logit, 0.0, ALU.is_gt, ALU.add,
                                                 accum_out=later[:, i, r:r + 1]))
                        c.step(dve.scalar_tensor_tensor(junk[:, :], Ls[:, r, :], own_logit, before[:, i, :],
                                                        ALU.is_equal, ALU.mult,
                                                        accum_out=ties[:, i, r:r + 1]))

                def route(c, g, par):
                    c.step(dve.tensor_tensor(rank[:, :, :], later[:, :, :], ties[:, :, :], ALU.add))
                    c.step(dve.tensor_scalar(mask[:, g, :], rank[:, :, 0], float(NQ), None, ALU.is_lt))
                    dve.tensor_tensor(sel[:, par], ranks[:, None, :].to_broadcast([P, TB, NK]),
                                      rank[:, :, 1:2].to_broadcast([P, TB, NK]), ALU.is_equal).then_inc(routed, 1)

                def route_all(c, b, g, par):
                    own_logits(b, g, par)
                    for i in range(TB):
                        rank_tile(c, par, i)
                    route(c, g, par)

                def weigh(c, b, g, par):
                    s = b * G + g
                    dve.wait_ge(sel_full, s + 1)
                    dve.tensor_copy(ksT[:, par, :], pM[:, 0:NK]).then_inc(ks_kept, 1)
                    dve.wait_ge(exq_done, s + 1)
                    dve.wait_ge(exk_done, s + 1)
                    c.step(dve.tensor_scalar(exk[:, par:par + 1], exk[:, par:par + 1], 1.0, None, ALU.add))
                    dve.reciprocal(kvs[:, par:par + 1], exk[:, par:par + 1]).then_inc(kvs_done, 1)

                def null_key(b, g, par):
                    s = b * G + g
                    dve.wait_ge(k_kept, s + 1)
                    dve.wait_ge(v_kept, s + 1)
                    dve.tensor_copy(V[NK:KK, par, :], nv[NK:KK, g, :])
                    dve.tensor_copy(kT[:, par, :, NK:KK], nk[:, g, :, None]).then_inc(null_in, 1)

                def keep_scores(c, b, g, par, i):
                    dve.wait_ge(s_full, TB * (b * G + g) + i + 1)
                    v = pS[:, :, 0:CH * KK].rearrange("p e (c k) -> p e c k", c=CH)
                    c.step(dve.tensor_reduce(m8[:, par, i], v, AX_X, ALU.max))
                    dve.tensor_tensor(Pr[:, par, i], v, m8[:, par, i, :, :, None].to_broadcast([P, 2, CH, KK]),
                                      ALU.subtract).then_inc(s_kept, 1)

                def denominators(c, b, g, par, i):
                    dve.wait_ge(e_done, TB * (b * G + g) + i + 1)
                    c.step(dve.tensor_reduce(m8[:, par, i], Pr[:, par, i], AX_X, ALU.add))
                    dve.reciprocal(r8[:, par, i], m8[:, par, i]).then_inc(r_done, 1)

                def keep_odd(b, g, i):
                    dve.wait_ge(t_odd, TB * (b * G + g) + i + 1)
                    dve.tensor_copy(PT[:, 1, :, i * P:(i + 1) * P],
                                    pA[0:KK, :].rearrange("p (c q) -> p c q", c=CH)).then_inc(odd_kept, 1)

                def query_scores(c, g):
                    c.step(dve.tensor_scalar(exq[:, g, :], exq[:, g, :], 1.0, None, ALU.add))
                    c.step(dve.reciprocal(exq[:, g, :], exq[:, g, :]))
                    c.step(dve.tensor_tensor(qs[:, g, :], exq[:, g, :], mask[:, g, :], ALU.mult))
                    if g == 0:
                        c.step(dve.tensor_copy(cnt[:, :], mask[:, g, :]))
                    else:
                        c.step(dve.tensor_tensor(cnt[:, :], cnt[:, :], mask[:, g, :], ALU.add))

                def add_output(b, g):
                    s = b * G + g
                    dve.wait_ge(y_full, s + 1)
                    dve.wait_ge(y_kept, TB * s + 1)
                    for i in range(TB):
                        y = pV[:, i * P:(i + 1) * P]
                        if g == 0:
                            dve.tensor_scalar(summed[:, i, :], y, qs[:, g, i:i + 1], None,
                                              ALU.mult).then_inc(y_kept, 1)
                        else:
                            dve.scalar_tensor_tensor(summed[:, i, :], y, qs[:, g, i:i + 1], summed[:, i, :],
                                                     ALU.mult, ALU.add).then_inc(y_kept, 1)

                def add_mean(c, b):
                    c.step(dve.tensor_scalar(inv[:, :], cnt[:, :], 1e-5, None, ALU.max))
                    c.step(dve.reciprocal(inv[:, :], inv[:, :]))
                    c.step(dve.tensor_scalar(inv[:, :], inv[:, :], gate, None, ALU.mult))
                    c.step(dve.tensor_scalar(none[:, :], cnt[:, :], 0.0, None, ALU.is_equal))
                    dve.wait_ge(y_kept, TB * G * (b + 1) + 1)
                    for i in range(TB):
                        xt = x[:, TB * b + i, :]
                        c.step(dve.scalar_tensor_tensor(xt, summed[:, i, :], inv[:, i:i + 1], xt,
                                                        ALU.mult, ALU.add))
                        c.step(dve.scalar_tensor_tensor(xt, null, none[:, i:i + 1], xt, ALU.mult, ALU.add))

                def first():
                    c = Chain(dve, own)
                    dve.wait_ge(const, 3)
                    dve.wait_ge(w_in, 16 * 7)
                    route_all(c, 0, 0, 0)
                    weigh(c, 0, 0, 0)
                    route_all(c, 0, 1, 1)
                    null_key(0, 0, 0)
                    keep_scores(c, 0, 0, 0, 0)
                    weigh(c, 0, 1, 1)
                    denominators(c, 0, 0, 0, 0)
                    keep_scores(c, 0, 0, 0, 1)
                    denominators(c, 0, 0, 0, 1)
                    null_key(0, 1, 1)
                    own_logits(0, 2, 0)
                    rank_tile(c, 0, 0)
                    assert c.n == FIRST_STEPS, c.n

                def step(b, g, more):
                    par = g % 2
                    n1, n2, n3 = (following(b, g, k) for k in (1, 2, 3))
                    if g == 0:
                        step.chain = Chain(dve, own, FIRST_STEPS + BATCH_STEPS * b)
                    c = step.chain
                    if more >= 1:
                        keep_scores(c, *n1, 1 - par, 0)
                    keep_odd(b, g, 0)
                    if more >= 2:
                        rank_tile(c, par, 1)
                        route(c, n2[1], par)
                    if more >= 1:
                        keep_scores(c, *n1, 1 - par, 1)
                    keep_odd(b, g, 1)
                    if more >= 1:
                        denominators(c, *n1, 1 - par, 0)
                    if more >= 2:
                        weigh(c, *n2, par)
                    query_scores(c, g)
                    if more >= 1:
                        denominators(c, *n1, 1 - par, 1)
                    if more >= 3:
                        own_logits(*n3, 1 - par)
                        rank_tile(c, 1 - par, 0)
                    if more >= 2:
                        null_key(*n2, par)
                    add_output(b, g)
                    if g == G - 1:
                        add_mean(c, b)
                        if more >= 3:
                            assert c.n == BATCH_STEPS, c.n

                steps(dve, step, first)


def routed_layouts(n, a):
    import numpy as np
    wkv = n["L0_ffn_w_kv"].reshape(G, 2, HR * E, D)
    router = np.stack([n["L0_ffn_w_qr"], n["L0_ffn_w_kvr"]], 1)
    a["r_router"] = np.broadcast_to(router.transpose(2, 0, 1)[:, :, :, None], (D, G, 2, P))
    a["r_wq"] = n["L0_ffn_w_q"].transpose(2, 0, 1)
    a["r_wk"] = wkv[:, 0].transpose(2, 0, 1)
    a["r_wv"] = wkv[:, 1].transpose(2, 0, 1)
    a["r_wo"] = n["L0_ffn_w_out"].reshape(G, D, CH, P).transpose(3, 0, 2, 1)
    nkv = n["L0_ffn_null_kv"].reshape(2, G, HR * E)
    a["r_null_k"] = nkv[0].reshape(G, CH, P).transpose(2, 0, 1)
    a["r_null_v"] = nkv[1][None]


DH = D // H
GH = 4
NG = H // GH
QD = P // GH
VD = DH + 1
KCHUNK = [(0, 401), (401, 400), (801, 400), (1201, 400)]


NRING = 3


def narrow_slot(t, par):
    return (t + par) % NRING


def narrow_since(t, par):
    if par == 1 or t >= NRING:
        return NRING
    return next(d for d in range(1, KT) if d > t and narrow_slot(KT + t - d, 1) == narrow_slot(t, 0))


def narrow_attention(nc, A, x, xnT, bias, gate, ident):
    MAXIMA = 2 * TB * NC
    VT = 2
    NV = (KT + VT - 1) // VT
    PREP = NG + NG * NC + NV
    FIRST = PREP + 1
    CARRY = TB + 2
    BATCH = PREP + NP * MAXIMA + 1 + TB * NP + 2
    PER_SLOT = 3
    QSLOTS = (PREP + PER_SLOT - 1) // PER_SLOT
    with ExitStack() as ctx:
        m = Pool_(nc, ctx, "na")
        wq = m.sb("wq", [D, NG, P])
        bq = m.sb("bq", [P, NG])
        wk = m.sb("wk", [C1, NG, P])
        wv = m.sb("wv", [C1, H * VD])
        wo = m.sb("wo", [D, D])
        lows = m.sb("lows", [P, 2])
        fold = m.sb("fold", [P, 2 * VD])
        ctxT = m.sb("ctxT", [C1, T])
        k16 = m.sb("k16", [P, 2, NG, T], F16)
        kh = m.sb("kh", [P, NRING, KCHUNK[0][1]], F16)
        q16 = m.sb("q16", [P, 2, H * S], F16)
        qa = m.sb("qa", [P, S])
        q_h = m.sb("q_h", [P, S], F16)
        vall = m.sb("vall", [P, 2, KT, H * VD])
        vst = m.sb("vst", [P, 2, KT, 2, QD])
        prob = m.sb("prob", [P, PRING + 1, PAIR])
        acc = m.sb("acc", [P, 2, S])
        mx = m.sb("mx", [P, UNITS * NC])
        mu = m.sb("mu", [P, UNITS])
        shift = m.sb("shift", [UNITS, P], F16)
        att = m.sb("att", [P, TB, H, VD])
        rec = m.sb("rec", [P, TB, H])
        attn = m.sb("attn", [P, TB, D])
        attnT = m.sb("attnT", [D, TB * P])
        banks = m.ps("banks", [P, 2 * NRING, 512])
        scores = banks[:, 0:NRING, :]
        helper = banks[:, NRING:2 * NRING, :]
        pacc = m.ps("pacc", [P, 2, 512])

        w_in = m.sem("w_in")
        w_ready = m.sem("w_ready")
        ctxT_in = m.sem("ctxT_in")
        v_clear = m.sem("v_clear")
        v_staged = m.sem("v_staged")
        kh_ready = m.sem("kh_ready")
        q_clear = m.sem("q_clear")
        qa_ready = m.sem("qa_ready")
        q_parts = m.sem("q_parts")
        filled = m.sem("helper_filled")
        freed = m.sem("helper_freed")
        prepared = m.sem("prepared")
        max_filled = m.sem("max_filled")
        max_freed = m.sem("max_freed")
        mu_ready = m.sem("mu_ready")
        shift_in = m.sem("shift_in")
        scores_ready = m.sem("scores_ready")
        exp_done = m.sem("exp_done")
        pv_done = m.sem("pv_done")
        acc_ready = m.sem("acc_ready")
        out_step = m.sem("out_step")
        attn_ready = m.sem("attn_ready")
        attnT_ready = m.sem("attnT_ready")

        def column(i, g):
            return (i * NG + g) * S

        def prep_items(kind, t):
            if kind != "first":
                return range(0)
            return range(PER_SLOT * t, min(PER_SLOT * (t + 1), PREP))

        def maxima(kind, t):
            if kind == "first":
                return range(4 * (t - QSLOTS), 4 * (t - QSLOTS + 1)) if QSLOTS <= t < QSLOTS + 4 else range(0)
            if kind == "middle":
                return range(MAXIMA * t // KT, MAXIMA * (t + 1) // KT)
            return range(2 * t, 2 * t + 2) if kind == "last" and t < 8 else range(0)

        assert QSLOTS + 4 <= KT

        def start_fill(b, p, kind, par):
            assert FIRST % NRING == 1 and BATCH % NRING == 0 and (MAXIMA + TB) % NRING == 0
            if isinstance(p, int) and p == 0:
                carried = 0 if isinstance(b, int) and b == 0 else CARRY
                return FIRST + BATCH * b - carried, (FIRST - carried) % NRING
            if kind == "idle":
                return FIRST + BATCH * b + TB * (p - 1), 0
            return FIRST + BATCH * b + PREP + MAXIMA + (MAXIMA + TB) * (p - 1), (FIRST + PREP + MAXIMA) % NRING

        def is_p(p, v):
            return isinstance(p, int) and p == v

        with nc.Block() as block:
            @block.sync
            def _(sp):
                for sb_, name in ((wq, "n_wq"), (bq, "n_bq"), (wk, "n_wk"), (wv, "n_wv"), (wo, "n_wo"),
                                  (lows, "n_lows"), (fold, "n_fold")):
                    sp.dma_start(sb_[:], A[name]).then_inc(w_in, 16)

                def load_T(b):
                    if b >= 1:
                        sp.wait_ge(filled, PREP if b == 1 else FIRST + BATCH * (b - 2) + PREP)
                    sp.dma_start(ctxT[:, :], A["ctxT"][b]).then_inc(ctxT_in, 16)

                def put_shift(b):
                    n = FIRST if b == 0 else FIRST + BATCH * b - CARRY
                    sp.wait_ge(freed, n)
                    for i in range(GH):
                        row, units = QD * i + 3 * DH, slice(TB * NG * i, TB * NG * (i + 1))
                        sp.dma_start(q16[row:row + 1, b % 2, column(i, 0):column(i + 1, 0)]
                                     .rearrange("a (u q) -> a u q", q=P), shift[units, :]).then_inc(shift_in, 16)

                load_T(0)
                load_T(1)
                put_shift(0)
                for b in range(1, NB):
                    if b + 1 < NB:
                        load_T(b + 1)
                    put_shift(b)

            @block.gpsimd
            def _(pool):
                pool.memset(vall[:, :, KT - 1, :], 0.0).then_inc(v_clear, 1)
                pool.memset(vst[:, :, :, :, :], 0.0).then_inc(v_clear, 1)
                pool.wait_ge(v_clear, 2)

                def batch(b, buf, prepares):
                    with pool.Fori(0, NP // 2) as i:
                        for par in range(2):
                            p = 2 * i + par
                            pool.wait_ge(prepared, b + 1)
                            pool.wait_ge(pv_done, KT * (b * NP + p) + 1)
                            for j in range(2):
                                pool.tensor_copy(vst[:, par, :, j, 0:VD],
                                                 vall[:, buf, :, bass.ds((2 * p + j) * VD, VD)]).then_inc(v_staged, 1)

                over_batches(pool, batch)

            @block.tensor
            def _(pe):
                def fill(f, alone=False):
                    if alone:
                        pe.wait_ge(freed, f)
                    elif not (isinstance(f, int) and f < NRING):
                        pe.wait_ge(freed, f - NRING + 1)

                def prepare(nb, j, f, bank):
                    fill(f)
                    if j < NG:
                        ins = pe.matmul(helper[:, bank, 0:S], wq[:, j, :], xnT[:, bass.ds(nb * S, S)],
                                        start=True, stop=True)
                    elif j < NG + NG * NC:
                        g, c = divmod(j - NG, NC)
                        c0, w = KCHUNK[c]
                        if j == NG:
                            pe.wait_ge(ctxT_in, 16 * nb + 16)
                        ins = pe.matmul(helper[:, bank, 0:w], wk[:, g, :], ctxT[:, c0:c0 + w], start=True, stop=True)
                    else:
                        t0 = VT * (j - NG - NG * NC)
                        for i, t in enumerate(range(t0, min(t0 + VT, KT))):
                            ins = pe.matmul(helper[0:keys(t), bank, i * H * VD:(i + 1) * H * VD],
                                            ctxT[:, t * P:t * P + keys(t)], wv[:, :], start=True, stop=True)
                    ins.then_inc(filled, 1)

                def maximum(buf, p, g, par, k, f, bank):
                    c0, w = CHUNK[k % NC]
                    fill(f)
                    j, q = divmod(k // NC, TB)
                    pe.matmul(helper[:, bank, 0:w], q16[:, buf, bass.ds(column(2 * par + j, g) + q * P, P)],
                              k16[:, buf, g, c0:c0 + w], start=True, stop=True).then_inc(filled, 1)

                def turn_mu(nb, f, bank):
                    pe.wait_ge(mu_ready, nb + 1)
                    fill(f)
                    pe.transpose(helper[0:UNITS, bank, 0:P], mu[:, :], ident[:, :]).then_inc(filled, 1)

                def score(b, p, g, par, buf, t):
                    n = (b * NP + p) * KT + t
                    if t == 0 and is_p(p, 0):
                        pe.wait_ge(shift_in, 16 * GH * (b + 1))
                    pe.wait_ge(exp_done, KT + n - narrow_since(t, par) + 1)
                    pe.matmul(scores[0:keys(t), narrow_slot(t, par), :], k16[:, buf, g, t * P:t * P + keys(t)],
                              q16[:, buf, :].rearrange("p (i c) -> p i c", i=GH)
                              [:, 2 * par:2 * par + 2, bass.ds(g * S, S)], start=True, stop=True).then_inc(scores_ready, 1)

                def attend(p, par, t):
                    for j in range(2):
                        r = QD * (2 * (t % 2) + j)
                        ins = pe.matmul(pacc[r:r + QD, par, 0:S], vst[0:keys(t), par, t, j, :],
                                        prob[0:keys(t), prob_slot(t), j * S:(j + 1) * S],
                                        start=(t < 2), stop=(t >= KT - 2))
                    ins.then_inc(pv_done, 1)

                def project(b, p, par, f, bank, alone):
                    pe.wait_ge(acc_ready, b * NP + p + 3)
                    for i in range(TB):
                        fill(f + i, alone)
                        pe.matmul(helper[:, (bank + i) % NRING, 0:2 * VD], acc[:, par, i * P:(i + 1) * P], fold[:, :],
                                  start=True, stop=True).then_inc(filled, 1)

                def turn_out(b, f, bank, alone=False):
                    pe.wait_ge(attn_ready, b + 1)
                    fill(f, alone)
                    for i in range(TB):
                        ins = pe.transpose(helper[:, bank, i * P:(i + 1) * P], attn[:, i, :], ident[:, :])
                    ins.then_inc(filled, 1)

                def output(b, f, bank, alone=False):
                    fill(f, alone)
                    pe.wait_ge(attnT_ready, b + 1)
                    for i in range(TB):
                        ins = pe.matmul(helper[:, bank, i * P:(i + 1) * P], attnT[:, i * P:(i + 1) * P],
                                        wo[:, :], start=True, stop=True)
                    ins.then_inc(filled, 1)

                def batch(b, buf, prepares):
                    def pair(p, par, kind, g):
                        f, bank = start_fill(b, p, kind, buf)
                        n = (b * NP + p) * KT
                        k = 0
                        before = pair_before(b, p)
                        gn = g + 1 if par == 1 and not is_p(p, NP - 1) else g
                        for t in range(KT):
                            if t + 2 < KT:
                                score(b, p, g, par, buf, t + 2)
                            elif kind == "last":
                                score(b + 1, 0, 0, 0, 1 - buf, t + 2 - KT)
                            elif not is_p(p, NP - 1):
                                score(b, p + 1, gn, 1 - par, buf, t + 2 - KT)
                            for i in prep_items(kind, t):
                                prepare(b + 1, i, f + k, (bank + k) % NRING)
                                k += 1
                            for i in maxima(kind, t)[:1]:
                                maximum(1 - buf, p, g, par, i, f + k, (bank + k) % NRING)
                                k += 1
                            if t == 1:
                                pe.wait_ge(acc_ready, b * NP + p + 1)
                                pe.wait_ge(v_staged, 2 * (b * NP + p + 1))
                            if t % 2 == 1 or t == KT - 1:
                                pe.wait_ge(exp_done, KT + n + t + 1)
                                if t % 2 == 1:
                                    attend(p, par, t - 1)
                                attend(p, par, t)
                            for i in maxima(kind, t)[1:]:
                                maximum(1 - buf, p, g, par, i, f + k, (bank + k) % NRING)
                                k += 1
                            if t == 2 and before:
                                project(*before, 1 - par, f + k, (bank + k) % NRING,
                                        kind == "idle" and not is_p(p, 0))
                                k += TB
                            if t in (5, 7) and before and is_p(p, 0):
                                (turn_out if t == 5 else output)(b - 1, f + k, (bank + k) % NRING)
                                k += 1
                            if kind == "last" and t == 9:
                                turn_mu(b + 1, f + k, (bank + k) % NRING)
                                k += 1
                        if kind == "idle" and is_p(p, NP - 1):
                            project(b, p, par, f + k, (bank + k) % NRING, True)
                            turn_out(b, f + k + TB, (bank + k + TB) % NRING, True)
                            output(b, f + k + TB + 1, (bank + k + TB + 1) % NRING, True)
                    over_pairs(pe, pair, prepares)

                pe.wait_ge(w_ready, 4)
                for j in range(PREP):
                    prepare(0, j, j, j % NRING)
                pe.wait_ge(prepared, 1)
                for n in range(NP * MAXIMA // 2):
                    half, unit = 2 * (n % 2), 2 * n // NC
                    h, q = divmod(unit, TB)
                    g, i_ = divmod(h, GH)
                    c = column(i_, g) + q * P
                    pe.wait_ge(max_freed, n + 1)
                    for i in range(2):
                        c0, w = CHUNK[(2 * n + i) % NC]
                        ins = pe.matmul(banks[:, half + i, 0:w], q16[:, 0, c:c + P],
                                        k16[:, 0, g, c0:c0 + w], start=True, stop=True)
                    ins.then_inc(max_filled, 1)
                turn_mu(0, FIRST - 1, (FIRST - 1) % NRING)
                for t in range(2):
                    score(0, 0, 0, 0, 0, t)
                over_batches(pe, batch)

            @block.scalar
            def _(act):
                act.sem_inc(exp_done, KT)
                act.sem_inc(acc_ready, 2)

                def keep_k_hi(nb, j, f, bank):
                    w = KCHUNK[(j - NG) % NC][1]
                    act.wait_ge(filled, f + 1)
                    act.activation(kh[:, bank, 0:w], helper[:, bank, 0:w], ACT.Copy).then_inc(kh_ready, 1)

                def keep_q(nb, j, f, bank):
                    act.wait_ge(filled, f + 1)
                    act.wait_ge(q_parts, GH * (NG * nb + j) + 1)
                    act.activation(qa[:, :], helper[:, bank, 0:S], ACT.Identity, bias=bq[:, j:j + 1]).then_inc(qa_ready, 1)
                    act.wait_ge(qa_ready, 2 * (NG * nb + j) + 1)
                    act.activation(q_h[:, :], qa[:, :], ACT.Copy).then_inc(qa_ready, 1)

                def keep_acc(b, p, par):
                    act.wait_ge(pv_done, KT * (b * NP + p + 2))
                    act.activation(acc[:, par, :], pacc[:, par, 0:S], ACT.Copy).then_inc(acc_ready, 1)

                def batch(b, buf, prepares):
                    def pair(p, par, kind, _):
                        f, bank = start_fill(b, p, kind, buf)
                        before = pair_before(b, p)
                        n = (b * NP + p) * KT
                        k = 0
                        for t in range(KT):
                            act.wait_ge(scores_ready, n + t + 1)
                            act.wait_ge(pv_done, KT + n + t - since_last(t, PRING) + 1)
                            act.activation(prob[0:keys(t), prob_slot(t), :],
                                           scores[0:keys(t), narrow_slot(t, par), :], ACT.Exp,
                                           scale=UNSPLIT).then_inc(exp_done, 1)
                            if t == 0 and before:
                                keep_acc(*before, 1 - par)
                            for i in prep_items(kind, t):
                                if i < NG:
                                    keep_q(b + 1, i, f + k, (bank + k) % NRING)
                                elif i < NG + NG * NC:
                                    keep_k_hi(b + 1, i, f + k, (bank + k) % NRING)
                                k += 1
                            if t == 2 and before:
                                k += TB
                            if t in (5, 7) and before and is_p(p, 0):
                                k += 1
                        if kind == "idle" and is_p(p, NP - 1):
                            keep_acc(b, p, par)
                    over_pairs(act, pair, prepares)

                act.wait_ge(w_ready, 4)
                for j in range(NG + NG * NC):
                    (keep_q if j < NG else keep_k_hi)(0, j, j, j % NRING)
                over_batches(act, batch)

            @block.vector
            def _(dve):
                dve.sem_inc(pv_done, KT)
                dve.sem_inc(q_parts, 1)
                dve.sem_inc(max_freed, 2)
                dve.memset(q16[:, :, :], 0.0).then_inc(q_clear, 1)
                dve.tensor_tensor(x[:, :, :], x[:, :, :], bias[:, None, :].to_broadcast([P, NT, D]),
                                  ALU.add).then_inc(q_clear, 1)
                dve.wait_ge(w_in, 16 * 7)
                dve.tensor_scalar(wk[:, :, :], wk[:, :, :], SPLIT, None, ALU.mult).then_inc(w_ready, 1)
                dve.tensor_scalar(wq[:, :, :], wq[:, :, :], SPLIT * DH ** -0.5, None, ALU.mult).then_inc(w_ready, 1)
                dve.tensor_scalar(bq[:, :], bq[:, :], SPLIT * DH ** -0.5, None, ALU.mult).then_inc(w_ready, 1)
                dve.tensor_scalar(wo[:, :], wo[:, :], gate, None, ALU.mult).then_inc(w_ready, 1)
                dve.wait_ge(w_ready, 4)
                dve.wait_ge(q_clear, 2)
                dve.wait_ge(v_clear, 2)

                def prepare(nb, buf, j, f, bank):
                    dve.wait_ge(filled, f + 1)
                    if j < NG:
                        dve.wait_ge(qa_ready, 2 * (NG * nb + j) + 2)
                        for i in range(GH):
                            r = slice(QD * i, QD * (i + 1))
                            h = column(i, j)
                            dve.scalar_tensor_tensor(q16[r, buf, h:h + S], q_h[r, :], lows[r, 1:2],
                                                     qa[r, :], ALU.mult, ALU.add).then_inc(q_parts, 1)
                        dve.sem_inc(freed, 1)
                    elif j < NG + NG * NC:
                        g, c = divmod(j - NG, NC)
                        c0, w = KCHUNK[c]
                        dve.wait_ge(kh_ready, NG * NC * nb + j - NG + 1)
                        dve.scalar_tensor_tensor(k16[:, buf, g, c0:c0 + w], kh[:, bank, 0:w], lows[:, 0:1],
                                                 helper[:, bank, 0:w], ALU.mult, ALU.add).then_inc(freed, 1)
                    else:
                        t0 = VT * (j - NG - NG * NC)
                        n = min(VT, KT - t0)
                        k = keys(t0 + n - 1)
                        assert n == 1 or k == P
                        dve.tensor_copy(vall[0:k, buf, t0:t0 + n, :].rearrange("p t v -> p (t v)"),
                                        helper[0:k, bank, 0:n * H * VD]).then_inc(freed, 1)
                        if j == PREP - 1:
                            dve.wait_ge(freed, f + 1)
                            dve.wait_ge(q_parts, GH * NG * (nb + 1) + 1)
                            dve.sem_inc(prepared, 1)

                def maximum(p, k, f, bank):
                    w = CHUNK[k % NC][1]
                    dve.wait_ge(filled, f + 1)
                    dve.tensor_reduce(mx[:, bass.ds(MAXIMA * p + k, 1)], helper[:, bank, 0:w], AX_X,
                                      ALU.max).then_inc(freed, 1)

                def gather_mu(nb, f):
                    dve.wait_ge(freed, f)
                    v = mx[:, :].rearrange("p (g i q c) -> p i g q c", g=NG, i=GH, q=TB)
                    for i in range(GH):
                        ins = dve.tensor_reduce(mu[:, 2 * NG * i:2 * NG * (i + 1)].rearrange("p (g q) -> p g q", g=NG),
                                                v[:, i], AX_X, ALU.max)
                    ins.then_inc(mu_ready, 1)

                def keep_shift(nb, f, bank):
                    dve.wait_ge(filled, f + 1)
                    if not (isinstance(nb, int) and nb == 0):
                        dve.wait_ge(shift_in, 16 * GH * nb)
                    dve.tensor_scalar(shift[:, :], helper[0:UNITS, bank, 0:P], -1.0 / SPLIT, None,
                                      ALU.mult).then_inc(freed, 1)

                def keep_out(b, p, f, bank):
                    for i in range(TB):
                        dve.wait_ge(filled, f + i + 1)
                        dve.tensor_copy(att[:, i].rearrange("p h v -> p (h v)")[:, bass.ds(2 * VD * p, 2 * VD)],
                                        helper[:, (bank + i) % NRING, 0:2 * VD]).then_inc(freed, 1)

                def normalise(b, f):
                    dve.wait_ge(freed, f)
                    dve.reciprocal(rec[:, :, :], att[:, :, :, DH]).then_inc(out_step, 1)
                    dve.wait_ge(out_step, 2 * b + 1)
                    for i in range(TB):
                        ins = dve.tensor_tensor(attn[:, i, :].rearrange("p (h v) -> p h v", h=H), att[:, i, :, 0:DH],
                                                rec[:, i, :, None].to_broadcast([P, H, DH]), ALU.mult)
                    ins.then_inc(attn_ready, 1)

                def keep_attnT(b, f, bank):
                    dve.wait_ge(filled, f + 1)
                    dve.tensor_copy(attnT[:, :], helper[:, bank, 0:TB * P]).then_inc(freed, 1)
                    dve.wait_ge(freed, f + 1)
                    dve.sem_inc(attnT_ready, 1)

                def add_out(b, f, bank):
                    dve.wait_ge(filled, f + 1)
                    for i in range(TB):
                        xt = x[:, TB * b + i, :]
                        ins = dve.tensor_tensor(xt, xt, helper[:, bank, i * P:(i + 1) * P], ALU.add)
                        ins.then_inc(out_step if i == 0 else freed, 1)

                def batch(b, buf, prepares):
                    def pair(p, par, kind, _):
                        f, bank = start_fill(b, p, kind, buf)
                        before = pair_before(b, p)
                        k = 0
                        for t in range(KT):
                            for i in prep_items(kind, t):
                                prepare(b + 1, 1 - buf, i, f + k, (bank + k) % NRING)
                                k += 1
                            for i in maxima(kind, t):
                                maximum(p, i, f + k, (bank + k) % NRING)
                                k += 1
                            if t == 2 and before:
                                keep_out(*before, f + k, (bank + k) % NRING)
                                k += TB
                                if is_p(p, 0):
                                    normalise(b - 1, f + k)
                            if t in (5, 7) and before and is_p(p, 0):
                                (keep_attnT if t == 5 else add_out)(b - 1, f + k, (bank + k) % NRING)
                                k += 1
                            if kind == "last" and t == 8:
                                gather_mu(b + 1, f + k)
                            if kind == "last" and t == 9:
                                keep_shift(b + 1, f + k, (bank + k) % NRING)
                                k += 1
                        if kind == "idle" and is_p(p, NP - 1):
                            keep_out(b, p, f + k, (bank + k) % NRING)
                            k += TB
                            normalise(b, f + k)
                            keep_attnT(b, f + k, (bank + k) % NRING)
                            add_out(b, f + k + 1, (bank + k + 1) % NRING)
                    over_pairs(dve, pair, prepares)

                for j in range(PREP):
                    prepare(0, 0, j, j, j % NRING)
                for n in range(NP * MAXIMA // 2):
                    half = 2 * (n % 2)
                    dve.wait_ge(max_filled, n + 1)
                    dve.tensor_reduce(mx[:, 2 * n:2 * n + 2], banks[:, half:half + 2, 0:CHUNK[0][1]], AX_X,
                                      ALU.max).then_inc(max_freed, 1)
                dve.wait_ge(max_freed, NP * MAXIMA // 2 + 2)
                gather_mu(0, FIRST - 1)
                keep_shift(0, FIRST - 1, (FIRST - 1) % NRING)
                over_batches(dve, batch)


def narrow_layouts(n, a):
    import numpy as np
    f = np.float32
    wq = n["L1_xattn_Wq"].reshape(NG, GH, DH, D)
    bq = n["L1_xattn_bq"].reshape(NG, GH, DH)
    wkv = np.concatenate([n["L1_xattn_Wkv"], n["L1_xattn_bkv"][:, None]], 1).reshape(H, 2, DH, C1)
    wk = wkv[:, 0].reshape(NG, GH, DH, C1)
    q = np.zeros((D, NG, GH, QD), f)
    qb = np.zeros((GH, QD, NG), f)
    k = np.zeros((C1, NG, GH, QD), f)
    lows = np.zeros((GH, QD, 2), f)
    for r in range(3):
        part = slice(r * DH, (r + 1) * DH)
        q[..., part] = wq.transpose(3, 0, 1, 2)
        qb[:, part] = bq.transpose(1, 2, 0)
        k[..., part] = wk.transpose(3, 0, 1, 2)
    k[C, :, :, 3 * DH] = 1.0
    lows[:, DH:2 * DH, 0] = -1.0
    lows[:, 2 * DH:3 * DH, 1] = -1.0
    v = np.zeros((C1, H, VD), f)
    v[..., 0:DH] = wkv[:, 1].transpose(2, 0, 1)
    v[C, :, DH] = 1.0
    fold = np.zeros((2, 2, QD, 2, VD), f)
    for j in range(2):
        fold[:, j, 0:VD, j, :] = np.eye(VD, dtype=f)
    a["n_wq"] = q.reshape(D, NG, P)
    a["n_bq"] = qb.reshape(P, NG)
    a["n_wk"] = k.reshape(C1, NG, P)
    a["n_wv"] = v.reshape(C1, H * VD)
    a["n_wo"] = n["L1_xattn_Wo"].T
    a["n_lows"] = lows.reshape(P, 2)
    a["n_fold"] = fold.reshape(P, 2 * VD)


NE, HRT, HSH, TAU = 12, 384, 256, 1.5
RC, SC = HRT // P, HSH // P
BLK = 512
NBLK = NB * S // BLK
BT = BLK // P


def experts(nc, A, x, xnT, bias, gate, ident):
    CHUNKS = SC + NE * RC
    with ExitStack() as ctx:
        m = Pool_(nc, ctx, "ex")
        w1 = m.sb("w1", [D, NE, 2 * HRT])
        w2 = m.sb("w2", [P, NE, RC, D])
        ws1 = m.sb("ws1", [D, 2 * HSH])
        ws2 = m.sb("ws2", [P, SC, D])
        b1 = m.sb("b1", [P, NE, 2 * RC])
        bs1 = m.sb("bs1", [P, 2 * SC])
        b2 = m.sb("b2", [NE, D])
        wr = m.sb("wr", [D, NE])
        br = m.sb("br", [P, NE])
        tri = m.sb("tri", [P, NE, NE])
        L = m.sb("logits", [P, NT, NE])
        gt = m.sb("larger", [P, NT, NE, NE])
        eq = m.sb("ties", [P, NT, NE, NE])
        rank = m.sb("rank", [P, NT, NE])
        top = m.sb("top", [P, NT])
        ex = m.sb("ex", [P, NT, NE])
        den = m.sb("den", [P, NT])
        wgt = m.sb("weight", [P, NT, NE])
        wgt_g = m.sb("gated_weight", [P, NT, NE])
        wT = m.sb("wT", [NE, NT * P])
        wTb = m.sb("wT_block", [NE, BLK])
        gl = m.sb("gelu", [P, 2, BLK])
        hidden = m.sb("hidden", [P, 2, RC, BLK])
        pa = m.ps("a", [P, 2, BLK])
        pg = m.ps("g", [P, 2, BLK])
        py = m.ps("y", [P, 2, BT, D])
        pr = m.ps("route", [P, 2, 512])

        small_in = m.sem("small_in")
        w_in = [m.sem(f"w_in{e}") for e in range(NE + 1)]
        tri_ready = m.sem("tri_ready")
        own = m.sem("own")
        logits_full = m.sem("logits_full")
        shifted = m.sem("shifted")
        ex_done = m.sem("ex_done")
        wgt_ready = m.sem("wgt_ready")
        wT_full = m.sem("wT_full")
        wT_kept = m.sem("wT_kept")
        wTb_ready = m.sem("wTb_ready")
        up_full = m.sem("up_full")
        gelu_done = m.sem("gelu_done")
        up_kept = m.sem("up_kept")
        y_full = m.sem("y_full")
        y_kept = m.sem("y_kept")

        def chunks(e):
            return SC if e == 0 else RC

        def chunk_index(e):
            return 0 if e == 0 else SC + RC * (e - 1)

        with nc.Block() as block:
            @block.sync
            def _(sp):
                for sb_, name in ((wr, "e_wr"), (br, "e_br"), (b2, "e_b2"), (b1, "e_b1"), (bs1, "e_bs1")):
                    sp.dma_start(sb_[:], A[name]).then_inc(small_in, 16)
                sp.dma_start(ws1[:, :], A["e_ws1"]).then_inc(w_in[0], 16)
                sp.dma_start(ws2[:, :, :], A["e_ws2"]).then_inc(w_in[0], 16)
                for e in range(NE):
                    sp.dma_start(w1[:, e, :], A["e_w1"][:, e, :]).then_inc(w_in[e + 1], 16)
                    sp.dma_start(w2[:, e, :, :], A["e_w2"][:, e, :, :]).then_inc(w_in[e + 1], 16)

            @block.gpsimd
            def _(pool):
                pool.memset(tri[:, :, :], 1.0).then_inc(tri_ready, 1)
                pool.wait_ge(tri_ready, 1)
                pool.affine_select(out=tri[:, :, :], in_=tri[:, :, :], compare_op=ALU.is_gt, fill=0.0, base=0,
                                   pattern=[[1, NE], [-1, NE]], channel_multiplier=0).then_inc(tri_ready, 1)
                pool.wait_ge(wT_kept, NT // 4)
                with pool.Fori(0, NBLK) as tb:
                    pool.wait_ge(wT_kept, NT // 4)
                    pool.wait_ge(y_full, tb * (NE + 1) + 1)
                    pool.tensor_copy(wTb[:, :], wT[:, bass.ds(tb * BLK, BLK)]).then_inc(wTb_ready, 1)

            @block.tensor
            def _(pe):
                def up(tb, e):
                    for c in range(chunks(e)):
                        k = chunk_index(e) + c
                        pe.wait_ge(up_kept, tb * CHUNKS + k + 1)
                        if c == 0 and isinstance(tb, int) and tb == 0:
                            pe.wait_ge(w_in[e], 32)
                        for bank, half in ((pa, 0), (pg, 1)):
                            if e == 0:
                                w = ws1[:, half * HSH + c * P:half * HSH + (c + 1) * P]
                            else:
                                w = w1[:, e - 1, half * HRT + c * P:half * HRT + (c + 1) * P]
                            ins = pe.matmul(bank[:, k % 2, :], w, xnT[:, bass.ds(tb * BLK, BLK)],
                                            start=True, stop=True)
                        ins.then_inc(up_full, 1)

                def down(tb, e):
                    n = tb * (NE + 1) + e
                    pe.wait_ge(up_kept, 2 + tb * CHUNKS + chunk_index(e) + chunks(e))
                    pe.wait_ge(y_kept, n + 2 if e == 0 else n + 1)
                    if e == 0:
                        pe.wait_ge(wTb_ready, tb + 1)
                    for t in range(BT):
                        if e == 0:
                            pe.matmul(py[:, 0, t, :], wTb[:, t * P:(t + 1) * P], b2[:, :], start=True, stop=False)
                        for c in range(chunks(e)):
                            w = ws2[:, c, :] if e == 0 else w2[:, e - 1, c, :]
                            ins = pe.matmul(py[:, e % 2, t, :], hidden[:, e % 2, c, t * P:(t + 1) * P], w,
                                            start=(c == 0 and e > 0), stop=(c == chunks(e) - 1))
                    ins.then_inc(y_full, 1)

                def token_block(tb):
                    for e in range(NE + 2):
                        if e <= NE:
                            up(tb, e)
                        if e >= 1:
                            down(tb, e - 1)

                pe.wait_ge(small_in, 16 * 5)
                for t in range(NT):
                    ins = pe.matmul(pr[:, 0, t * NE:(t + 1) * NE], xnT[:, t * P:(t + 1) * P], wr[:, :],
                                    start=True, stop=True)
                ins.then_inc(logits_full, 1)
                pe.wait_ge(wgt_ready, 1)
                for t in range(NT):
                    if t % 4 == 0 and t >= 8:
                        pe.wait_ge(wT_kept, t // 4 - 1)
                    ins = pe.transpose(pr[0:NE, t // 4 % 2, t % 4 * P:(t % 4 + 1) * P], wgt[:, t, :], ident[:, :])
                    if t % 4 == 3:
                        ins.then_inc(wT_full, 1)
                token_block(0)
                with pe.Fori(1, NBLK) as tb:
                    token_block(tb)

            @block.scalar
            def _(act):
                act.wait_ge(shifted, 1)
                act.activation(ex[:, :, :], ex[:, :, :], ACT.Exp).then_inc(ex_done, 1)
                for q in range(NT // 4):
                    act.wait_ge(wT_full, q + 1)
                    act.activation(wT[:, 4 * q * P:4 * (q + 1) * P], pr[0:NE, q % 2, :], ACT.Copy).then_inc(wT_kept, 1)
                with act.Fori(0, NBLK) as tb:
                    for e in range(NE + 1):
                        for c in range(chunks(e)):
                            k = chunk_index(e) + c
                            act.wait_ge(up_full, tb * CHUNKS + k + 1)
                            act.wait_ge(up_kept, tb * CHUNKS + k + 1)
                            b = bs1[:, SC + c:SC + c + 1] if e == 0 else b1[:, e - 1, RC + c:RC + c + 1]
                            act.activation(gl[:, k % 2, :], pg[:, k % 2, :], ACT.Gelu, bias=b).then_inc(gelu_done, 1)

            @block.vector
            def _(dve):
                c = Chain(dve, own)
                dve.sem_inc(up_kept, 2)
                dve.sem_inc(y_kept, 2)
                dve.sem_inc(y_full, 2)
                dve.tensor_tensor(x[:, :, :], x[:, :, :], bias[:, None, :].to_broadcast([P, NT, D]), ALU.add)
                dve.wait_ge(small_in, 16 * 5)
                dve.wait_ge(tri_ready, 2)
                dve.wait_ge(logits_full, 1)
                c.step(dve.tensor_tensor(L[:, :, :], pr[:, 0, 0:NT * NE].rearrange("p (t e) -> p t e", t=NT),
                                         br[:, None, :].to_broadcast([P, NT, NE]), ALU.add))
                c.step(dve.tensor_scalar(L[:, :, :], L[:, :, :], 1.0 / TAU, None, ALU.mult))
                other = L[:, :, None, :].to_broadcast([P, NT, NE, NE])
                mine = L[:, :, :, None].to_broadcast([P, NT, NE, NE])
                c.step(dve.tensor_tensor(gt[:, :, :, :], other, mine, ALU.is_gt))
                c.step(dve.tensor_tensor(eq[:, :, :, :], other, mine, ALU.is_equal))
                for t in range(NT):
                    ins = dve.tensor_tensor(eq[:, t, :, :], eq[:, t, :, :], tri[:, :, :], ALU.mult)
                c.step(ins)
                c.step(dve.tensor_tensor(gt[:, :, :, :], gt[:, :, :, :], eq[:, :, :, :], ALU.add))
                c.step(dve.tensor_reduce(rank[:, :, :], gt[:, :, :, :], AX_X, ALU.add))
                c.step(dve.tensor_reduce(top[:, :], L[:, :, :], AX_X, ALU.max))
                dve.tensor_tensor(ex[:, :, :], L[:, :, :], top[:, :, None].to_broadcast([P, NT, NE]),
                                  ALU.subtract).then_inc(shifted, 1)
                c.step(dve.tensor_scalar(rank[:, :, :], rank[:, :, :], 2.0, None, ALU.is_lt))
                dve.wait_ge(ex_done, 1)
                c.step(dve.tensor_tensor(ex[:, :, :], ex[:, :, :], rank[:, :, :], ALU.mult))
                c.step(dve.tensor_reduce(den[:, :], ex[:, :, :], AX_X, ALU.add))
                c.step(dve.reciprocal(den[:, :], den[:, :]))
                dve.tensor_tensor(wgt[:, :, :], ex[:, :, :], den[:, :, None].to_broadcast([P, NT, NE]),
                                  ALU.mult).then_inc(wgt_ready, 1)
                dve.wait_ge(wgt_ready, 1)
                c.step(dve.tensor_scalar(wgt_g[:, :, :], wgt[:, :, :], gate, None, ALU.mult))

                def hide(tb, e):
                    n = tb * (NE + 1) + e
                    dve.wait_ge(y_full, n + 2 if e == 0 else n if e == 1 else n + 1)
                    for c in range(chunks(e)):
                        k = chunk_index(e) + c
                        dve.wait_ge(gelu_done, tb * CHUNKS + k + 1)
                        b = bs1[:, c:c + 1] if e == 0 else b1[:, e - 1, c:c + 1]
                        dve.scalar_tensor_tensor(hidden[:, e % 2, c, :], pa[:, k % 2, :], b, gl[:, k % 2, :],
                                                 ALU.add, ALU.mult).then_inc(up_kept, 1)

                def add(tb, e):
                    n = tb * (NE + 1) + e
                    dve.wait_ge(y_full, n + 3)
                    dve.wait_ge(y_kept, n + 2)
                    for t in range(BT):
                        xt = x[:, tb * BT + t, :]
                        w = gate if e == 0 else wgt_g[:, bass.ds(tb * BT + t, 1), e - 1]
                        ins = dve.scalar_tensor_tensor(xt, py[:, e % 2, t, :], w, xt, ALU.mult, ALU.add)
                    ins.then_inc(y_kept, 1)

                with dve.Fori(0, NBLK) as tb:
                    for e in range(NE + 2):
                        if e <= NE:
                            hide(tb, e)
                        if e >= 1:
                            add(tb, e - 1)


def expert_layouts(n, a):
    import numpy as np
    a["e_w1"] = n["L1_ffn_We1"].transpose(1, 0, 2)
    a["e_w2"] = n["L1_ffn_We2"].reshape(NE, RC, P, D).transpose(2, 0, 1, 3)
    a["e_ws1"] = n["L1_ffn_Ws1"]
    a["e_ws2"] = n["L1_ffn_Ws2"].reshape(SC, P, D).transpose(1, 0, 2)
    a["e_b1"] = n["L1_ffn_be1"].reshape(NE, 2 * RC, P).transpose(2, 0, 1)
    a["e_bs1"] = n["L1_ffn_bs1"].reshape(2 * SC, P).T
    a["e_b2"] = n["L1_ffn_be2"]
    a["e_wr"] = n["L1_ffn_Wr"]
    a["e_br"] = np.tile(n["L1_ffn_br"].reshape(1, NE), (P, 1))


def setup(nc, A, x, ident, gate, rowvec, ROWVECS):
    with ExitStack() as ctx:
        m = Pool_(nc, ctx, "su")
        raw = m.sb("raw_gate", [P, 4])
        x_in = m.sem("x_in")
        gate_in = m.sem("gate_in")
        zeroed = m.sem("zeroed")
        gate_ready = m.sem("gate_ready")
        with nc.Block() as block:
            @block.sync
            def _(sp):
                sp.dma_start(raw[:, :], A["gates"]).then_inc(gate_in, 16)
                sp.dma_start(rowvec[:, :, :], A["rowvecs"]).then_inc(gate_in, 16)
                sp.dma_start(x[:, :, :], A["x"]).then_inc(x_in, 16)
                sp.wait_ge(x_in, 16)

            @block.gpsimd
            def _(pool):
                pool.memset(ident[:, :], 0.0).then_inc(zeroed, 1)
                pool.wait_ge(zeroed, 1)
                pool.affine_select(out=ident[:, :], in_=ident[:, :], compare_op=ALU.not_equal, fill=1.0,
                                   base=0, pattern=[[-1, P]], channel_multiplier=1)

            @block.scalar
            def _(act):
                act.wait_ge(gate_in, 32)
                act.activation(gate[:, :], raw[:, :], ACT.Tanh).then_inc(gate_ready, 1)

            @block.vector
            def _(dve):
                dve.wait_ge(gate_ready, 1)
                for i, g in enumerate(ROWVECS):
                    if g is not None:
                        dve.tensor_scalar(rowvec[:, i, :], rowvec[:, i, :], gate[:, g:g + 1], None, ALU.mult)


def store(nc, x, out):
    with nc.semaphore("stored") as stored, nc.Block() as block:
        @block.sync
        def _(sp):
            sp.dma_start(out, x[:, :, :]).then_inc(stored, 16)
            sp.wait_ge(stored, 16)


G_XATTN0, G_XATTN1, G_FFN0, G_FFN1 = range(4)
ROWVECS = [G_XATTN0, G_FFN0, G_XATTN1, G_FFN1]


def build(nc, A, out, stages=5, start=0):
    with ExitStack() as ctx:
        m = Pool_(nc, ctx, "all")
        x = m.sb("x", [P, NT, D])
        xn = m.sb("xn", [P, NT, D])
        xnT = m.sb("xnT", [D, NT * P])
        ident = m.sb("ident", [P, P])
        gate = m.sb("gate", [P, 4])
        rowvec = m.sb("rowvec", [P, len(ROWVECS), D])
        setup(nc, A, x, ident, gate, rowvec, ROWVECS)
        if stages >= 1 > start:
            with ExitStack() as own:
                w = Pool_(nc, own, "w")
                wide_M = w.sb("M", [D, H, C])
                wide_VO = w.sb("VO", [C1, H, D + 1])
                wide_setup(nc, A, wide_M, wide_VO, gate[:, G_XATTN0:G_XATTN0 + 1])
                layernorm(nc, "ln0", x, xn, xnT, ident)
                wide_attention(nc, A, x, xnT, wide_M, wide_VO, rowvec[:, 0, :], ident)
        if stages >= 2 > start:
            layernorm(nc, "ln1", x, xn, xnT, ident)
            routed_attention(nc, A, x, xn, xnT, rowvec[:, 1, :], gate[:, G_FFN0:G_FFN0 + 1], ident)
        if stages >= 3 > start:
            layernorm(nc, "ln2", x, xn, xnT, ident)
            narrow_attention(nc, A, x, xnT, rowvec[:, 2, :], gate[:, G_XATTN1:G_XATTN1 + 1], ident)
        if stages >= 4 > start:
            layernorm(nc, "ln3", x, xn, xnT, ident)
            experts(nc, A, x, xnT, rowvec[:, 3, :], gate[:, G_FFN1:G_FFN1 + 1], ident)
        store(nc, x, out)


def laid_out(i):
    import numpy as np
    f = np.float32
    B, T_, C_ = i["ctx_768"].shape
    ctx = np.asarray(i["ctx_768"])
    ctx1 = np.concatenate([ctx, np.ones((B, T_, 1), f)], 2)
    padded = np.concatenate([ctx1, np.zeros((B, KT * P - T_, C1), f)], 1)
    tile = lambda v: np.tile(np.asarray(v).reshape(1, -1), (P, 1))
    gx, gf = np.asarray(i["g_xattn"]), np.asarray(i["g_ffn"])
    a = {
        "x": np.asarray(i["x"]).reshape(NT, P, D).transpose(1, 0, 2),
        "ctxT": ctx1.transpose(0, 2, 1),
        "ctx_rows": padded.reshape(B, KT, P, C1).transpose(0, 2, 1, 3),
        "gates": tile(np.concatenate([gx, gf])),
        "rowvecs": np.stack([tile(i["L0_xattn_bo"]), tile(i["L0_ffn_null_token"]),
                             tile(i["L1_xattn_bo"]), tile(i["L1_ffn_bs2"])], 1),
        "a_wq": np.asarray(i["L0_xattn_Wq"]).reshape(D, H, E0).transpose(2, 1, 0),
        "a_wk": np.asarray(i["L0_xattn_Wk"]).reshape(C, H, E0).transpose(2, 1, 0),
        "a_wv": np.asarray(i["L0_xattn_Wv"]).reshape(C, H, E0).transpose(2, 1, 0),
        "a_wo": np.asarray(i["L0_xattn_Wo"]).reshape(H, E0, D).transpose(1, 0, 2),
    }
    n = {k: np.asarray(v) for k, v in i.items()}
    for layouts in (routed_layouts, narrow_layouts, expert_layouts):
        layouts(n, a)
    return {k: np.ascontiguousarray(v) for k, v in a.items()}


def kernel(**inputs):
    import numpy as np
    import concourse.bacc as bacc
    from concourse.bass_utils import run_bass_kernel_spmd

    nc = bacc.Bacc("TRN2", target_bir_lowering=False, num_devices=1)
    arrays = laid_out(inputs)
    A = {k: nc.dram_tensor(k, v.shape, F32, kind="ExternalInput").ap() for k, v in arrays.items()}
    out = nc.dram_tensor("out", (P, NT, D), F32, kind="ExternalOutput").ap()
    build(nc, A, out)
    r = run_bass_kernel_spmd(nc, [arrays], core_ids=[0])
    y = r.results[0]["out"]
    return np.ascontiguousarray(y.transpose(1, 0, 2).reshape(NB, S, D))
```

```python
import math
from contextlib import ExitStack

import concourse.bass as bass
from concourse import mybir

P = 128
F32 = mybir.dt.float32
F16 = mybir.dt.float16
ALU = mybir.AluOpType
ACT = mybir.ActivationFunctionType
AX_X = mybir.AxisListType.X

NB, S, D = 8, 256, 128
NT = NB * S // P
TB = S // P
C, T = 96, 1601
C1 = C + 1
H = 16
NP = H // 2
KT = (T + P - 1) // P
KLAST = T - (KT - 1) * P
E0 = 64
EPS = 1e-5
SPLIT = 64.0
UNSPLIT = 1.0 / (SPLIT * SPLIT)
CHUNK = [(400 * i, T - 1200) for i in range(4)]
NC = len(CHUNK)
UNITS = H * TB


def keys(t):
    return P if t < KT - 1 else KLAST


class Chain:

    def __init__(self, eng, sem, base=0):
        self.eng, self.sem, self.base, self.n = eng, sem, base, 0

    def step(self, ins):
        ins.then_inc(self.sem, 1)
        self.n += 1
        self.eng.wait_ge(self.sem, self.base + self.n)


class Stage:

    def __init__(self, nc, ctx, tag):
        self.nc, self.ctx, self.tag = nc, ctx, tag

    def sb(self, name, shape, dt=F32):
        return self.ctx.enter_context(self.nc.sbuf_tensor(f"{self.tag}_{name}", shape, dt))

    def ps(self, name, shape, dt=F32):
        return self.ctx.enter_context(self.nc.psum_tensor(f"{self.tag}_{name}", shape, dt))

    def sem(self, name):
        return self.ctx.enter_context(self.nc.semaphore(f"{self.tag}_{name}"))


class Weights:

    def __init__(self, nc, ctx, A, tag, shapes):
        m = Stage(nc, ctx, tag)
        self.A = A
        self.buf = {name: m.sb(name, shape) for name, shape in shapes.items()}
        self.arrived = m.sem("arrived")
        self.all = 16 * len(shapes)

    def load(self, sp):
        for name, buf in self.buf.items():
            sp.dma_start(buf[:], self.A[name]).then_inc(self.arrived, 16)


def layernorm(nc, tag, x, xn, xnT, ident, *weights, folding=None):
    with ExitStack() as ctx:
        m = Stage(nc, ctx, tag)
        stats = m.sb("stats", [P, NT, 6])
        mv = m.sb("mv", [P, NT, 2])
        var = m.sb("var", [P, NT])
        std = m.sb("std", [P, NT])
        r = m.sb("r", [P, NT])
        e = m.sb("e", [P, NT])
        pt = m.ps("pt", [P, 4, 4 * P])
        own = m.sem("own")
        var_ready = m.sem("var_ready")
        std_ready = m.sem("std_ready")
        xn_ready = m.sem("xn_ready")
        turned = m.sem("turned")
        xnt_ready = m.sem("xnt_ready")
        stat_ready = m.sem("stat_ready")
        with nc.Block() as block:
            @block.sync
            def _(sp):
                for w in weights:
                    w.load(sp)

            @block.vector
            def _(dve):
                for t in range(NT):
                    dve.bn_stats(stats[:, t, :], x[:, t, :]).then_inc(stat_ready, 1)
                for t in range(NT):
                    dve.wait_ge(stat_ready, t + 1)
                    dve.bn_aggr(mv[:, t, :], stats[:, t, :]).then_inc(stat_ready, 1)
                dve.wait_ge(stat_ready, 2 * NT)
                dve.tensor_scalar(var[:, :], mv[:, :, 1], EPS, None, ALU.add).then_inc(var_ready, 1)
                dve.wait_ge(std_ready, 1)
                c = Chain(dve, own)
                c.step(dve.reciprocal(r[:, :], std[:, :]))
                c.step(dve.tensor_tensor(e[:, :], r[:, :], r[:, :], ALU.mult))
                c.step(dve.tensor_tensor(e[:, :], e[:, :], var[:, :], ALU.mult))
                c.step(dve.tensor_scalar(e[:, :], e[:, :], -0.5, 1.5, ALU.mult, ALU.add))
                c.step(dve.tensor_tensor(r[:, :], r[:, :], e[:, :], ALU.mult))
                for t in range(NT):
                    dve.tensor_scalar(xn[:, t, :], x[:, t, :], mv[:, t, 0:1], r[:, t:t + 1],
                                      ALU.subtract, ALU.mult).then_inc(xn_ready, 1)
                if folding:
                    folding.keep(dve)

            @block.tensor
            def _(pe):
                if folding:
                    folding.multiply(pe, range(0, 2))
                for t in range(NT):
                    pe.wait_ge(xn_ready, t + 1)
                    pe.transpose(pt[:, t // 4, (t % 4) * P:(t % 4 + 1) * P], xn[:, t, :],
                                 ident[:, :]).then_inc(turned, 1)
                if folding:
                    folding.multiply(pe, range(2, H // folding.HEADS))

            @block.scalar
            def _(act):
                act.wait_ge(var_ready, 1)
                act.activation(std[:, :], var[:, :], ACT.Sqrt).then_inc(std_ready, 1)
                for g in range(NT // 4):
                    act.wait_ge(turned, 4 * g + 4)
                    act.activation(xnT[:, 4 * g * P:4 * (g + 1) * P], pt[:, g, :],
                                   ACT.Copy).then_inc(xnt_ready, 1)


class Folding:
    HEADS = 4

    def __init__(self, nc, ctx, A, M, VO, gate):
        self.weights = Weights(nc, ctx, A, "fo", {
            "a_wq": [E0, H, D], "a_wk": [E0, H, C], "a_wv": [E0, H, C], "a_wo": [E0, H, D]})
        m = Stage(nc, ctx, "fo")
        self.M, self.VO, self.gate = M, VO, gate
        self.pm = m.ps("pm", [P, 2, self.HEADS, 128])
        self.pv = m.ps("pv", [P, 2, self.HEADS, 128])
        self.product = m.sem("product")
        self.kept = m.sem("kept")
        self.cleared = m.sem("cleared")

    def multiply(self, pe, turns):
        wq, wk, wv, wo = self.weights.buf.values()
        pe.wait_ge(self.weights.arrived, self.weights.all)
        for g in turns:
            if g >= 2:
                pe.wait_ge(self.kept, 2 * (g - 1))
            for j in range(self.HEADS):
                h = g * self.HEADS + j
                pe.matmul(self.pm[:, g % 2, j, 0:C], wq[:, h, :], wk[:, h, :], start=True, stop=True)
                ins = pe.matmul(self.pv[0:C, g % 2, j, :], wv[:, h, :], wo[:, h, :], start=True, stop=True)
            ins.then_inc(self.product, 1)

    def keep(self, dve):
        dve.memset(self.VO[:, :, :], 0.0).then_inc(self.cleared, 1)
        dve.wait_ge(self.cleared, 1)
        dve.memset(self.VO[C:C1, :, D:D + 1], 1.0)
        for g in range(H // self.HEADS):
            heads = slice(g * self.HEADS, (g + 1) * self.HEADS)
            dve.wait_ge(self.product, g + 1)
            dve.tensor_scalar(self.M[:, heads, :], self.pm[:, g % 2, :, 0:C],
                              SPLIT * E0 ** -0.5, None, ALU.mult).then_inc(self.kept, 1)
            dve.tensor_scalar(self.VO[0:C, heads, 0:D], self.pv[0:C, g % 2, :, :],
                              self.gate[0:C, 0:1], None, ALU.mult).then_inc(self.kept, 1)


RING = 3
PRING = 4
WRING = 2
LIFT = 10 * math.log(2.0)
PAIR = 2 * S

OUT_SLOTS = (2, 3)


def score_slot(t, par):
    return (t + par) % RING


def scores_ago(t, par):
    if par == 1 or t >= RING:
        return RING
    return next(d for d in range(t + 1, KT) if score_slot(KT + t - d, 1) == score_slot(t, 0))


def prob_slot(t, ring=PRING):
    return t % ring if t < KT - 1 else ring


def since_last(t, ring):
    if t == KT - 1:
        return KT
    return ring if t >= ring else ring + 1


def over_batches(eng, batch):
    batch(0, 0, True)
    with eng.Fori(0, NB // 2 - 1) as i:
        batch(2 * i + 1, 1, True)
        batch(2 * i + 2, 0, True)
    batch(NB - 1, 1, False)


def pair_before(b, p):
    if isinstance(p, int) and p == 0:
        return None if isinstance(b, int) and b == 0 else (b - 1, NP - 1)
    return b, p - 1


def over_pairs(eng, pair, prepares):
    first, middle, last = ("first", "middle", "last") if prepares else ("idle",) * 3
    pair(0, 0, first, 0)
    with eng.Fori(0, NP // 2 - 1) as i:
        pair(2 * i + 1, 1, middle, i)
        pair(2 * i + 2, 0, middle, i + 1)
    pair(NP - 1, 1, last, NP // 2 - 1)


def wide_attention(nc, A, x, xnT, wide_M, wide_VO, bias, ident, *weights):
    MAXIMA = 2 * TB * NC
    LAST_PER_SLOT = 2
    MU_SLOT = -(-MAXIMA // LAST_PER_SLOT)
    FIRST = NP + 1
    BATCH = NP + NP * MAXIMA + 1 + TB * NP
    with ExitStack() as ctx:
        m = Stage(nc, ctx, "wa")
        ctxT = m.sb("ctxT", [C1, T])
        ch = m.sb("ctx_hi", [C1, 2, T], F16)
        cl = m.sb("ctx_lo", [C1, 2, T], F16)
        rows = m.sb("ctx_rows", [P, KT, C1])
        rh = m.sb("rows_hi", [P, 2, KT, C1], F16)
        rl = m.sb("rows_lo", [P, 2, KT, C1], F16)
        qh = m.sb("q_hi", [C1, 2, H * S], F16)
        ql = m.sb("q_lo", [C1, 2, H * S], F16)
        prob = m.sb("prob", [P, WRING + 1, PAIR])
        prob_hi = m.sb("prob_hi", [P, PRING + 1, PAIR], F16)
        prob_lo = m.sb("prob_lo", [P, PRING + 1, PAIR], F16)
        lift = m.sb("lift", [P, 1])
        acc = m.sb("acc", [C1, 2, PAIR])
        mx = m.sb("mx", [P, UNITS * NC])
        mu = m.sb("mu", [P, UNITS])
        shift = m.sb("shift", [UNITS, P], F16)
        rec = m.sb("rec", [P, 2])
        banks = m.ps("banks", [P, 2 * RING, 512])
        scores = banks[:, 0:RING, :]
        helper = banks[:, RING:2 * RING, :]
        pacc = m.ps("pacc", [P, 2, PAIR])

        ctxT_in = m.sem("ctxT_in")
        rows_in = m.sem("rows_in")
        scaled = m.sem("scaled")
        hi_ready = m.sem("hi_ready")
        split = m.sem("split")
        rows_scaled = m.sem("rows_scaled")
        rows_split = m.sem("rows_split")
        lift_ready = m.sem("lift_ready")
        q_hi_ready = m.sem("q_hi_ready")
        filled = m.sem("helper_filled")
        freed = m.sem("helper_freed")
        max_filled = m.sem("max_filled")
        max_freed = m.sem("max_freed")
        mu_ready = m.sem("mu_ready")
        shift_in = m.sem("shift_in")
        scores_ready = m.sem("scores_ready")
        exp_done = m.sem("exp_done")
        lo_done = m.sem("prob_lo_done")
        pv_done = m.sem("pv_done")
        acc_ready = m.sem("acc_ready")
        x_step = m.sem("x_step")

        def maxima(kind, t):
            if kind == "first":
                n = KT - NP
                return range(MAXIMA * (t - NP) // n, MAXIMA * (t - NP + 1) // n) if t >= NP else range(0)
            if kind == "middle":
                return range(MAXIMA * t // KT, MAXIMA * (t + 1) // KT)
            return range(min(LAST_PER_SLOT * t, MAXIMA), min(LAST_PER_SLOT * (t + 1), MAXIMA)) if kind == "last" else range(0)

        def start_fill(b, p, kind):
            assert FIRST % RING == 0 and BATCH % RING == 0 and (MAXIMA + TB) % RING == 0
            if isinstance(p, int) and p == 0:
                carried = 0 if isinstance(b, int) and b == 0 else TB
                return FIRST + BATCH * b - carried, -carried % RING
            if kind == "idle":
                return FIRST + BATCH * b + TB * (p - 1), 0
            return FIRST + BATCH * b + NP + MAXIMA + (MAXIMA + TB) * (p - 1), (NP + MAXIMA) % RING

        with nc.Block() as block:
            @block.sync
            def _(sp):
                def load_T(b):
                    if b >= 1:
                        sp.wait_ge(split, b)
                    sp.dma_start(ctxT[:, :], A["ctxT"][b]).then_inc(ctxT_in, 16)

                def load_rows(b):
                    if b >= 1:
                        sp.wait_ge(rows_split, b)
                    sp.dma_start(rows[:, :, :], A["ctx_rows"][b]).then_inc(rows_in, 16)

                def put_shift(b):
                    n = FIRST if b == 0 else FIRST + BATCH * b - TB
                    sp.wait_ge(freed, n)
                    sp.dma_start(qh[C:C1, b % 2, :].rearrange("a (u q) -> a u q", u=UNITS),
                                 shift[:, :]).then_inc(shift_in, 16)

                load_T(0)
                load_rows(0)
                load_T(1)
                load_rows(1)
                for w in weights:
                    w.load(sp)
                put_shift(0)
                for b in range(1, NB):
                    if b + 1 < NB:
                        load_T(b + 1)
                    put_shift(b)
                    if b + 1 < NB:
                        load_rows(b + 1)

            @block.gpsimd
            def _(pool):
                def split_rows(b):
                    pool.wait_ge(rows_in, 16 * (b + 1))
                    pool.tensor_scalar(rows[:, :, :], rows[:, :, :], SPLIT, None, ALU.mult).then_inc(rows_scaled, 1)
                    if b >= 2:
                        pool.wait_ge(pv_done, KT + (b - 1) * NP * KT)
                    pool.wait_ge(rows_scaled, 2 * b + 1)
                    pool.tensor_copy(rh[:, b % 2], rows[:, :, :]).then_inc(rows_scaled, 1)
                    pool.wait_ge(rows_scaled, 2 * b + 2)
                    pool.tensor_tensor(rl[:, b % 2], rows[:, :, :], rh[:, b % 2],
                                       ALU.subtract).then_inc(rows_split, 1)

                pool.memset(lift[:, :], LIFT).then_inc(lift_ready, 1)
                split_rows(0)
                pool.tensor_tensor(x[:, :, :], x[:, :, :], bias[:, None, :].to_broadcast([P, NT, D]),
                                   ALU.add).then_inc(x_step, 1)
                for b in range(1, NB):
                    pool.wait_ge(ctxT_in, 16 * (b + 1))
                    pool.tensor_scalar(ctxT[:, :], ctxT[:, :], SPLIT, None, ALU.mult).then_inc(scaled, 1)
                    if b >= 2:
                        pool.wait_ge(scores_ready, (b - 1) * NP * KT)
                    pool.wait_ge(scaled, 2 * b - 1)
                    pool.tensor_copy(ch[:, b % 2, :], ctxT[:, :]).then_inc(scaled, 1)
                    pool.wait_ge(scaled, 2 * b)
                    pool.tensor_tensor(cl[:, b % 2, :], ctxT[:, :], ch[:, b % 2, :],
                                       ALU.subtract).then_inc(split, 1)
                    split_rows(b)

            @block.tensor
            def _(pe):
                def fill(f, alone=False):
                    if alone:
                        pe.wait_ge(freed, f)
                    elif not (isinstance(f, int) and f < RING):
                        pe.wait_ge(freed, f - RING + 1)

                def q_product(nb, j, f, bank):
                    fill(f)
                    for i in range(2):
                        ins = pe.matmul(helper[0:C, bank, i * S:(i + 1) * S], wide_M[:, 2 * j + i, :],
                                        xnT[:, bass.ds(nb * S, S)], start=True, stop=True)
                    ins.then_inc(filled, 1)

                def maximum(buf, p, k, f, bank):
                    c0, w = CHUNK[k % NC]
                    fill(f)
                    pe.matmul(helper[:, bank, 0:w], qh[0:C, buf, bass.ds((4 * p + k // NC) * P, P)],
                              ch[0:C, buf, c0:c0 + w], start=True, stop=True).then_inc(filled, 1)

                def turn_mu(nb, f, bank):
                    pe.wait_ge(mu_ready, nb + 1)
                    fill(f)
                    pe.transpose(helper[0:UNITS, bank, 0:P], mu[:, :], ident[:, :]).then_inc(filled, 1)

                def score(b, p, par, buf, t):
                    n = (b * NP + p) * KT + t
                    if t == 0 and isinstance(p, int) and p == 0:
                        pe.wait_ge(shift_in, 16 * b + 16)
                    pe.wait_ge(exp_done, KT + n - scores_ago(t, par) + 1)
                    out = scores[0:keys(t), score_slot(t, par), :]
                    kk = slice(t * P, t * P + keys(t))
                    qq = bass.ds(p * PAIR, PAIR)
                    pe.matmul(out, ch[:, buf, kk], qh[:, buf, qq], start=True, stop=False)
                    pe.matmul(out, ch[0:C, buf, kk], ql[0:C, buf, qq], start=False, stop=False)
                    pe.matmul(out, cl[0:C, buf, kk], qh[0:C, buf, qq],
                              start=False, stop=True).then_inc(scores_ready, 1)

                def project(b, p, par, i, f, bank, alone=False):
                    if i == 0:
                        pe.wait_ge(acc_ready, b * NP + p + 3)
                    fill(f, alone)
                    for j in range(2):
                        ins = pe.matmul(helper[:, bank, j * (D + 1):(j + 1) * (D + 1)],
                                        acc[:, par, j * S + i * P:j * S + (i + 1) * P],
                                        wide_VO[:, 2 * p + j, :], start=True, stop=True)
                    ins.then_inc(filled, 1)

                def batch(b, buf, prepares):
                    def pair(p, par, kind, _):
                        f, bank = start_fill(b, p, kind)
                        n = (b * NP + p) * KT
                        before = pair_before(b, p)
                        k = 0
                        for t in range(KT):
                            if t + 2 < KT:
                                score(b, p, par, buf, t + 2)
                            elif kind == "last":
                                score(b + 1, 0, 0, 1 - buf, t + 2 - KT)
                            elif not (isinstance(p, int) and p == NP - 1):
                                score(b, p + 1, 1 - par, buf, t + 2 - KT)
                            if kind == "first" and t < NP:
                                q_product(b + 1, t, f + k, (bank + k) % RING)
                                k += 1
                            for i in maxima(kind, t):
                                if i == 0:
                                    pe.wait_ge(q_hi_ready, NP * (b + 1) + p + 1)
                                if i == 0 and kind == "first":
                                    pe.wait_ge(split, b + 2)
                                maximum(1 - buf, p, i, f + k, (bank + k) % RING)
                                k += 1
                            if t in OUT_SLOTS and before:
                                project(*before, 1 - par, OUT_SLOTS.index(t), f + k, (bank + k) % RING,
                                        kind == "idle")
                                k += 1
                            if kind == "last" and t == MU_SLOT + 1:
                                turn_mu(b + 1, f + k, (bank + k) % RING)
                                k += 1
                            if t == 0:
                                pe.wait_ge(acc_ready, b * NP + p + 1)
                                if isinstance(p, int) and p == 0:
                                    pe.wait_ge(rows_split, b + 1)
                            pe.wait_ge(exp_done, KT + n + t + 1)
                            ks, slot = slice(0, keys(t)), prob_slot(t)
                            pe.matmul(pacc[0:C1, par, :], rh[ks, buf, t, :], prob_hi[ks, slot, :],
                                      start=(t == 0), stop=False)
                            pe.matmul(pacc[0:C1, par, :], rl[ks, buf, t, :], prob_hi[ks, slot, :],
                                      start=False, stop=False)
                            pe.wait_ge(lo_done, KT + n + t + 1)
                            pe.matmul(pacc[0:C1, par, :], rh[ks, buf, t, :], prob_lo[ks, slot, :],
                                      start=False, stop=(t == KT - 1)).then_inc(pv_done, 1)
                        if kind == "idle" and isinstance(p, int) and p == NP - 1:
                            for i in range(TB):
                                project(b, p, par, i, f + k + i, (bank + k + i) % RING, True)
                    over_pairs(pe, pair, prepares)

                pe.wait_ge(split, 1)
                for j in range(NP):
                    q_product(0, j, j, j % RING)
                pe.wait_ge(q_hi_ready, NP)
                pe.wait_ge(freed, NP)
                with pe.Fori(0, NP) as p:
                    for k in range(MAXIMA // 2):
                        half = 2 * (k % 2)
                        pe.wait_ge(max_freed, MAXIMA // 2 * p + k + 1)
                        for i in range(2):
                            c0, w = CHUNK[(2 * k + i) % NC]
                            ins = pe.matmul(banks[:, half + i, 0:w],
                                            qh[0:C, 0, bass.ds((4 * p + 2 * k // NC) * P, P)],
                                            ch[0:C, 0, c0:c0 + w], start=True, stop=True)
                        ins.then_inc(max_filled, 1)
                turn_mu(0, FIRST - 1, (FIRST - 1) % RING)
                for t in range(2):
                    score(0, 0, 0, 0, t)
                over_batches(pe, batch)

            @block.scalar
            def _(act):
                act.sem_inc(exp_done, KT)
                act.sem_inc(acc_ready, 2)
                act.wait_ge(lift_ready, 1)
                act.wait_ge(ctxT_in, 16)
                act.activation(ch[:, 0, :], ctxT[:, :], ACT.Copy, scale=SPLIT).then_inc(hi_ready, 1)

                def keep_q_hi(nb, buf, j, f, bank):
                    act.wait_ge(filled, f + 1)
                    act.activation(qh[0:C, buf, j * PAIR:(j + 1) * PAIR], helper[0:C, bank, :],
                                   ACT.Copy).then_inc(q_hi_ready, 1)

                def keep_acc(b, p, par):
                    act.wait_ge(pv_done, KT * (b * NP + p + 2))
                    act.activation(acc[:, par, :], pacc[0:C1, par, :], ACT.Copy).then_inc(acc_ready, 1)

                def batch(b, buf, prepares):
                    def pair(p, par, kind, _):
                        f, bank = start_fill(b, p, kind)
                        before = pair_before(b, p)
                        n = (b * NP + p) * KT
                        for t in range(KT):
                            act.wait_ge(scores_ready, n + t + 1)
                            act.wait_ge(pv_done, KT + n + t - since_last(t, PRING) + 1)
                            act.wait_ge(lo_done, n + t - since_last(t, WRING) + 1 + KT)
                            for out in (prob[0:keys(t), prob_slot(t, WRING), :], prob_hi[0:keys(t), prob_slot(t), :]):
                                ins = act.activation(out, scores[0:keys(t), score_slot(t, par), :], ACT.Exp,
                                                     scale=UNSPLIT, bias=lift[0:keys(t), :])
                            ins.then_inc(exp_done, 1)
                            if t == 0 and before:
                                keep_acc(*before, 1 - par)
                            if kind == "first" and t < NP:
                                k = t + (sum(o < t for o in OUT_SLOTS) if before else 0)
                                keep_q_hi(b + 1, 1 - buf, t, f + k, (bank + k) % RING)
                        if kind == "idle" and isinstance(p, int) and p == NP - 1:
                            keep_acc(b, p, par)
                    over_pairs(act, pair, prepares)

                for j in range(NP):
                    keep_q_hi(0, 0, j, j, j % RING)
                over_batches(act, batch)

            @block.vector
            def _(dve):
                dve.sem_inc(pv_done, KT)
                dve.sem_inc(lo_done, KT)
                dve.sem_inc(max_freed, 2)
                dve.wait_ge(hi_ready, 1)
                dve.scalar_tensor_tensor(cl[:, 0, :], ctxT[:, :], SPLIT, ch[:, 0, :], ALU.mult,
                                         ALU.subtract).then_inc(split, 1)

                def keep_q_lo(nb, buf, j, f, bank):
                    dve.wait_ge(q_hi_ready, NP * nb + j + 1)
                    cols = slice(j * PAIR, (j + 1) * PAIR)
                    dve.tensor_tensor(ql[0:C, buf, cols], helper[0:C, bank, :], qh[0:C, buf, cols],
                                      ALU.subtract).then_inc(freed, 1)

                def maximum(p, k, f, bank):
                    w = CHUNK[k % NC][1]
                    dve.wait_ge(filled, f + 1)
                    dve.tensor_reduce(mx[:, bass.ds(MAXIMA * p + k, 1)], helper[:, bank, 0:w], AX_X,
                                      ALU.max).then_inc(freed, 1)

                def gather_mu(f):
                    dve.wait_ge(freed, f)
                    dve.tensor_reduce(mu[:, :], mx[:, :].rearrange("p (u c) -> p u c", c=NC), AX_X,
                                      ALU.max).then_inc(mu_ready, 1)

                def keep_shift(nb, f, bank):
                    dve.wait_ge(filled, f + 1)
                    if not (isinstance(nb, int) and nb == 0):
                        dve.wait_ge(shift_in, 16 * nb)
                    dve.tensor_scalar(shift[:, :], helper[0:UNITS, bank, 0:P], -1.0 / SPLIT, None,
                                      ALU.mult).then_inc(freed, 1)

                def add_out(b, p, i, f, bank):
                    v = helper[:, bank, 0:2 * (D + 1)].rearrange("p (a c) -> p a c", c=D + 1)
                    xt = x[:, TB * b + i, :]
                    s = 2 * (TB * (b * NP + p) + i) + 1
                    dve.wait_ge(filled, f + 1)
                    dve.wait_ge(freed, f)
                    dve.reciprocal(rec[:, :], v[:, :, D]).then_inc(x_step, 1)
                    dve.wait_ge(x_step, s + 1)
                    dve.scalar_tensor_tensor(xt, v[:, 0, 0:D], rec[:, 0:1], xt, ALU.mult,
                                             ALU.add).then_inc(x_step, 1)
                    dve.wait_ge(x_step, s + 2)
                    dve.scalar_tensor_tensor(xt, v[:, 1, 0:D], rec[:, 1:2], xt, ALU.mult,
                                             ALU.add).then_inc(freed, 1)

                def keep_lo(n, t):
                    ks = slice(0, keys(t))
                    dve.wait_ge(exp_done, KT + n + t + 1)
                    dve.wait_ge(pv_done, KT + n + t - since_last(t, PRING) + 1)
                    dve.tensor_tensor(prob_lo[ks, prob_slot(t), :], prob[ks, prob_slot(t, WRING), :],
                                      prob_hi[ks, prob_slot(t), :], ALU.subtract).then_inc(lo_done, 1)

                def batch(b, buf, prepares):
                    def pair(p, par, kind, _):
                        f, bank = start_fill(b, p, kind)
                        before = pair_before(b, p)
                        k = 0
                        for t in range(KT):
                            keep_lo((b * NP + p) * KT, t)
                            if kind == "first" and t < NP:
                                keep_q_lo(b + 1, 1 - buf, t, f + k, (bank + k) % RING)
                                k += 1
                            for i in maxima(kind, t):
                                maximum(p, i, f + k, (bank + k) % RING)
                                k += 1
                            if t in OUT_SLOTS and before:
                                add_out(*before, OUT_SLOTS.index(t), f + k, (bank + k) % RING)
                                k += 1
                            if kind == "last" and t == MU_SLOT:
                                gather_mu(f + k)
                            if kind == "last" and t == MU_SLOT + 1:
                                keep_shift(b + 1, f + k, (bank + k) % RING)
                                k += 1
                        if kind == "idle" and isinstance(p, int) and p == NP - 1:
                            for i in range(TB):
                                add_out(b, p, i, f + k + i, (bank + k + i) % RING)
                    over_pairs(dve, pair, prepares)

                for j in range(NP):
                    keep_q_lo(0, 0, j, j, j % RING)
                with dve.Fori(0, NP) as p:
                    for k in range(MAXIMA // 2):
                        n, half = MAXIMA // 2 * p + k, 2 * (k % 2)
                        dve.wait_ge(max_filled, n + 1)
                        dve.tensor_reduce(mx[:, bass.ds(2 * n, 2)], banks[:, half:half + 2, 0:CHUNK[0][1]], AX_X,
                                          ALU.max).then_inc(max_freed, 1)
                dve.wait_ge(max_freed, NP * MAXIMA // 2 + 2)
                dve.wait_ge(x_step, 1)
                gather_mu(FIRST - 1)
                keep_shift(0, FIRST - 1, (FIRST - 1) % RING)
                over_batches(dve, batch)


G, NQ, NK, HR, E = 4, 128, 64, 8, 64
KK = NK + 1
CH = HR * E // P


def routed_weights(nc, ctx, A):
    return Weights(nc, ctx, A, "rw", {
        "r_router": [D, G, 2, P], "r_wq": [D, G, HR * E], "r_wk": [D, G, HR * E], "r_wv": [D, G, HR * E],
        "r_wo": [P, G, CH, D], "r_null_k": [P, G, CH], "r_null_v": [KK, G, HR * E]})


def routed_attention(nc, A, x, xn, xnT, null, gate, ident, weights):
    with ExitStack() as ctx:
        m = Stage(nc, ctx, "ra")
        wr, wq, wk, wv, wo, nk, nv = weights.buf.values()
        before = m.sb("before", [P, TB, S])
        ranks = m.sb("ranks", [P, NK])
        xb = m.sb("xb", [P, TB, D])
        Ls = m.sb("logits", [P, 2, S])
        dg = m.sb("diag", [P, TB, 2, P])
        junk = m.sb("junk", [P, S])
        li = m.sb("own_logit", [P, 2, TB, 2])
        later = m.sb("larger", [P, TB, 2])
        ties = m.sb("ties", [P, TB, 2])
        rank = m.sb("rank", [P, TB, 2])
        sel = m.sb("sel", [P, 2, TB, NK])
        mask = m.sb("mask", [P, G, TB])
        exq = m.sb("exq", [P, G, TB])
        qs = m.sb("q_score", [P, G, TB])
        cnt = m.sb("count", [P, TB])
        inv = m.sb("inverse", [P, TB])
        none = m.sb("none", [P, TB])
        ksT = m.sb("keysT", [D, 2, NK])
        exk = m.sb("exk", [NK, 2])
        kvs = m.sb("kv_score", [NK, 2])
        kT = m.sb("kT", [P, 2, CH, KK])
        V = m.sb("V", [KK, 2, HR * E])
        qT = m.sb("qT", [P, 2, CH, S])
        Pr = m.sb("prob", [P, 2, TB, 2, CH, KK])
        m8 = m.sb("m8", [P, 2, TB, 2, CH])
        r8 = m.sb("r8", [P, 2, TB, 2, CH])
        PT = m.sb("PT", [KK, 2, CH, S])
        oT = m.sb("oT", [P, CH, S])
        summed = m.sb("summed", [P, TB, D])
        pA = m.ps("bank_logits", [P, 512])
        pM = m.ps("bank_keys", [P, 512])
        pV = m.ps("bank_values", [P, 512])
        pQ = m.ps("bank_q", [P, CH, S])
        pS = m.ps("bank_scores", [P, 2, 512])
        pT = m.ps("bank_turn", [P, 512])

        const = m.sem("const")
        xb_ready = m.sem("xb_ready")
        L_full = m.sem("L_full")
        L_kept = m.sem("L_kept")
        own = m.sem("own")
        diag_ready = m.sem("diag_ready")
        own_li = m.sem("li_ready")
        routed = m.sem("routed")
        exq_done = m.sem("exq_done")
        sel_full = m.sem("sel_full")
        ks_kept = m.sem("ks_kept")
        exk_done = m.sem("exk_done")
        kvs_done = m.sem("kvs_done")
        k_full = m.sem("k_full")
        v_full = m.sem("v_full")
        k_kept = m.sem("k_kept")
        null_in = m.sem("null_in")
        v_kept = m.sem("v_kept")
        q_full = m.sem("q_full")
        q_kept = m.sem("q_kept")
        s_full = m.sem("s_full")
        s_kept = m.sem("s_kept")
        e_done = m.sem("e_done")
        r_done = m.sem("r_done")
        p_ready = m.sem("p_ready")
        t_even = m.sem("t_even")
        t_odd = m.sem("t_odd")
        even_kept = m.sem("even_kept")
        odd_kept = m.sem("odd_kept")
        o_full = m.sem("o_full")
        o_kept = m.sem("o_kept")
        y_full = m.sem("y_full")
        y_kept = m.sem("y_kept")

        def steps(eng, step, first):
            first()
            with eng.Fori(0, NB - 1) as b:
                for g in range(G):
                    step(b, g, 3)
            for g in range(G):
                step(NB - 1, g, min(G - 1 - g, 3))

        def following(b, g, k):
            return (b, g + k) if g + k < G else (b + 1, g + k - G)

        with nc.Block() as block:
            @block.gpsimd
            def _(pool):
                pool.iota(ranks[:, :], pattern=[[1, NK]], base=0, channel_multiplier=0,
                          allow_small_or_imprecise_dtypes=True).then_inc(const, 1)
                pool.memset(before[:, :, :], 1.0).then_inc(const, 1)
                pool.wait_ge(const, 2)
                pool.affine_select(out=before[:, :, :], in_=before[:, :, :], compare_op=ALU.is_gt, fill=0.0,
                                   base=0, pattern=[[P, TB], [-1, S]], channel_multiplier=1).then_inc(const, 1)

                def stage_x(b):
                    pool.tensor_copy(xb[:, :, :], xn[:, bass.ds(b * TB, TB), :]).then_inc(xb_ready, 1)

                def normalise(b, g, par, tiles=range(TB)):
                    s = b * G + g
                    for i in tiles:
                        pool.wait_ge(r_done, TB * s + i + 1)
                        pool.tensor_tensor(Pr[:, par, i].rearrange("p e c k -> p (e c) k"),
                                           Pr[:, par, i].rearrange("p e c k -> p (e c) k"),
                                           r8[:, par, i].rearrange("p e c -> p (e c)")[:, :, None].to_broadcast([P, HR, KK]),
                                           ALU.mult).then_inc(p_ready, 1)

                def diagonal(b, g):
                    s = b * G + g
                    pool.wait_ge(L_kept, s + 1)
                    if not (isinstance(s, int) and s == 0):
                        pool.wait_ge(own_li, s)
                    for i in range(TB):
                        pool.tensor_tensor(dg[:, i], Ls[:, :, i * P:(i + 1) * P],
                                           ident[:, None, :].to_broadcast([P, 2, P]), ALU.mult).then_inc(diag_ready, 1)

                def first():
                    stage_x(0)
                    for g in range(3):
                        diagonal(0, g)
                    normalise(0, 0, 0)

                def step(b, g, more):
                    if more >= 1:
                        normalise(*following(b, g, 1), (g + 1) % 2, [0])
                    if more >= 3:
                        diagonal(*following(b, g, 3))
                    if more >= 1:
                        normalise(*following(b, g, 1), (g + 1) % 2, [1])
                    if g + 2 == G - 1 and more >= 3:
                        pool.wait_ge(const, 3)
                        pool.wait_ge(sel_full, b * G + G)
                        stage_x(b + 1)

                steps(pool, step, first)

            @block.tensor
            def _(pe):
                def logits(b, g):
                    s = b * G + g
                    pe.wait_ge(L_kept, s)
                    if not (isinstance(s, int) and s < 3):
                        pe.wait_ge(odd_kept, TB * (s - 2) + 1)
                    for r in range(2):
                        ins = pe.matmul(pA[:, r * S:(r + 1) * S], wr[:, g, r, :], xnT[:, bass.ds(b * S, S)],
                                        start=True, stop=True)
                    ins.then_inc(L_full, 1)

                def queries(b, g):
                    s = b * G + g
                    pe.wait_ge(q_kept, s)
                    if not (isinstance(s, int) and s < 3):
                        pe.wait_ge(o_kept, s - 1)
                    for c in range(CH):
                        ins = pe.matmul(pQ[:, c, :], wq[:, g, c * P:(c + 1) * P], xnT[:, bass.ds(b * S, S)],
                                        start=True, stop=True)
                    ins.then_inc(q_full, 1)

                def gather(b, g, par):
                    s = b * G + g
                    pe.wait_ge(routed, s + 1)
                    pe.wait_ge(xb_ready, b + 1)
                    pe.wait_ge(k_kept, s)
                    for i in range(TB):
                        pe.matmul(pM[:, 0:NK], xb[:, i, :], sel[:, par, i, :], start=(i == 0), stop=(i == TB - 1))
                    for i in range(TB):
                        ins = pe.matmul(pM[0:NK, NK:NK + 1], sel[:, par, i, :], li[:, par, i, 1:2],
                                        start=(i == 0), stop=(i == TB - 1))
                    ins.then_inc(sel_full, 1)

                def keys_values(b, g, par):
                    s = b * G + g
                    pe.wait_ge(ks_kept, s + 1)
                    pe.wait_ge(exk_done, s + 1)
                    for c in range(CH):
                        ins = pe.matmul(pM[:, P + c * NK:P + (c + 1) * NK], wk[:, g, c * P:(c + 1) * P],
                                        ksT[:, par, :], start=True, stop=True)
                    ins.then_inc(k_full, 1)
                    pe.wait_ge(v_kept, s)
                    if not (isinstance(s, int) and s < 3):
                        pe.wait_ge(y_kept, TB * (s - 2) + 1)
                    pe.matmul(pV[0:NK, :], ksT[:, par, :], wv[:, g, :], start=True, stop=True).then_inc(v_full, 1)

                def scores(b, g, par, i):
                    s = b * G + g
                    if i == 0:
                        pe.wait_ge(q_kept, s + 1)
                        pe.wait_ge(k_kept, s + 1)
                        pe.wait_ge(null_in, s + 1)
                    pe.wait_ge(s_kept, TB * s + i + 1)
                    for c in range(CH):
                        for e in range(2):
                            ins = pe.matmul(pS[:, e, c * KK:(c + 1) * KK],
                                            qT[e * E:(e + 1) * E, par, c, i * P:(i + 1) * P],
                                            kT[e * E:(e + 1) * E, par, c, :], start=True, stop=True)
                    ins.then_inc(s_full, 1)

                def turn(b, g, par, i, more):
                    s = b * G + g
                    pe.wait_ge(p_ready, TB * s + i + 1)
                    if i == 0:
                        pe.wait_ge(L_kept, s + 3 if more >= 2 else NB * G)
                    for e, (bank, kept, done) in enumerate(((pT, even_kept, t_even), (pA, odd_kept, t_odd))):
                        pe.wait_ge(kept, TB * s + i + 1)
                        for c in range(CH):
                            ins = pe.transpose(bank[0:KK, c * P:(c + 1) * P], Pr[:, par, i, e, c, :], ident[:, :])
                        ins.then_inc(done, 1)

                def values_product(b, g, par, more):
                    s = b * G + g
                    if more >= 2:
                        pe.wait_ge(q_kept, s + 3)
                    pe.wait_ge(even_kept, TB * (s + 1) + 1)
                    pe.wait_ge(odd_kept, TB * (s + 1) + 1)
                    pe.wait_ge(v_kept, s + 1)
                    for c in range(CH):
                        for e in range(2):
                            h = 2 * c + e
                            ins = pe.matmul(pQ[e * E:(e + 1) * E, c, :], V[:, par, h * E:(h + 1) * E],
                                            PT[:, e, c, :], start=True, stop=True)
                    ins.then_inc(o_full, 1)

                def output(b, g, more):
                    s = b * G + g
                    pe.wait_ge(o_kept, s + 2)
                    if more >= 2:
                        pe.wait_ge(v_kept, s + 3)
                    else:
                        pe.wait_ge(y_kept, TB * s + 1)
                    for i in range(TB):
                        for c in range(CH):
                            ins = pe.matmul(pV[:, i * P:(i + 1) * P], oT[:, c, i * P:(i + 1) * P], wo[:, g, c, :],
                                            start=(c == 0), stop=(c == CH - 1))
                    ins.then_inc(y_full, 1)

                def first():
                    pe.wait_ge(weights.arrived, weights.all)
                    logits(0, 0)
                    queries(0, 0)
                    gather(0, 0, 0)
                    logits(0, 1)
                    keys_values(0, 0, 0)
                    queries(0, 1)
                    scores(0, 0, 0, 0)
                    gather(0, 1, 1)
                    logits(0, 2)
                    scores(0, 0, 0, 1)
                    keys_values(0, 1, 1)

                def step(b, g, more):
                    par = g % 2
                    n1, n2, n3 = (following(b, g, k) for k in (1, 2, 3))
                    if more >= 1:
                        scores(*n1, 1 - par, 0)
                    turn(b, g, par, 0, more)
                    if more >= 2:
                        queries(*n2)
                    if more >= 1:
                        scores(*n1, 1 - par, 1)
                    turn(b, g, par, 1, more)
                    if more >= 2:
                        gather(*n2, par)
                    if more >= 3:
                        logits(*n3)
                    values_product(b, g, par, more)
                    if more >= 2:
                        keys_values(*n2, par)
                    output(b, g, more)

                steps(pe, step, first)

            @block.scalar
            def _(act):
                act.sem_inc(even_kept, 1)
                act.sem_inc(o_kept, 1)

                def keep_logits(b, g):
                    s = b * G + g
                    act.wait_ge(L_full, s + 1)
                    act.wait_ge(routed, s)
                    act.activation(Ls[:, :, :].rearrange("p r n -> p (r n)"), pA[:, :], ACT.Copy).then_inc(L_kept, 1)

                def keep_queries(b, g, par):
                    s = b * G + g
                    act.wait_ge(q_full, s + 1)
                    act.activation(qT[:, par, :, :], pQ[:, :, :], ACT.Copy, scale=E ** -0.5).then_inc(q_kept, 1)

                def exp_logits(b, g, par):
                    s = b * G + g
                    act.wait_ge(own_li, s + 1)
                    act.activation(exq[:, g, :], li[:, par, :, 0], ACT.Exp, scale=-1.0).then_inc(exq_done, 1)
                    act.wait_ge(ks_kept, s + 1)
                    act.activation(exk[:, par:par + 1], pM[0:NK, NK:NK + 1], ACT.Exp, scale=-1.0).then_inc(exk_done, 1)

                def keep_keys_values(b, g, par):
                    s = b * G + g
                    act.wait_ge(k_full, s + 1)
                    act.activation(kT[:, par, :, 0:NK],
                                   pM[:, P:P + CH * NK].rearrange("p (c k) -> p c k", c=CH),
                                   ACT.Copy).then_inc(k_kept, 1)
                    act.wait_ge(v_full, s + 1)
                    act.wait_ge(kvs_done, s + 1)
                    act.activation(V[0:NK, par, :], pV[0:NK, :], ACT.Copy, scale=kvs[:, par:par + 1]).then_inc(v_kept, 1)

                def exp_scores(b, g, par, i):
                    act.wait_ge(s_kept, TB * (b * G + g) + i + 2)
                    act.activation(Pr[:, par, i], Pr[:, par, i], ACT.Exp).then_inc(e_done, 1)

                def keep_even(b, g, i):
                    act.wait_ge(t_even, TB * (b * G + g) + i + 1)
                    act.activation(PT[:, 0, :, i * P:(i + 1) * P],
                                   pT[0:KK, :].rearrange("p (c q) -> p c q", c=CH), ACT.Copy).then_inc(even_kept, 1)

                def keep_heads(b, g):
                    act.wait_ge(o_full, b * G + g + 1)
                    act.activation(oT[:, :, :], pQ[:, :, :], ACT.Copy).then_inc(o_kept, 1)

                def first():
                    keep_logits(0, 0)
                    keep_queries(0, 0, 0)
                    exp_logits(0, 0, 0)
                    keep_logits(0, 1)
                    keep_keys_values(0, 0, 0)
                    keep_queries(0, 1, 1)
                    exp_scores(0, 0, 0, 0)
                    exp_logits(0, 1, 1)
                    keep_logits(0, 2)
                    exp_scores(0, 0, 0, 1)
                    keep_keys_values(0, 1, 1)

                def step(b, g, more):
                    par = g % 2
                    n1, n2, n3 = (following(b, g, k) for k in (1, 2, 3))
                    if more >= 1:
                        exp_scores(*n1, 1 - par, 0)
                    keep_even(b, g, 0)
                    if more >= 2:
                        keep_queries(*n2, par)
                    if more >= 1:
                        exp_scores(*n1, 1 - par, 1)
                    keep_even(b, g, 1)
                    if more >= 2:
                        exp_logits(*n2, par)
                    if more >= 3:
                        keep_logits(*n3)
                    keep_heads(b, g)
                    if more >= 2:
                        keep_keys_values(*n2, par)

                steps(act, step, first)

            @block.vector
            def _(dve):
                for kept in (s_kept, odd_kept, y_kept):
                    dve.sem_inc(kept, 1)
                FIRST_STEPS = 2 * 11 + 4 + 2 * TB
                BATCH_STEPS = G * (2 * TB + 11 + 4) + 4 + 2 * TB

                def own_logits(b, g, par):
                    s = b * G + g
                    dve.wait_ge(diag_ready, TB * (s + 1))
                    dve.tensor_reduce(li[:, par], dg[:, :, :, :], AX_X, ALU.add).then_inc(own_li, 1)
                    dve.wait_ge(own_li, s + 1)

                def rank_tile(c, par, i):
                    for r in range(2):
                        own_logit = li[:, par, i, r:r + 1]
                        c.step(dve.tensor_scalar(junk[:, :], Ls[:, r, :], own_logit, 0.0, ALU.is_gt, ALU.add,
                                                 accum_out=later[:, i, r:r + 1]))
                        c.step(dve.scalar_tensor_tensor(junk[:, :], Ls[:, r, :], own_logit, before[:, i, :],
                                                        ALU.is_equal, ALU.mult,
                                                        accum_out=ties[:, i, r:r + 1]))

                def route(c, g, par):
                    c.step(dve.tensor_tensor(rank[:, :, :], later[:, :, :], ties[:, :, :], ALU.add))
                    c.step(dve.tensor_scalar(mask[:, g, :], rank[:, :, 0], float(NQ), None, ALU.is_lt))
                    dve.tensor_tensor(sel[:, par], ranks[:, None, :].to_broadcast([P, TB, NK]),
                                      rank[:, :, 1:2].to_broadcast([P, TB, NK]), ALU.is_equal).then_inc(routed, 1)

                def route_all(c, b, g, par):
                    own_logits(b, g, par)
                    for i in range(TB):
                        rank_tile(c, par, i)
                    route(c, g, par)

                def weigh(c, b, g, par):
                    s = b * G + g
                    dve.wait_ge(sel_full, s + 1)
                    dve.tensor_copy(ksT[:, par, :], pM[:, 0:NK]).then_inc(ks_kept, 1)
                    dve.wait_ge(exq_done, s + 1)
                    dve.wait_ge(exk_done, s + 1)
                    c.step(dve.tensor_scalar(exk[:, par:par + 1], exk[:, par:par + 1], 1.0, None, ALU.add))
                    dve.reciprocal(kvs[:, par:par + 1], exk[:, par:par + 1]).then_inc(kvs_done, 1)

                def null_key(b, g, par):
                    s = b * G + g
                    dve.wait_ge(k_kept, s + 1)
                    dve.wait_ge(v_kept, s + 1)
                    dve.tensor_copy(V[NK:KK, par, :], nv[NK:KK, g, :])
                    dve.tensor_copy(kT[:, par, :, NK:KK], nk[:, g, :, None]).then_inc(null_in, 1)

                def keep_scores(c, b, g, par, i):
                    dve.wait_ge(s_full, TB * (b * G + g) + i + 1)
                    v = pS[:, :, 0:CH * KK].rearrange("p e (c k) -> p e c k", c=CH)
                    c.step(dve.tensor_reduce(m8[:, par, i], v, AX_X, ALU.max))
                    dve.tensor_tensor(Pr[:, par, i], v, m8[:, par, i, :, :, None].to_broadcast([P, 2, CH, KK]),
                                      ALU.subtract).then_inc(s_kept, 1)

                def denominators(c, b, g, par, i):
                    dve.wait_ge(e_done, TB * (b * G + g) + i + 1)
                    c.step(dve.tensor_reduce(m8[:, par, i], Pr[:, par, i], AX_X, ALU.add))
                    dve.reciprocal(r8[:, par, i], m8[:, par, i]).then_inc(r_done, 1)

                def keep_odd(b, g, i):
                    dve.wait_ge(t_odd, TB * (b * G + g) + i + 1)
                    dve.tensor_copy(PT[:, 1, :, i * P:(i + 1) * P],
                                    pA[0:KK, :].rearrange("p (c q) -> p c q", c=CH)).then_inc(odd_kept, 1)

                def query_scores(c, g):
                    c.step(dve.tensor_scalar(exq[:, g, :], exq[:, g, :], 1.0, None, ALU.add))
                    c.step(dve.reciprocal(exq[:, g, :], exq[:, g, :]))
                    c.step(dve.tensor_tensor(qs[:, g, :], exq[:, g, :], mask[:, g, :], ALU.mult))
                    if g == 0:
                        c.step(dve.tensor_copy(cnt[:, :], mask[:, g, :]))
                    else:
                        c.step(dve.tensor_tensor(cnt[:, :], cnt[:, :], mask[:, g, :], ALU.add))

                def add_output(b, g):
                    s = b * G + g
                    dve.wait_ge(y_full, s + 1)
                    dve.wait_ge(y_kept, TB * s + 1)
                    for i in range(TB):
                        y = pV[:, i * P:(i + 1) * P]
                        if g == 0:
                            dve.tensor_scalar(summed[:, i, :], y, qs[:, g, i:i + 1], None,
                                              ALU.mult).then_inc(y_kept, 1)
                        else:
                            dve.scalar_tensor_tensor(summed[:, i, :], y, qs[:, g, i:i + 1], summed[:, i, :],
                                                     ALU.mult, ALU.add).then_inc(y_kept, 1)

                def add_mean(c, b):
                    c.step(dve.tensor_scalar(inv[:, :], cnt[:, :], 1e-5, None, ALU.max))
                    c.step(dve.reciprocal(inv[:, :], inv[:, :]))
                    c.step(dve.tensor_scalar(inv[:, :], inv[:, :], gate, None, ALU.mult))
                    c.step(dve.tensor_scalar(none[:, :], cnt[:, :], 0.0, None, ALU.is_equal))
                    dve.wait_ge(y_kept, TB * G * (b + 1) + 1)
                    for i in range(TB):
                        xt = x[:, TB * b + i, :]
                        c.step(dve.scalar_tensor_tensor(xt, summed[:, i, :], inv[:, i:i + 1], xt,
                                                        ALU.mult, ALU.add))
                        c.step(dve.scalar_tensor_tensor(xt, null, none[:, i:i + 1], xt, ALU.mult, ALU.add))

                def first():
                    c = Chain(dve, own)
                    dve.wait_ge(const, 3)
                    dve.wait_ge(weights.arrived, weights.all)
                    route_all(c, 0, 0, 0)
                    weigh(c, 0, 0, 0)
                    route_all(c, 0, 1, 1)
                    null_key(0, 0, 0)
                    keep_scores(c, 0, 0, 0, 0)
                    weigh(c, 0, 1, 1)
                    denominators(c, 0, 0, 0, 0)
                    keep_scores(c, 0, 0, 0, 1)
                    denominators(c, 0, 0, 0, 1)
                    null_key(0, 1, 1)
                    own_logits(0, 2, 0)
                    rank_tile(c, 0, 0)
                    assert c.n == FIRST_STEPS, c.n

                def step(b, g, more):
                    par = g % 2
                    n1, n2, n3 = (following(b, g, k) for k in (1, 2, 3))
                    if g == 0:
                        step.chain = Chain(dve, own, FIRST_STEPS + BATCH_STEPS * b)
                    c = step.chain
                    if more >= 1:
                        keep_scores(c, *n1, 1 - par, 0)
                    keep_odd(b, g, 0)
                    if more >= 2:
                        rank_tile(c, par, 1)
                        route(c, n2[1], par)
                    if more >= 1:
                        keep_scores(c, *n1, 1 - par, 1)
                    keep_odd(b, g, 1)
                    if more >= 1:
                        denominators(c, *n1, 1 - par, 0)
                    if more >= 2:
                        weigh(c, *n2, par)
                    query_scores(c, g)
                    if more >= 1:
                        denominators(c, *n1, 1 - par, 1)
                    if more >= 3:
                        own_logits(*n3, 1 - par)
                        rank_tile(c, 1 - par, 0)
                    if more >= 2:
                        null_key(*n2, par)
                    add_output(b, g)
                    if g == G - 1:
                        add_mean(c, b)
                        if more >= 3:
                            assert c.n == BATCH_STEPS, c.n

                steps(dve, step, first)


def routed_layouts(n, a):
    import numpy as np
    wkv = n["L0_ffn_w_kv"].reshape(G, 2, HR * E, D)
    router = np.stack([n["L0_ffn_w_qr"], n["L0_ffn_w_kvr"]], 1)
    a["r_router"] = np.broadcast_to(router.transpose(2, 0, 1)[:, :, :, None], (D, G, 2, P))
    a["r_wq"] = n["L0_ffn_w_q"].transpose(2, 0, 1)
    a["r_wk"] = wkv[:, 0].transpose(2, 0, 1)
    a["r_wv"] = wkv[:, 1].transpose(2, 0, 1)
    a["r_wo"] = n["L0_ffn_w_out"].reshape(G, D, CH, P).transpose(3, 0, 2, 1)
    nkv = n["L0_ffn_null_kv"].reshape(2, G, HR * E)
    a["r_null_k"] = nkv[0].reshape(G, CH, P).transpose(2, 0, 1)
    a["r_null_v"] = np.broadcast_to(nkv[1], (KK, G, HR * E))


DH = D // H
GH = 4
NG = H // GH
QD = P // GH
VD = DH + 1
KCHUNK = [(0, 401), (401, 400), (801, 400), (1201, 400)]


def narrow_weights(nc, ctx, A):
    return Weights(nc, ctx, A, "nw", {
        "n_wq": [D, NG, P], "n_bq": [P, NG], "n_wk": [C1, NG, P], "n_wv": [C1, H * VD], "n_wo": [D, D],
        "n_lows": [P, 2], "n_fold": [P, 2 * VD]})


def narrow_attention(nc, A, x, xnT, bias, gate, ident, weights, *later):
    MAXIMA = 2 * TB * NC
    VT = 2
    NV = (KT + VT - 1) // VT
    PREP = NG + NG * NC + NV
    ITEMS = [j for g in range(NG) for j in [g, *range(NG + g * NC, NG + (g + 1) * NC)]]
    ITEMS += range(NG + NG * NC, PREP)
    FIRST = PREP + 1
    CARRY = TB + 2
    BATCH = PREP + NP * MAXIMA + 1 + TB * NP + 2
    PER_SLOT = 4
    LAST_PER_SLOT = 3
    MU_SLOT = -(-MAXIMA // LAST_PER_SLOT)
    QSLOTS = (PREP + PER_SLOT - 1) // PER_SLOT
    with ExitStack() as ctx:
        m = Stage(nc, ctx, "na")
        wq, bq, wk, wv, wo, lows, fold = weights.buf.values()
        ctxT = m.sb("ctxT", [C1, T])
        k16 = m.sb("k16", [P, 2, NG, T], F16)
        kh = m.sb("kh", [P, RING, KCHUNK[0][1]], F16)
        q16 = m.sb("q16", [P, 2, H * S], F16)
        qa = m.sb("qa", [P, S])
        q_h = m.sb("q_h", [P, S], F16)
        vall = m.sb("vall", [P, 2, KT, H * VD])
        vst = m.sb("vst", [P, 2, KT, 2, QD])
        prob = m.sb("prob", [P, PRING + 1, PAIR])
        acc = m.sb("acc", [P, 2, S])
        mx = m.sb("mx", [P, UNITS * NC])
        mu = m.sb("mu", [P, UNITS])
        shift = m.sb("shift", [UNITS, P], F16)
        att = m.sb("att", [P, TB, H, VD])
        rec = m.sb("rec", [P, TB, H])
        attn = m.sb("attn", [P, TB, D])
        attnT = m.sb("attnT", [D, TB * P])
        banks = m.ps("banks", [P, 2 * RING, 512])
        scores = banks[:, 0:RING, :]
        helper = banks[:, RING:2 * RING, :]
        pacc = m.ps("pacc", [P, 2, 512])

        w_ready = m.sem("w_ready")
        ctxT_in = m.sem("ctxT_in")
        v_clear = m.sem("v_clear")
        v_staged = m.sem("v_staged")
        kh_ready = m.sem("kh_ready")
        q_clear = m.sem("q_clear")
        qa_ready = m.sem("qa_ready")
        q_parts = m.sem("q_parts")
        filled = m.sem("helper_filled")
        freed = m.sem("helper_freed")
        prepared = m.sem("prepared")
        max_filled = m.sem("max_filled")
        max_freed = m.sem("max_freed")
        mu_ready = m.sem("mu_ready")
        shift_in = m.sem("shift_in")
        scores_ready = m.sem("scores_ready")
        exp_done = m.sem("exp_done")
        pv_done = m.sem("pv_done")
        acc_ready = m.sem("acc_ready")
        out_step = m.sem("out_step")
        attn_ready = m.sem("attn_ready")
        attnT_ready = m.sem("attnT_ready")

        def column(i, g):
            return (i * NG + g) * S

        def prep_items(kind, t):
            if kind != "first":
                return range(0)
            return ITEMS[PER_SLOT * t:PER_SLOT * (t + 1)]

        def maxima(kind, t):
            if kind == "first":
                n = KT - QSLOTS
                return range(MAXIMA * (t - QSLOTS) // n, MAXIMA * (t - QSLOTS + 1) // n) if t >= QSLOTS else range(0)
            if kind == "middle":
                return range(MAXIMA * t // KT, MAXIMA * (t + 1) // KT)
            return range(min(LAST_PER_SLOT * t, MAXIMA), min(LAST_PER_SLOT * (t + 1), MAXIMA)) if kind == "last" else range(0)

        def start_fill(b, p, kind, par):
            assert FIRST % RING == 1 and BATCH % RING == 0 and (MAXIMA + TB) % RING == 0
            if isinstance(p, int) and p == 0:
                carried = 0 if isinstance(b, int) and b == 0 else CARRY
                return FIRST + BATCH * b - carried, (FIRST - carried) % RING
            if kind == "idle":
                return FIRST + BATCH * b + TB * (p - 1), 0
            return FIRST + BATCH * b + PREP + MAXIMA + (MAXIMA + TB) * (p - 1), (FIRST + PREP + MAXIMA) % RING

        def is_p(p, v):
            return isinstance(p, int) and p == v

        with nc.Block() as block:
            @block.sync
            def _(sp):
                def load_T(b):
                    if b >= 1:
                        sp.wait_ge(filled, PREP if b == 1 else FIRST + BATCH * (b - 2) + PREP)
                    sp.dma_start(ctxT[:, :], A["ctxT"][b]).then_inc(ctxT_in, 16)

                def put_shift(b):
                    n = FIRST if b == 0 else FIRST + BATCH * b - CARRY
                    sp.wait_ge(freed, n)
                    for i in range(GH):
                        row, units = QD * i + 3 * DH, slice(TB * NG * i, TB * NG * (i + 1))
                        sp.dma_start(q16[row:row + 1, b % 2, column(i, 0):column(i + 1, 0)]
                                     .rearrange("a (u q) -> a u q", q=P), shift[units, :]).then_inc(shift_in, 16)

                load_T(0)
                put_shift(0)
                load_T(1)
                for w in later:
                    w.load(sp)
                for b in range(1, NB):
                    if b + 1 < NB:
                        load_T(b + 1)
                    put_shift(b)

            @block.gpsimd
            def _(pool):
                pool.memset(vall[:, :, KT - 1, :], 0.0).then_inc(v_clear, 1)
                pool.memset(vst[:, :, :, :, :], 0.0).then_inc(v_clear, 1)
                pool.wait_ge(v_clear, 2)

                def batch(b, buf, prepares):
                    with pool.Fori(0, NP // 2) as i:
                        for par in range(2):
                            p = 2 * i + par
                            pool.wait_ge(prepared, b + 1)
                            pool.wait_ge(pv_done, KT * (b * NP + p) + 1)
                            for j in range(2):
                                pool.tensor_copy(vst[:, par, :, j, 0:VD],
                                                 vall[:, buf, :, bass.ds((2 * p + j) * VD, VD)]).then_inc(v_staged, 1)

                over_batches(pool, batch)

            @block.tensor
            def _(pe):
                def fill(f, alone=False):
                    if alone:
                        pe.wait_ge(freed, f)
                    elif not (isinstance(f, int) and f < RING):
                        pe.wait_ge(freed, f - RING + 1)

                def prepare(nb, j, f, bank):
                    fill(f)
                    if j < NG:
                        ins = pe.matmul(helper[:, bank, 0:S], wq[:, j, :], xnT[:, bass.ds(nb * S, S)],
                                        start=True, stop=True)
                    elif j < NG + NG * NC:
                        g, c = divmod(j - NG, NC)
                        c0, w = KCHUNK[c]
                        if j == NG:
                            pe.wait_ge(ctxT_in, 16 * nb + 16)
                        ins = pe.matmul(helper[:, bank, 0:w], wk[:, g, :], ctxT[:, c0:c0 + w], start=True, stop=True)
                    else:
                        t0 = VT * (j - NG - NG * NC)
                        for i, t in enumerate(range(t0, min(t0 + VT, KT))):
                            ins = pe.matmul(helper[0:keys(t), bank, i * H * VD:(i + 1) * H * VD],
                                            ctxT[:, t * P:t * P + keys(t)], wv[:, :], start=True, stop=True)
                    ins.then_inc(filled, 1)

                def maximum(buf, p, g, par, k, f, bank):
                    c0, w = CHUNK[k % NC]
                    fill(f)
                    j, q = divmod(k // NC, TB)
                    pe.matmul(helper[:, bank, 0:w], q16[:, buf, bass.ds(column(2 * par + j, g) + q * P, P)],
                              k16[:, buf, g, c0:c0 + w], start=True, stop=True).then_inc(filled, 1)

                def turn_mu(nb, f, bank):
                    pe.wait_ge(mu_ready, nb + 1)
                    fill(f)
                    pe.transpose(helper[0:UNITS, bank, 0:P], mu[:, :], ident[:, :]).then_inc(filled, 1)

                def score(b, p, g, par, buf, t):
                    n = (b * NP + p) * KT + t
                    if t == 0 and is_p(p, 0):
                        pe.wait_ge(shift_in, 16 * GH * (b + 1))
                    pe.wait_ge(exp_done, KT + n - scores_ago(t, par) + 1)
                    pe.matmul(scores[0:keys(t), score_slot(t, par), :], k16[:, buf, g, t * P:t * P + keys(t)],
                              q16[:, buf, :].rearrange("p (i c) -> p i c", i=GH)
                              [:, 2 * par:2 * par + 2, bass.ds(g * S, S)], start=True, stop=True).then_inc(scores_ready, 1)

                def attend(p, par, t):
                    for j in range(2):
                        r = QD * (2 * (t % 2) + j)
                        ins = pe.matmul(pacc[r:r + QD, par, 0:S], vst[0:keys(t), par, t, j, :],
                                        prob[0:keys(t), prob_slot(t), j * S:(j + 1) * S],
                                        start=(t < 2), stop=(t >= KT - 2))
                    ins.then_inc(pv_done, 1)

                def project(b, p, par, f, bank, alone):
                    pe.wait_ge(acc_ready, b * NP + p + 3)
                    for i in range(TB):
                        fill(f + i, alone)
                        pe.matmul(helper[:, (bank + i) % RING, 0:2 * VD], acc[:, par, i * P:(i + 1) * P], fold[:, :],
                                  start=True, stop=True).then_inc(filled, 1)

                def turn_out(b, f, bank, alone=False):
                    pe.wait_ge(attn_ready, b + 1)
                    fill(f, alone)
                    for i in range(TB):
                        ins = pe.transpose(helper[:, bank, i * P:(i + 1) * P], attn[:, i, :], ident[:, :])
                    ins.then_inc(filled, 1)

                def output(b, f, bank, alone=False):
                    fill(f, alone)
                    pe.wait_ge(attnT_ready, b + 1)
                    for i in range(TB):
                        ins = pe.matmul(helper[:, bank, i * P:(i + 1) * P], attnT[:, i * P:(i + 1) * P],
                                        wo[:, :], start=True, stop=True)
                    ins.then_inc(filled, 1)

                def batch(b, buf, prepares):
                    def pair(p, par, kind, g):
                        f, bank = start_fill(b, p, kind, buf)
                        n = (b * NP + p) * KT
                        k = 0
                        before = pair_before(b, p)
                        gn = g + 1 if par == 1 and not is_p(p, NP - 1) else g
                        for t in range(KT):
                            if t + 2 < KT:
                                score(b, p, g, par, buf, t + 2)
                            elif kind == "last":
                                score(b + 1, 0, 0, 0, 1 - buf, t + 2 - KT)
                            elif not is_p(p, NP - 1):
                                score(b, p + 1, gn, 1 - par, buf, t + 2 - KT)
                            for i in prep_items(kind, t):
                                prepare(b + 1, i, f + k, (bank + k) % RING)
                                k += 1
                            for i in maxima(kind, t)[:1]:
                                maximum(1 - buf, p, g, par, i, f + k, (bank + k) % RING)
                                k += 1
                            if t == 1:
                                pe.wait_ge(acc_ready, b * NP + p + 1)
                                pe.wait_ge(v_staged, 2 * (b * NP + p + 1))
                            if t % 2 == 1 or t == KT - 1:
                                pe.wait_ge(exp_done, KT + n + t + 1)
                                if t % 2 == 1:
                                    attend(p, par, t - 1)
                                attend(p, par, t)
                            for i in maxima(kind, t)[1:]:
                                maximum(1 - buf, p, g, par, i, f + k, (bank + k) % RING)
                                k += 1
                            if t == 2 and before:
                                project(*before, 1 - par, f + k, (bank + k) % RING,
                                        kind == "idle" and not is_p(p, 0))
                                k += TB
                            if t in (5, 7) and before and is_p(p, 0):
                                (turn_out if t == 5 else output)(b - 1, f + k, (bank + k) % RING)
                                k += 1
                            if kind == "last" and t == MU_SLOT + 1:
                                turn_mu(b + 1, f + k, (bank + k) % RING)
                                k += 1
                        if kind == "idle" and is_p(p, NP - 1):
                            project(b, p, par, f + k, (bank + k) % RING, True)
                            turn_out(b, f + k + TB, (bank + k + TB) % RING, True)
                            output(b, f + k + TB + 1, (bank + k + TB + 1) % RING, True)
                    over_pairs(pe, pair, prepares)

                pe.wait_ge(w_ready, 4)
                for f, j in enumerate(ITEMS):
                    prepare(0, j, f, f % RING)
                pe.wait_ge(prepared, 1)
                for n in range(NP * MAXIMA // 2):
                    half, unit = 2 * (n % 2), 2 * n // NC
                    h, q = divmod(unit, TB)
                    g, i_ = divmod(h, GH)
                    c = column(i_, g) + q * P
                    pe.wait_ge(max_freed, n + 1)
                    for i in range(2):
                        c0, w = CHUNK[(2 * n + i) % NC]
                        ins = pe.matmul(banks[:, half + i, 0:w], q16[:, 0, c:c + P],
                                        k16[:, 0, g, c0:c0 + w], start=True, stop=True)
                    ins.then_inc(max_filled, 1)
                turn_mu(0, FIRST - 1, (FIRST - 1) % RING)
                for t in range(2):
                    score(0, 0, 0, 0, 0, t)
                over_batches(pe, batch)

            @block.scalar
            def _(act):
                act.sem_inc(exp_done, KT)
                act.sem_inc(acc_ready, 2)

                def keep_k_hi(nb, j, f, bank):
                    w = KCHUNK[(j - NG) % NC][1]
                    act.wait_ge(filled, f + 1)
                    act.activation(kh[:, bank, 0:w], helper[:, bank, 0:w], ACT.Copy).then_inc(kh_ready, 1)

                def keep_q(nb, j, f, bank):
                    act.wait_ge(filled, f + 1)
                    act.wait_ge(q_parts, GH * (NG * nb + j) + 1)
                    act.activation(qa[:, :], helper[:, bank, 0:S], ACT.Identity, bias=bq[:, j:j + 1]).then_inc(qa_ready, 1)
                    act.wait_ge(qa_ready, 2 * (NG * nb + j) + 1)
                    act.activation(q_h[:, :], qa[:, :], ACT.Copy).then_inc(qa_ready, 1)

                def keep_acc(b, p, par):
                    act.wait_ge(pv_done, KT * (b * NP + p + 2))
                    act.activation(acc[:, par, :], pacc[:, par, 0:S], ACT.Copy).then_inc(acc_ready, 1)

                def batch(b, buf, prepares):
                    def pair(p, par, kind, _):
                        f, bank = start_fill(b, p, kind, buf)
                        before = pair_before(b, p)
                        n = (b * NP + p) * KT
                        k = 0
                        for t in range(KT):
                            act.wait_ge(scores_ready, n + t + 1)
                            act.wait_ge(pv_done, KT + n + t - since_last(t, PRING) + 1)
                            act.activation(prob[0:keys(t), prob_slot(t), :],
                                           scores[0:keys(t), score_slot(t, par), :], ACT.Exp,
                                           scale=UNSPLIT).then_inc(exp_done, 1)
                            if t == 0 and before:
                                keep_acc(*before, 1 - par)
                            for i in prep_items(kind, t):
                                if i < NG:
                                    keep_q(b + 1, i, f + k, (bank + k) % RING)
                                elif i < NG + NG * NC:
                                    keep_k_hi(b + 1, i, f + k, (bank + k) % RING)
                                k += 1
                            if t == 2 and before:
                                k += TB
                            if t in (5, 7) and before and is_p(p, 0):
                                k += 1
                        if kind == "idle" and is_p(p, NP - 1):
                            keep_acc(b, p, par)
                    over_pairs(act, pair, prepares)

                act.wait_ge(w_ready, 4)
                for f, j in enumerate(ITEMS[:NG + NG * NC]):
                    (keep_q if j < NG else keep_k_hi)(0, j, f, f % RING)
                over_batches(act, batch)

            @block.vector
            def _(dve):
                dve.sem_inc(pv_done, KT)
                dve.sem_inc(q_parts, 1)
                dve.sem_inc(max_freed, 2)
                dve.memset(q16[:, :, :], 0.0).then_inc(q_clear, 1)
                dve.tensor_tensor(x[:, :, :], x[:, :, :], bias[:, None, :].to_broadcast([P, NT, D]),
                                  ALU.add).then_inc(q_clear, 1)
                dve.wait_ge(weights.arrived, weights.all)
                dve.tensor_scalar(wk[:, :, :], wk[:, :, :], SPLIT, None, ALU.mult).then_inc(w_ready, 1)
                dve.tensor_scalar(wq[:, :, :], wq[:, :, :], SPLIT * DH ** -0.5, None, ALU.mult).then_inc(w_ready, 1)
                dve.tensor_scalar(bq[:, :], bq[:, :], SPLIT * DH ** -0.5, None, ALU.mult).then_inc(w_ready, 1)
                dve.tensor_scalar(wo[:, :], wo[:, :], gate, None, ALU.mult).then_inc(w_ready, 1)
                dve.wait_ge(w_ready, 4)
                dve.wait_ge(q_clear, 2)
                dve.wait_ge(v_clear, 2)

                def prepare(nb, buf, j, f, bank):
                    dve.wait_ge(filled, f + 1)
                    if j < NG:
                        dve.wait_ge(qa_ready, 2 * (NG * nb + j) + 2)
                        for i in range(GH):
                            r = slice(QD * i, QD * (i + 1))
                            h = column(i, j)
                            dve.scalar_tensor_tensor(q16[r, buf, h:h + S], q_h[r, :], lows[r, 1:2],
                                                     qa[r, :], ALU.mult, ALU.add).then_inc(q_parts, 1)
                        if not (isinstance(f, int) and f == 0):
                            dve.wait_ge(freed, f)
                        dve.sem_inc(freed, 1)
                    elif j < NG + NG * NC:
                        g, c = divmod(j - NG, NC)
                        c0, w = KCHUNK[c]
                        dve.wait_ge(kh_ready, NG * NC * nb + j - NG + 1)
                        dve.scalar_tensor_tensor(k16[:, buf, g, c0:c0 + w], kh[:, bank, 0:w], lows[:, 0:1],
                                                 helper[:, bank, 0:w], ALU.mult, ALU.add).then_inc(freed, 1)
                    else:
                        t0 = VT * (j - NG - NG * NC)
                        n = min(VT, KT - t0)
                        k = keys(t0 + n - 1)
                        assert n == 1 or k == P
                        dve.tensor_copy(vall[0:k, buf, t0:t0 + n, :].rearrange("p t v -> p (t v)"),
                                        helper[0:k, bank, 0:n * H * VD]).then_inc(freed, 1)
                        if j == PREP - 1:
                            dve.wait_ge(freed, f + 1)
                            dve.wait_ge(q_parts, GH * NG * (nb + 1) + 1)
                            dve.sem_inc(prepared, 1)

                def maximum(p, k, f, bank):
                    w = CHUNK[k % NC][1]
                    dve.wait_ge(filled, f + 1)
                    dve.tensor_reduce(mx[:, bass.ds(MAXIMA * p + k, 1)], helper[:, bank, 0:w], AX_X,
                                      ALU.max).then_inc(freed, 1)

                def gather_mu(nb, f):
                    dve.wait_ge(freed, f)
                    v = mx[:, :].rearrange("p (g i q c) -> p i g q c", g=NG, i=GH, q=TB)
                    for i in range(GH):
                        ins = dve.tensor_reduce(mu[:, 2 * NG * i:2 * NG * (i + 1)].rearrange("p (g q) -> p g q", g=NG),
                                                v[:, i], AX_X, ALU.max)
                    ins.then_inc(mu_ready, 1)

                def keep_shift(nb, f, bank):
                    dve.wait_ge(filled, f + 1)
                    if not (isinstance(nb, int) and nb == 0):
                        dve.wait_ge(shift_in, 16 * GH * nb)
                    dve.tensor_scalar(shift[:, :], helper[0:UNITS, bank, 0:P], -1.0 / SPLIT, None,
                                      ALU.mult).then_inc(freed, 1)

                def keep_out(b, p, f, bank):
                    for i in range(TB):
                        dve.wait_ge(filled, f + i + 1)
                        dve.tensor_copy(att[:, i].rearrange("p h v -> p (h v)")[:, bass.ds(2 * VD * p, 2 * VD)],
                                        helper[:, (bank + i) % RING, 0:2 * VD]).then_inc(freed, 1)

                def normalise(b, f):
                    dve.wait_ge(freed, f)
                    dve.reciprocal(rec[:, :, :], att[:, :, :, DH]).then_inc(out_step, 1)
                    dve.wait_ge(out_step, 2 * b + 1)
                    for i in range(TB):
                        ins = dve.tensor_tensor(attn[:, i, :].rearrange("p (h v) -> p h v", h=H), att[:, i, :, 0:DH],
                                                rec[:, i, :, None].to_broadcast([P, H, DH]), ALU.mult)
                    ins.then_inc(attn_ready, 1)

                def keep_attnT(b, f, bank):
                    dve.wait_ge(filled, f + 1)
                    dve.tensor_copy(attnT[:, :], helper[:, bank, 0:TB * P]).then_inc(freed, 1)
                    dve.wait_ge(freed, f + 1)
                    dve.sem_inc(attnT_ready, 1)

                def add_out(b, f, bank):
                    dve.wait_ge(filled, f + 1)
                    for i in range(TB):
                        xt = x[:, TB * b + i, :]
                        ins = dve.tensor_tensor(xt, xt, helper[:, bank, i * P:(i + 1) * P], ALU.add)
                        ins.then_inc(out_step if i == 0 else freed, 1)

                def batch(b, buf, prepares):
                    def pair(p, par, kind, _):
                        f, bank = start_fill(b, p, kind, buf)
                        before = pair_before(b, p)
                        k = 0
                        for t in range(KT):
                            for i in prep_items(kind, t):
                                prepare(b + 1, 1 - buf, i, f + k, (bank + k) % RING)
                                k += 1
                            for i in maxima(kind, t):
                                maximum(p, i, f + k, (bank + k) % RING)
                                k += 1
                            if t == 2 and before:
                                keep_out(*before, f + k, (bank + k) % RING)
                                k += TB
                                if is_p(p, 0):
                                    normalise(b - 1, f + k)
                            if t in (5, 7) and before and is_p(p, 0):
                                (keep_attnT if t == 5 else add_out)(b - 1, f + k, (bank + k) % RING)
                                k += 1
                            if kind == "last" and t == MU_SLOT:
                                gather_mu(b + 1, f + k)
                            if kind == "last" and t == MU_SLOT + 1:
                                keep_shift(b + 1, f + k, (bank + k) % RING)
                                k += 1
                        if kind == "idle" and is_p(p, NP - 1):
                            keep_out(b, p, f + k, (bank + k) % RING)
                            k += TB
                            normalise(b, f + k)
                            keep_attnT(b, f + k, (bank + k) % RING)
                            add_out(b, f + k + 1, (bank + k + 1) % RING)
                    over_pairs(dve, pair, prepares)

                for f, j in enumerate(ITEMS):
                    prepare(0, 0, j, f, f % RING)
                for n in range(NP * MAXIMA // 2):
                    half = 2 * (n % 2)
                    dve.wait_ge(max_filled, n + 1)
                    dve.tensor_reduce(mx[:, 2 * n:2 * n + 2], banks[:, half:half + 2, 0:CHUNK[0][1]], AX_X,
                                      ALU.max).then_inc(max_freed, 1)
                dve.wait_ge(max_freed, NP * MAXIMA // 2 + 2)
                gather_mu(0, FIRST - 1)
                keep_shift(0, FIRST - 1, (FIRST - 1) % RING)
                over_batches(dve, batch)


def narrow_layouts(n, a):
    import numpy as np
    f = np.float32
    wq = n["L1_xattn_Wq"].reshape(NG, GH, DH, D)
    bq = n["L1_xattn_bq"].reshape(NG, GH, DH)
    wkv = np.concatenate([n["L1_xattn_Wkv"], n["L1_xattn_bkv"][:, None]], 1).reshape(H, 2, DH, C1)
    wk = wkv[:, 0].reshape(NG, GH, DH, C1)
    q = np.zeros((D, NG, GH, QD), f)
    qb = np.zeros((GH, QD, NG), f)
    k = np.zeros((C1, NG, GH, QD), f)
    lows = np.zeros((GH, QD, 2), f)
    for r in range(3):
        part = slice(r * DH, (r + 1) * DH)
        q[..., part] = wq.transpose(3, 0, 1, 2)
        qb[:, part] = bq.transpose(1, 2, 0)
        k[..., part] = wk.transpose(3, 0, 1, 2)
    k[C, :, :, 3 * DH] = 1.0
    lows[:, DH:2 * DH, 0] = -1.0
    lows[:, 2 * DH:3 * DH, 1] = -1.0
    v = np.zeros((C1, H, VD), f)
    v[..., 0:DH] = wkv[:, 1].transpose(2, 0, 1)
    v[C, :, DH] = 1.0
    fold = np.zeros((2, 2, QD, 2, VD), f)
    for j in range(2):
        fold[:, j, 0:VD, j, :] = np.eye(VD, dtype=f)
    a["n_wq"] = q.reshape(D, NG, P)
    a["n_bq"] = qb.reshape(P, NG)
    a["n_wk"] = k.reshape(C1, NG, P)
    a["n_wv"] = v.reshape(C1, H * VD)
    a["n_wo"] = n["L1_xattn_Wo"].T
    a["n_lows"] = lows.reshape(P, 2)
    a["n_fold"] = fold.reshape(P, 2 * VD)


NE, HRT, HSH, TAU = 12, 384, 256, 1.5
RC, SC = HRT // P, HSH // P
BLK = 512
NBLK = NB * S // BLK
BT = BLK // P
LOWEST = -3.0e38
AHEAD = 4


def expert_weights(nc, ctx, A):
    return Weights(nc, ctx, A, "ew", {
        "e_wr": [D, NE], "e_br": [P, NE], "e_b1": [P, NE, 2 * RC], "e_bs1": [P, 2 * SC], "e_b2": [NE, D],
        "e_ws1": [D, 2 * HSH], "e_ws2": [P, SC, D], "e_w1": [D, NE, 2 * HRT], "e_w2": [P, NE, RC, D]})


def experts(nc, A, x, xnT, bias, gate, ident, weights):
    CHUNKS = SC + NE * RC
    with ExitStack() as ctx:
        m = Stage(nc, ctx, "ex")
        wr, br, b1, bs1, b2, ws1, ws2, w1, w2 = weights.buf.values()
        xh = m.sb("x_hi", [D, NT * P], F16)
        xl = m.sb("x_lo", [D, NT * P], F16)
        sh = m.sb("ws1_hi", [D, 2 * HSH], F16)
        sl = m.sb("ws1_lo", [D, 2 * HSH], F16)
        wh = m.sb("w1_hi", [D, NE, 2 * HRT], F16)
        wl = m.sb("w1_lo", [D, NE, 2 * HRT], F16)
        gate_u = m.sb("gate_unsplit", [P, 1])
        order = m.sb("order", [P, NE])
        L = m.sb("logits", [P, NT, NE])
        tied = m.sb("tied", [P, NT, NE])
        first = m.sb("first", [P, NT])
        best = m.sb("best", [P, 2, NT, NE])
        top = m.sb("top", [P, NT])
        ex = m.sb("ex", [P, NT, NE])
        den = m.sb("den", [P, NT])
        wgt = m.sb("weight", [P, NT, NE])
        wgt_g = m.sb("gated_weight", [P, NT, NE])
        wT = m.sb("wT", [NE, NT * P])
        wTb = m.sb("wT_block", [NE, BLK])
        gl = m.sb("gelu", [P, 2, BLK])
        hidden = m.sb("hidden", [P, 2, RC, BLK])
        pa = m.ps("a", [P, 2, BLK])
        pg = m.ps("g", [P, 2, BLK])
        py = m.ps("y", [P, 2, BT, D])
        pr = m.ps("route", [P, 2, 512])

        hi_ready = m.sem("hi_ready")
        lo_ready = m.sem("lo_ready")
        w_scaled = m.sem("w_scaled")
        w_hi = m.sem("w_hi")
        w_split = m.sem("w_split")
        b_scaled = m.sem("b_scaled")
        order_ready = m.sem("order_ready")
        own = m.sem("own")
        logits_full = m.sem("logits_full")
        shifted = m.sem("shifted")
        ex_done = m.sem("ex_done")
        wgt_ready = m.sem("wgt_ready")
        wT_full = m.sem("wT_full")
        wT_kept = m.sem("wT_kept")
        wTb_ready = m.sem("wTb_ready")
        up_full = m.sem("up_full")
        gelu_done = m.sem("gelu_done")
        up_kept = m.sem("up_kept")
        y_full = m.sem("y_full")
        y_kept = m.sem("y_kept")

        def chunks(e):
            return SC if e == 0 else RC

        def chunk_index(e):
            return 0 if e == 0 else SC + RC * (e - 1)

        with nc.Block() as block:
            @block.gpsimd
            def _(pool):
                pool.iota(order[:, :], pattern=[[-1, NE]], base=NE, channel_multiplier=0,
                          allow_small_or_imprecise_dtypes=True).then_inc(order_ready, 1)

                def scale(e):
                    pool.tensor_scalar(w1[:, e, :], w1[:, e, :], SPLIT, None, ALU.mult).then_inc(w_scaled, 1)

                def keep_lo(e):
                    pool.wait_ge(w_hi, e + 1)
                    pool.tensor_tensor(wl[:, e, :], w1[:, e, :], wh[:, e, :], ALU.subtract).then_inc(w_split, 1)

                def keep_weights(tb):
                    pool.wait_ge(wT_kept, NT // 4)
                    pool.wait_ge(y_full, tb * (NE + 1) + 1)
                    pool.tensor_copy(wTb[:, :], wT[:, bass.ds(tb * BLK, BLK)]).then_inc(wTb_ready, 1)

                pool.wait_ge(weights.arrived, weights.all)
                scale(0)
                for e in range(NE):
                    if e + 1 < NE:
                        scale(e + 1)
                    keep_lo(e)
                    if e == AHEAD - 1:
                        keep_weights(0)
                with pool.Fori(1, NBLK) as tb:
                    keep_weights(tb)

            @block.tensor
            def _(pe):
                def up(tb, e):
                    for c in range(chunks(e)):
                        k = chunk_index(e) + c
                        pe.wait_ge(up_kept, tb * CHUNKS + k + 1)
                        if c == 0 and isinstance(tb, int) and e >= 1:
                            pe.wait_ge(w_split, e)
                        for bank, half in ((pa, 0), (pg, 1)):
                            if e == 0:
                                cols = slice(half * HSH + c * P, half * HSH + (c + 1) * P)
                                hi, lo = sh[:, cols], sl[:, cols]
                            else:
                                cols = slice(half * HRT + c * P, half * HRT + (c + 1) * P)
                                hi, lo = wh[:, e - 1, cols], wl[:, e - 1, cols]
                            tokens = bass.ds(tb * BLK, BLK)
                            pe.matmul(bank[:, k % 2, :], hi, xh[:, tokens], start=True, stop=False)
                            pe.matmul(bank[:, k % 2, :], lo, xh[:, tokens], start=False, stop=False)
                            ins = pe.matmul(bank[:, k % 2, :], hi, xl[:, tokens], start=False, stop=True)
                        ins.then_inc(up_full, 1)

                def down(tb, e):
                    n = tb * (NE + 1) + e
                    pe.wait_ge(up_kept, 2 + tb * CHUNKS + chunk_index(e) + chunks(e))
                    pe.wait_ge(y_kept, n + 2 if e == 0 else n + 1)
                    if e == 0:
                        pe.wait_ge(wTb_ready, tb + 1)
                    for t in range(BT):
                        if e == 0:
                            pe.matmul(py[:, 0, t, :], wTb[:, t * P:(t + 1) * P], b2[:, :], start=True, stop=False)
                        for c in range(chunks(e)):
                            w = ws2[:, c, :] if e == 0 else w2[:, e - 1, c, :]
                            ins = pe.matmul(py[:, e % 2, t, :], hidden[:, e % 2, c, t * P:(t + 1) * P], w,
                                            start=(c == 0 and e > 0), stop=(c == chunks(e) - 1))
                    ins.then_inc(y_full, 1)

                def token_block(tb):
                    for e in range(NE + 2):
                        if e <= NE:
                            up(tb, e)
                        if e >= 1:
                            down(tb, e - 1)

                pe.wait_ge(weights.arrived, weights.all)
                for t in range(NT):
                    ins = pe.matmul(pr[:, 0, t * NE:(t + 1) * NE], xnT[:, t * P:(t + 1) * P], wr[:, :],
                                    start=True, stop=True)
                ins.then_inc(logits_full, 1)
                pe.wait_ge(wgt_ready, 1)
                for t in range(NT):
                    if t % 4 == 0 and t >= 8:
                        pe.wait_ge(wT_kept, t // 4 - 1)
                    ins = pe.transpose(pr[0:NE, t // 4 % 2, t % 4 * P:(t % 4 + 1) * P], wgt[:, t, :], ident[:, :])
                    if t % 4 == 3:
                        ins.then_inc(wT_full, 1)
                pe.wait_ge(lo_ready, 2)
                pe.wait_ge(b_scaled, 4)
                token_block(0)
                with pe.Fori(1, NBLK) as tb:
                    token_block(tb)

            @block.scalar
            def _(act):
                def keep_hi(e):
                    act.wait_ge(w_scaled, e + 1)
                    act.activation(wh[:, e, :], w1[:, e, :], ACT.Copy).then_inc(w_hi, 1)

                act.activation(xh[:, :], xnT[:, :], ACT.Copy, scale=SPLIT).then_inc(hi_ready, 1)
                act.wait_ge(weights.arrived, weights.all)
                act.activation(sh[:, :], ws1[:, :], ACT.Copy, scale=SPLIT).then_inc(hi_ready, 1)
                for e in range(AHEAD):
                    keep_hi(e)
                act.wait_ge(shifted, 1)
                act.activation(ex[:, :, :], ex[:, :, :], ACT.Exp).then_inc(ex_done, 1)
                for q in range(NT // 4):
                    act.wait_ge(wT_full, q + 1)
                    act.activation(wT[:, 4 * q * P:4 * (q + 1) * P], pr[0:NE, q % 2, :], ACT.Copy).then_inc(wT_kept, 1)

                def token_block(tb):
                    for e in range(NE + 1):
                        if isinstance(tb, int) and 1 <= e <= NE - AHEAD:
                            keep_hi(e - 1 + AHEAD)
                        for c in range(chunks(e)):
                            k = chunk_index(e) + c
                            act.wait_ge(up_full, tb * CHUNKS + k + 1)
                            act.wait_ge(up_kept, tb * CHUNKS + k + 1)
                            b = bs1[:, SC + c:SC + c + 1] if e == 0 else b1[:, e - 1, RC + c:RC + c + 1]
                            act.activation(gl[:, k % 2, :], pg[:, k % 2, :], ACT.Gelu, bias=b,
                                           scale=UNSPLIT).then_inc(gelu_done, 1)

                token_block(0)
                with act.Fori(1, NBLK) as tb:
                    token_block(tb)

            @block.vector
            def _(dve):
                c = Chain(dve, own)
                dve.sem_inc(up_kept, 2)
                dve.sem_inc(y_kept, 2)
                dve.sem_inc(y_full, 2)
                dve.tensor_tensor(x[:, :, :], x[:, :, :], bias[:, None, :].to_broadcast([P, NT, D]), ALU.add)
                dve.wait_ge(weights.arrived, weights.all)
                dve.wait_ge(hi_ready, 2)
                dve.scalar_tensor_tensor(xl[:, :], xnT[:, :], SPLIT, xh[:, :], ALU.mult,
                                         ALU.subtract).then_inc(lo_ready, 1)
                dve.scalar_tensor_tensor(sl[:, :], ws1[:, :], SPLIT, sh[:, :], ALU.mult,
                                         ALU.subtract).then_inc(lo_ready, 1)
                dve.tensor_scalar(b1[:, :, 0:RC], b1[:, :, 0:RC], 1.0 / UNSPLIT, None, ALU.mult).then_inc(b_scaled, 1)
                dve.tensor_scalar(bs1[:, 0:SC], bs1[:, 0:SC], 1.0 / UNSPLIT, None, ALU.mult).then_inc(b_scaled, 1)
                dve.tensor_scalar(b2[:, :], b2[:, :], 1.0 / UNSPLIT, None, ALU.mult).then_inc(b_scaled, 1)
                dve.tensor_scalar(gate_u[:, :], gate, UNSPLIT, None, ALU.mult).then_inc(b_scaled, 1)
                dve.wait_ge(order_ready, 1)
                dve.wait_ge(logits_full, 1)
                c.step(dve.tensor_tensor(L[:, :, :], pr[:, 0, 0:NT * NE].rearrange("p (t e) -> p t e", t=NT),
                                         br[:, None, :].to_broadcast([P, NT, NE]), ALU.add))
                c.step(dve.tensor_scalar(L[:, :, :], L[:, :, :], 1.0 / TAU, None, ALU.mult))
                in_order = order[:, None, :].to_broadcast([P, NT, NE])
                for i in range(2):
                    c.step(dve.tensor_reduce(top[:, :], L[:, :, :], AX_X, ALU.max))
                    if i == 0:
                        c.step(dve.tensor_tensor(ex[:, :, :], L[:, :, :], top[:, :, None].to_broadcast([P, NT, NE]),
                                                 ALU.subtract))
                        dve.sem_inc(shifted, 1)
                    c.step(dve.tensor_tensor(tied[:, :, :], L[:, :, :], top[:, :, None].to_broadcast([P, NT, NE]),
                                             ALU.is_equal))
                    c.step(dve.tensor_tensor(tied[:, :, :], tied[:, :, :], in_order, ALU.mult))
                    c.step(dve.tensor_reduce(first[:, :], tied[:, :, :], AX_X, ALU.max))
                    c.step(dve.tensor_tensor(best[:, i, :, :], in_order,
                                             first[:, :, None].to_broadcast([P, NT, NE]), ALU.is_equal))
                    if i == 0:
                        c.step(dve.scalar_tensor_tensor(L[:, :, :], best[:, 0, :, :], LOWEST, L[:, :, :],
                                                        ALU.mult, ALU.add))
                c.step(dve.tensor_tensor(best[:, 0, :, :], best[:, 0, :, :], best[:, 1, :, :], ALU.add))
                dve.wait_ge(ex_done, 1)
                c.step(dve.tensor_tensor(ex[:, :, :], ex[:, :, :], best[:, 0, :, :], ALU.mult))
                c.step(dve.tensor_reduce(den[:, :], ex[:, :, :], AX_X, ALU.add))
                c.step(dve.reciprocal(den[:, :], den[:, :]))
                dve.tensor_tensor(wgt[:, :, :], ex[:, :, :], den[:, :, None].to_broadcast([P, NT, NE]),
                                  ALU.mult).then_inc(wgt_ready, 1)
                dve.wait_ge(wgt_ready, 1)
                c.step(dve.tensor_scalar(wgt_g[:, :, :], wgt[:, :, :], gate, UNSPLIT, ALU.mult, ALU.mult))
                dve.wait_ge(b_scaled, 4)

                def hide(tb, e):
                    n = tb * (NE + 1) + e
                    dve.wait_ge(y_full, n + 2 if e == 0 else n if e == 1 else n + 1)
                    for c in range(chunks(e)):
                        k = chunk_index(e) + c
                        dve.wait_ge(gelu_done, tb * CHUNKS + k + 1)
                        b = bs1[:, c:c + 1] if e == 0 else b1[:, e - 1, c:c + 1]
                        dve.scalar_tensor_tensor(hidden[:, e % 2, c, :], pa[:, k % 2, :], b, gl[:, k % 2, :],
                                                 ALU.add, ALU.mult).then_inc(up_kept, 1)

                def add(tb, e):
                    n = tb * (NE + 1) + e
                    dve.wait_ge(y_full, n + 3)
                    dve.wait_ge(y_kept, n + 2)
                    for t in range(BT):
                        xt = x[:, tb * BT + t, :]
                        w = gate_u[:, :] if e == 0 else wgt_g[:, bass.ds(tb * BT + t, 1), e - 1]
                        ins = dve.scalar_tensor_tensor(xt, py[:, e % 2, t, :], w, xt, ALU.mult, ALU.add)
                    ins.then_inc(y_kept, 1)

                with dve.Fori(0, NBLK) as tb:
                    for e in range(NE + 2):
                        if e <= NE:
                            hide(tb, e)
                        if e >= 1:
                            add(tb, e - 1)


def expert_layouts(n, a):
    import numpy as np
    a["e_w1"] = n["L1_ffn_We1"].transpose(1, 0, 2)
    a["e_w2"] = n["L1_ffn_We2"].reshape(NE, RC, P, D).transpose(2, 0, 1, 3)
    a["e_ws1"] = n["L1_ffn_Ws1"]
    a["e_ws2"] = n["L1_ffn_Ws2"].reshape(SC, P, D).transpose(1, 0, 2)
    a["e_b1"] = n["L1_ffn_be1"].reshape(NE, 2 * RC, P).transpose(2, 0, 1)
    a["e_bs1"] = n["L1_ffn_bs1"].reshape(2 * SC, P).T
    a["e_b2"] = n["L1_ffn_be2"]
    a["e_wr"] = n["L1_ffn_Wr"]
    a["e_br"] = np.tile(n["L1_ffn_br"].reshape(1, NE), (P, 1))


def setup(nc, A, x, ident, gate, rowvec, *weights):
    with ExitStack() as ctx:
        m = Stage(nc, ctx, "su")
        raw = m.sb("raw_gate", [P, 4])
        x_in = m.sem("x_in")
        gate_in = m.sem("gate_in")
        zeroed = m.sem("zeroed")
        gate_ready = m.sem("gate_ready")
        with nc.Block() as block:
            @block.sync
            def _(sp):
                sp.dma_start(raw[:, :], A["gates"]).then_inc(gate_in, 16)
                sp.dma_start(rowvec[:, :, :], A["rowvecs"]).then_inc(gate_in, 16)
                sp.dma_start(x[:, :, :], A["x"]).then_inc(x_in, 16)
                for w in weights:
                    w.load(sp)
                sp.wait_ge(x_in, 16)

            @block.gpsimd
            def _(pool):
                pool.memset(ident[:, :], 0.0).then_inc(zeroed, 1)
                pool.wait_ge(zeroed, 1)
                pool.affine_select(out=ident[:, :], in_=ident[:, :], compare_op=ALU.not_equal, fill=1.0,
                                   base=0, pattern=[[-1, P]], channel_multiplier=1)

            @block.scalar
            def _(act):
                act.wait_ge(gate_in, 32)
                act.activation(gate[:, :], raw[:, :], ACT.Tanh).then_inc(gate_ready, 1)

            @block.vector
            def _(dve):
                dve.wait_ge(gate_ready, 1)
                for i, g in enumerate(ROWVECS):
                    if g is not None:
                        dve.tensor_scalar(rowvec[:, i, :], rowvec[:, i, :], gate[:, g:g + 1], None, ALU.mult)


def store(nc, x, out):
    with nc.semaphore("stored") as stored, nc.Block() as block:
        @block.sync
        def _(sp):
            sp.dma_start(out, x[:, :, :]).then_inc(stored, 16)
            sp.wait_ge(stored, 16)


G_XATTN0, G_XATTN1, G_FFN0, G_FFN1 = range(4)
ROWVECS = [G_XATTN0, G_FFN0, G_XATTN1, G_FFN1]


def build(nc, A, out):
    with ExitStack() as ctx:
        m = Stage(nc, ctx, "all")
        x = m.sb("x", [P, NT, D])
        xn = m.sb("xn", [P, NT, D])
        xnT = m.sb("xnT", [D, NT * P])
        ident = m.sb("ident", [P, P])
        gate = m.sb("gate", [P, 4])
        rowvec = m.sb("rowvec", [P, len(ROWVECS), D])
        with ExitStack() as layer:
            routed_w = routed_weights(nc, layer, A)
            with ExitStack() as wide:
                w = Stage(nc, wide, "w")
                wide_M = w.sb("M", [D, H, C])
                wide_VO = w.sb("VO", [C1, H, D + 1])
                with ExitStack() as folded:
                    folding = Folding(nc, folded, A, wide_M, wide_VO, gate[:, G_XATTN0:G_XATTN0 + 1])
                    setup(nc, A, x, ident, gate, rowvec, folding.weights)
                    layernorm(nc, "ln0", x, xn, xnT, ident, folding=folding)
                wide_attention(nc, A, x, xnT, wide_M, wide_VO, rowvec[:, 0, :], ident, routed_w)
            layernorm(nc, "ln1", x, xn, xnT, ident)
            routed_attention(nc, A, x, xn, xnT, rowvec[:, 1, :], gate[:, G_FFN0:G_FFN0 + 1], ident, routed_w)
        with ExitStack() as layer:
            expert_w = expert_weights(nc, layer, A)
            with ExitStack() as narrow:
                narrow_w = narrow_weights(nc, narrow, A)
                layernorm(nc, "ln2", x, xn, xnT, ident, narrow_w)
                narrow_attention(nc, A, x, xnT, rowvec[:, 2, :], gate[:, G_XATTN1:G_XATTN1 + 1], ident,
                                 narrow_w, expert_w)
            layernorm(nc, "ln3", x, xn, xnT, ident)
            experts(nc, A, x, xnT, rowvec[:, 3, :], gate[:, G_FFN1:G_FFN1 + 1], ident, expert_w)
        store(nc, x, out)


def laid_out(i):
    import numpy as np
    f = np.float32
    B, T_, C_ = i["ctx_768"].shape
    ctx = np.asarray(i["ctx_768"])
    ctx1 = np.concatenate([ctx, np.ones((B, T_, 1), f)], 2)
    padded = np.concatenate([ctx1, np.zeros((B, KT * P - T_, C1), f)], 1)
    tile = lambda v: np.tile(np.asarray(v).reshape(1, -1), (P, 1))
    gx, gf = np.asarray(i["g_xattn"]), np.asarray(i["g_ffn"])
    a = {
        "x": np.asarray(i["x"]).reshape(NT, P, D).transpose(1, 0, 2),
        "ctxT": ctx1.transpose(0, 2, 1),
        "ctx_rows": padded.reshape(B, KT, P, C1).transpose(0, 2, 1, 3),
        "gates": tile(np.concatenate([gx, gf])),
        "rowvecs": np.stack([tile(i["L0_xattn_bo"]), tile(i["L0_ffn_null_token"]),
                             tile(i["L1_xattn_bo"]), tile(i["L1_ffn_bs2"])], 1),
        "a_wq": np.asarray(i["L0_xattn_Wq"]).reshape(D, H, E0).transpose(2, 1, 0),
        "a_wk": np.asarray(i["L0_xattn_Wk"]).reshape(C, H, E0).transpose(2, 1, 0),
        "a_wv": np.asarray(i["L0_xattn_Wv"]).reshape(C, H, E0).transpose(2, 1, 0),
        "a_wo": np.asarray(i["L0_xattn_Wo"]).reshape(H, E0, D).transpose(1, 0, 2),
    }
    n = {k: np.asarray(v) for k, v in i.items()}
    for layouts in (routed_layouts, narrow_layouts, expert_layouts):
        layouts(n, a)
    return {k: np.ascontiguousarray(v) for k, v in a.items()}


def kernel(**inputs):
    import numpy as np
    import concourse.bacc as bacc
    from concourse.bass_utils import run_bass_kernel_spmd

    nc = bacc.Bacc("TRN2", target_bir_lowering=False, num_devices=1)
    arrays = laid_out(inputs)
    A = {k: nc.dram_tensor(k, v.shape, F32, kind="ExternalInput").ap() for k, v in arrays.items()}
    out = nc.dram_tensor("out", (P, NT, D), F32, kind="ExternalOutput").ap()
    build(nc, A, out)
    r = run_bass_kernel_spmd(nc, [arrays], core_ids=[0])
    y = r.results[0]["out"]
    return np.ascontiguousarray(y.transpose(1, 0, 2).reshape(NB, S, D))
```
